# Optimizing a Trainium2 kernel written in Bass

```python
import numpy as np
import jax
import jax.numpy as jnp

def _softmax(x, axis=-1):
    return jax.nn.softmax(x, axis=axis)

def _gelu(x):
    return jax.nn.gelu(x, approximate=True)

def _silu(x):
    return jax.nn.silu(x)

def _sigmoid(x):
    return jax.nn.sigmoid(x)

def _layernorm(x, axis=-1, eps=1e-05):
    m = jnp.mean(x, axis=axis, keepdims=True)
    v = jnp.var(x, axis=axis, keepdims=True)
    return (x - m) / jnp.sqrt(v + eps)

def _scatter_add(tgt, idx, src, axis=0):
    return tgt.at[idx].add(src)

def _segment_sum(src, seg, n):
    return jax.ops.segment_sum(src, seg, n)
kernel_name = 'mk_audio_tower_d1_tok_audfeat512_r4_5d9ee3'

def setup_inputs(seed: int=0):
    np.random.seed(seed)
    _w = jnp.asarray

    def _rec_inputs():
        import jax
        import jax.numpy as jnp
        _rk = jax.random.key(seed)
        x = -0.00190633 + 1.00279 * jax.random.normal(jax.random.fold_in(_rk, 1), (64, 64, 7), jnp.float32)
        return x
    x = _rec_inputs()

    def _L0_tok_setup():
        import jax, jax.numpy as jnp
        import numpy as np
        SIG_DEPTH = 4

        def _outer(a, b):
            return (a[:, :, None] * b[:, None, :]).reshape(a.shape[0], -1)
        key = jax.random.key(seed)
        k1, k2 = jax.random.split(key)
        B, L, Cin = (64, 64, 7)
        out_dim = 128
        C = Cin + 1
        sig_channels = sum((C ** k for k in range(1, SIG_DEPTH + 1)))
        inp = jax.random.normal(k1, (B, L, Cin), dtype=jnp.float32)
        W = jax.random.normal(k2, (out_dim, sig_channels), dtype=jnp.float32) * 0.02
        b = jnp.zeros((out_dim,), dtype=jnp.float32)
        return {'inp': inp, 'W': W, 'b': b}
    _L0_tok_all = _L0_tok_setup()
    _L0_tok_in = {k: v for k, v in _L0_tok_all.items() if k in ('W', 'b')}
    del _L0_tok_all

    def _L0_attn_setup():
        import jax, jax.numpy as jnp
        from jax import lax
        import numpy as np
        B, T, F, H = (8, 256, 128, 8)
        DK = F // H
        DU = 1
        EPS = 1e-05

        def _bn(x2d, gamma, beta):
            mu = jnp.mean(x2d, axis=0)
            var = jnp.var(x2d, axis=0)
            return (x2d - mu) * lax.rsqrt(var + EPS) * gamma + beta
        key = jax.random.key(seed)
        ks = jax.random.split(key, 7)
        s = 0.02
        return {'x': jax.random.normal(ks[0], (B, T, F), dtype=jnp.float32), 'Wq': jax.random.normal(ks[1], (F, F), dtype=jnp.float32) * s, 'bq': jnp.zeros((F,), jnp.float32), 'Wk': jax.random.normal(ks[2], (F, DU * DK), dtype=jnp.float32) * s, 'bk': jnp.zeros((DU * DK,), jnp.float32), 'Wv': jax.random.normal(ks[3], (F, DU * DK), dtype=jnp.float32) * s, 'bv': jnp.zeros((DU * DK,), jnp.float32), 'gq': jnp.ones((F,), jnp.float32), 'betaq': jnp.zeros((F,), jnp.float32), 'gv': jnp.ones((DU * DK,), jnp.float32), 'betav': jnp.zeros((DU * DK,), jnp.float32), 'Wpos': jax.random.normal(ks[4], (DK, DU, 3, 3), dtype=jnp.float32) * s, 'Wout': jax.random.normal(ks[5], (F, F), dtype=jnp.float32) * s, 'bout': jnp.zeros((F,), jnp.float32)}
    _L0_attn_all = _L0_attn_setup()
    _L0_attn_in = {k: v for k, v in _L0_attn_all.items() if k in ('Wq', 'bq', 'Wk', 'bk', 'Wv', 'bv', 'gq', 'betaq', 'gv', 'betav', 'Wpos', 'Wout', 'bout')}
    del _L0_attn_all

    def _L0_ffn_setup():
        import jax, jax.numpy as jnp
        import numpy as np
        E = 8
        K = 1
        D = 128
        I = 512
        B, T = (2, 512)
        key = jax.random.key(seed)
        ks = jax.random.split(key, 7)
        s = 0.02
        x = jax.random.normal(ks[0], (B, T, D), jnp.float32)
        gate_w = jax.random.normal(ks[1], (E, D), jnp.float32) * s
        w1 = jax.random.normal(ks[2], (E, I, D), jnp.float32) * s
        w2 = jax.random.normal(ks[3], (E, D, I), jnp.float32) * s
        w3 = jax.random.normal(ks[4], (E, I, D), jnp.float32) * s
        sw1 = jax.random.normal(ks[5], (I, D), jnp.float32) * s
        sw2 = jax.random.normal(ks[6], (D, I), jnp.float32) * s
        return {'x': x, 'gate_w': gate_w, 'w1': w1, 'w2': w2, 'w3': w3, 'sw1': sw1, 'sw2': sw2}
    _L0_ffn_all = _L0_ffn_setup()
    _L0_ffn_in = {k: v for k, v in _L0_ffn_all.items() if k in ('gate_w', 'w1', 'w2', 'w3', 'sw1', 'sw2')}
    del _L0_ffn_all
    return {'x': x, 'L0_tok_W': _L0_tok_in['W'], 'L0_tok_b': _L0_tok_in['b'], 'L0_attn_Wq': _L0_attn_in['Wq'], 'L0_attn_bq': _L0_attn_in['bq'], 'L0_attn_Wk': _L0_attn_in['Wk'], 'L0_attn_bk': _L0_attn_in['bk'], 'L0_attn_Wv': _L0_attn_in['Wv'], 'L0_attn_bv': _L0_attn_in['bv'], 'L0_attn_gq': _L0_attn_in['gq'], 'L0_attn_betaq': _L0_attn_in['betaq'], 'L0_attn_gv': _L0_attn_in['gv'], 'L0_attn_betav': _L0_attn_in['betav'], 'L0_attn_Wpos': _L0_attn_in['Wpos'], 'L0_attn_Wout': _L0_attn_in['Wout'], 'L0_attn_bout': _L0_attn_in['bout'], 'L0_ffn_gate_w': _L0_ffn_in['gate_w'], 'L0_ffn_w1': _L0_ffn_in['w1'], 'L0_ffn_w2': _L0_ffn_in['w2'], 'L0_ffn_w3': _L0_ffn_in['w3'], 'L0_ffn_sw1': _L0_ffn_in['sw1'], 'L0_ffn_sw2': _L0_ffn_in['sw2']}

def reference(x, L0_tok_W, L0_tok_b, L0_attn_Wq, L0_attn_bq, L0_attn_Wk, L0_attn_bk, L0_attn_Wv, L0_attn_bv, L0_attn_gq, L0_attn_betaq, L0_attn_gv, L0_attn_betav, L0_attn_Wpos, L0_attn_Wout, L0_attn_bout, L0_ffn_gate_w, L0_ffn_w1, L0_ffn_w2, L0_ffn_w3, L0_ffn_sw1, L0_ffn_sw2):
    import jax
    import jax.numpy as jnp

    def _L0_tok_ref(inp, W, b):
        import jax, jax.numpy as jnp
        import numpy as np
        SIG_DEPTH = 4

        def _outer(a, b):
            return (a[:, :, None] * b[:, None, :]).reshape(a.shape[0], -1)
        B, L, Cin = inp.shape
        t = jnp.broadcast_to(jnp.linspace(0.0, 1.0, L, dtype=inp.dtype)[None, :, None], (B, L, 1))
        x = jnp.concatenate([t, inp], axis=-1)
        C = Cin + 1
        d = SIG_DEPTH
        dx = jnp.transpose(x[:, 1:] - x[:, :-1], (1, 0, 2))
        init = tuple((jnp.zeros((B, C ** (k + 1)), x.dtype) for k in range(d)))

        def step(levels, v):
            e = [v]
            for k in range(1, d):
                e.append(_outer(e[-1], v) / (k + 1))
            new = []
            for k in range(d):
                acc = levels[k] + e[k]
                for i in range(k):
                    acc = acc + _outer(levels[i], e[k - 1 - i])
                new.append(acc)
            sig = jnp.concatenate(new, axis=-1)
            return (tuple(new), sig)
        _, sigs = jax.lax.scan(step, init, dx)
        sigs = jnp.transpose(sigs, (1, 0, 2))
        return sigs @ W.T + b

    def _L0_attn_ref(x, Wq, bq, Wk, bk, Wv, bv, gq, betaq, gv, betav, Wpos, Wout, bout):
        import jax, jax.numpy as jnp
        from jax import lax
        import numpy as np
        B, T, F, H = (8, 256, 128, 8)
        DK = F // H
        DU = 1
        EPS = 1e-05

        def _bn(x2d, gamma, beta):
            mu = jnp.mean(x2d, axis=0)
            var = jnp.var(x2d, axis=0)
            return (x2d - mu) * lax.rsqrt(var + EPS) * gamma + beta
        b, t, f = x.shape
        q = _bn((x @ Wq + bq).reshape(b * t, f), gq, betaq).reshape(b, H, DK, t)
        k = jax.nn.softmax((x @ Wk + bk).reshape(b, DU, DK, t), axis=-1)
        v = _bn((x @ Wv + bv).reshape(b * t, DU * DK), gv, betav).reshape(b, DU, DK, t)
        lam_c = jnp.einsum('bukt,buvt->bkv', k, v)
        Yc = jnp.einsum('bhkt,bkv->bhvt', q, lam_c)
        lam_p = jax.nn.relu(lax.conv_general_dilated(v, Wpos, window_strides=(1, 1), padding=[(1, 1), (1, 1)], dimension_numbers=('NCHW', 'OIHW', 'NCHW')))
        Yp = jnp.einsum('bhkt,bkvt->bhvt', q, lam_p)
        Y = (Yc + Yp).reshape(b, H * DK, t).transpose(0, 2, 1)
        return Y @ Wout + bout

    def _L0_ffn_ref(x, gate_w, w1, w2, w3, sw1, sw2):
        import jax, jax.numpy as jnp
        import numpy as np
        E = 8
        K = 1
        D = 128
        I = 512
        B, T = (2, 512)
        xf = x.reshape(-1, D)
        logits = xf @ gate_w.T
        wts, idx = jax.lax.top_k(logits, K)
        wts = jax.nn.softmax(wts, axis=-1)
        comb = jnp.einsum('nke,nk->ne', jax.nn.one_hot(idx, E, dtype=xf.dtype), wts)
        h = jax.nn.silu(jnp.einsum('nd,eid->nei', xf, w1)) * jnp.einsum('nd,eid->nei', xf, w3)
        y = jnp.einsum('nei,edi->nd', h * comb[:, :, None], w2)
        y = y + jax.nn.gelu(xf @ sw1.T, approximate=False) @ sw2.T
        return y.reshape(x.shape)
    h = _L0_tok_ref(x, L0_tok_W, L0_tok_b)
    h = h + _L0_attn_ref(_layernorm(h, axis=-1), L0_attn_Wq, L0_attn_bq, L0_attn_Wk, L0_attn_bk, L0_attn_Wv, L0_attn_bv, L0_attn_gq, L0_attn_betaq, L0_attn_gv, L0_attn_betav, L0_attn_Wpos, L0_attn_Wout, L0_attn_bout)
    h = h + _L0_ffn_ref(_layernorm(h, axis=-1), L0_ffn_gate_w, L0_ffn_w1, L0_ffn_w2, L0_ffn_w3, L0_ffn_sw1, L0_ffn_sw2)
    return h

_drawn_inputs = setup_inputs


def setup_inputs(seed=0):
    import zlib

    import numpy as np

    out = dict(_drawn_inputs(seed))
    spreads = {'L0_tok_b': (0.0, 0.8),
     'L0_attn_bq': (0.0, 0.8),
     'L0_attn_bk': (0.0, 0.8),
     'L0_attn_bv': (0.0, 0.8),
     'L0_attn_gq': (1.0, 0.6),
     'L0_attn_betaq': (0.0, 0.8),
     'L0_attn_gv': (1.0, 0.6),
     'L0_attn_betav': (0.0, 0.8),
     'L0_attn_bout': (0.0, 0.8)}
    factors = {'L0_attn_Wq': 3.72,
     'L0_attn_Wk': 8.0,
     'L0_attn_Wv': 3.596,
     'L0_attn_Wpos': 8.0,
     'L0_attn_Wout': 3.636,
     'L0_ffn_gate_w': 8.0,
     'L0_ffn_w1': 8.0,
     'L0_ffn_w2': 8.0,
     'L0_ffn_w3': 8.0,
     'L0_ffn_sw1': 8.0,
     'L0_ffn_sw2': 8.0}
    for name, (base, spread) in spreads.items():
        noise = np.random.default_rng([zlib.crc32(name.encode()), seed]).standard_normal(out[name].shape)
        drawn = base * np.exp(spread * noise) if base else spread * noise
        out[name] = jnp.asarray(drawn.astype(out[name].dtype))
    for name, factor in factors.items():
        out[name] = (out[name] * factor).astype(out[name].dtype)
    return out
```

```python
import concourse.bass as bass
from concourse import mybir
from contextlib import ExitStack
import numpy as np

f32 = mybir.dt.float32
f32r = mybir.dt.float32r
i32 = mybir.dt.int32
u32 = mybir.dt.uint32
ALU = mybir.AluOpType
ACT = mybir.ActivationFunctionType
AX = mybir.AxisListType

NB, S, F = 64, 63, 128
C = 8
NT, TOK = 32, 126
N = NB * S
DK, NH = 16, 8
QKV = F + 2 * DK
C3, C2 = C ** 3, C ** 2
TAIL = C2 + C + 1
NCH = C3 // 128
EPS = 1e-5
SP = 64
VB = 18 * SP + SP
GB = 4
NG = NB // GB
E, I = 8, 512
SLOTS = 39
ROW = 132
NOBODY = 1 << 20

K_ID, K_LX, K_LI, K_LR, K_ONE, K_MB, K_REV, K_IO = 0, 128, 254, 380, 506, 634, 642, 650
K_CV = K_IO + SLOTS
K_END = K_CV + 2
P_GQ, P_BETAQ, P_BQ, P_BOUT, P_GV, P_BETAV, P_BV = range(7)


class Links:

    def __init__(self, eng, sem):
        self.eng, self.sem, self.base, self.n = eng, sem, 0, 0

    def made(self, ins):
        ins.then_inc(self.sem, 1)
        self.n += 1

    def wait(self):
        self.eng.wait_ge(self.sem, self.base + self.n)

    def link(self, ins):
        self.made(ins)
        self.wait()

    def loop(self, first, i, per):
        self.start, self.per = self.n, per
        self.base = self.n + (i - first) * per
        self.n = 0

    def end(self, passes):
        assert self.n == self.per, (self.n, self.per)
        self.n = self.start + passes * self.per
        self.base = 0


def on(k, low, high):
    return not isinstance(k, int) or low <= k < high


def hold_waits(eng, turn):
    eng.nop().then_inc(turn, 1)


def wait_from_one(eng, sem, value):
    if not isinstance(value, int) or value > 0:
        eng.wait_ge(sem, value)


def build(nc, path_now, path_next, path_first, wsig, consts, token_ids, tok_b, qkv_b, vecs, wqkv, wpos, wout_v, wout,
          gate_w, sw1, sw2, w13, w2, out):
    q_raw = nc.dram_tensor("q_raw", [N, F], f32, kind="Internal").ap()
    k_raw = nc.dram_tensor("k_raw", [N, DK], f32, kind="Internal").ap()
    v_raw = nc.dram_tensor("v_raw", [N, DK], f32, kind="Internal").ap()

    v_pad = nc.dram_tensor("v_pad", [2, NB, VB], f32, kind="Internal").ap()
    pat_q = nc.dram_tensor("pat_q", [2, S, F], f32, kind="Internal").ap()
    pat_v = nc.dram_tensor("pat_v", [2, S, DK], f32, kind="Internal").ap()
    x_rows = nc.dram_tensor("x_rows", [N, ROW], f32, kind="Internal").ap()
    routed = nc.dram_tensor("routed", [SLOTS * 128, ROW], f32, kind="Internal").ap()
    base = nc.dram_tensor("base", [N, F], f32, kind="Internal").ap()
    out_rows = out.rearrange("b s f -> (b s) f")

    with ExitStack() as whole:
        def keep(name, shape, dt=f32):
            return whole.enter_context(nc.sbuf_tensor(name, shape, dt))

        K = keep("K", [128, K_END])
        ident, ident_t = K[:, K_ID:K_ID + 128], K[0:TOK, K_ID:K_ID + TOK]
        before, upto_now = K[0:TOK, K_LX:K_LX + TOK], K[0:TOK, K_LI:K_LI + TOK]
        H = keep("H", [TOK, NT, F])
        PV = keep("PV", [128, 7])
        eps = keep("eps", [128, 1])
        carrier = keep("carrier", [1, 1])
        stQ, stV = keep("stQ", [128, NT, 6]), keep("stV", [DK, NT, 6])
        LG = keep("LG", [TOK, NT, E])
        X2h, X2l = keep("X2h", [128, N], f32r), keep("X2l", [128, N], f32r)
        PS = [whole.enter_context(nc.psum_tensor(f"PS{n}", [128, 512], f32)) for n in range(8)]
        with ExitStack() as attn:
            QR = attn.enter_context(nc.sbuf_tensor("QR", [128, NB, SP], f32))
            signatures(nc, locals())
            attention(nc, locals())
        ffn(nc, locals())


def signatures(nc, m):
    K, ident_t, before, upto_now, H, PV, eps, carrier = (m[n] for n in "K ident_t before upto_now H PV eps carrier".split())
    stQ, stV, PS, QR, q_raw, k_raw, v_raw = (m[n] for n in "stQ stV PS QR q_raw k_raw v_raw".split())
    path_now, path_next, path_first, wsig, consts, tok_b, qkv_b, vecs, wqkv = (
        m[n] for n in "path_now path_next path_first wsig consts tok_b qkv_b vecs wqkv".split())
    with ExitStack() as ctx:
        def sb(name, shape, dt=f32):
            return ctx.enter_context(nc.sbuf_tensor(name, shape, dt))

        def sem(name):
            return ctx.enter_context(nc.semaphore(name))

        pnow, pnext, pfirst = (sb(n, [TOK, NT, C]) for n in ("pnow", "pnext", "pfirst"))
        V, Vhalf, Vthird, S1, C2h, C3h, C4h = (sb(n, [TOK, NT, C]) for n in ("V", "Vhalf", "Vthird", "S1", "C2h", "C3h", "C4h"))
        E2, E3, A2T = (sb(n, [TOK, NT, C, C]) for n in ("E2", "E3", "A2T"))
        A2X = sb("A2X", [TOK, NT, TAIL])
        INC, TOP = (sb(n, [TOK, 2, C3]) for n in ("INC", "TOP"))
        AXs = sb("AXs", [TOK, 2, TAIL])
        Ah, Al = (sb(n, [128, 2, NCH + 1, TOK], f32r) for n in ("Ah", "Al"))
        WR = sb("WR", [128, 2, 2, 512])
        Wh, Wl = (sb(n, [128, NCH + 1, 2, 512], f32r) for n in ("Wh", "Wl"))
        Vt = sb("Vt", [TOK, 2, C])
        Z = sb("Z", [TOK, 2, F])
        tokb = sb("tokb", [TOK, F])
        qkvb = sb("qkvb", [TOK, QKV])
        wqkv_s = sb("wqkv_s", [128, QKV])
        ST, MV, SD = sb("ST", [TOK, 2, 6]), sb("MV", [TOK, 2, 2]), sb("SD", [TOK, 2, 2])
        XN = sb("XN", [TOK, 2, F])
        XT = sb("XT", [128, 2, TOK])
        QS = sb("QS", [TOK, 2, QKV])

        psA = PS[0][:, 0:NCH * TOK].rearrange("p (c s) -> p c s", c=NCH)
        psB = PS[1][0:TAIL, 0:TOK]
        psU = [[PS[2 + 2 * u + h][0:TOK, :].rearrange("p (d o) -> p d o", d=4) for h in range(2)] for u in range(2)]
        psH = PS[6][0:TOK, 0:F]
        psX = PS[7][:, 0:TOK]
        psQKV, psQT, psVT = PS[7][0:TOK, 0:QKV], PS[7][:, QKV:QKV + TOK], PS[7][0:DK, 288:288 + TOK]

        path_in, const_in, wsig_in0, wsig_in1 = sem("path_in"), sem("const_in"), sem("wsig_in0"), sem("wsig_in1")
        small_in = sem("small_in")
        consts_set = sem("consts_set")
        w_hi, w_split = sem("w_hi"), sem("w_split")
        e2_ready, s2_done, a2_ready, a2x_ready = sem("e2_ready"), sem("s2_done"), sem("a2_ready"), sem("a2x_ready")
        inc_ready, top_ready, ax_ready, at_done = sem("inc_ready"), sem("top_ready"), sem("ax_ready"), sem("at_done")
        ah_ready, al_ready = sem("ah_ready"), sem("al_ready")
        u0_done, u1_done, c0_done, z_ready = sem("u0_done"), sem("u1_done"), sem("c0_done"), sem("z_ready")
        h_done, h_ready, mv_ready, sd_ready, xn_ready = sem("h_done"), sem("h_ready"), sem("mv_ready"), sem("sd_ready"), sem("xn_ready")
        xt_done, xt_ready, qkv_done, qs_ready, stats_done = sem("xt_done"), sem("xt_ready"), sem("qkv_done"), sem("qs_ready"), sem("stats_done")
        qs_stored = [sem("qs_stored0"), sem("qs_stored1")]
        q_loaded = sem("q_loaded")
        dve_link, act_link = sem("dve_link"), sem("act_link")

        block = ctx.enter_context(nc.Block())

        def run_steps(eng, step, links=None, per=0):
            for k in range(-1, 4):
                step(k, k % 2)
            with eng.Fori(2, 15) as j:
                if links:
                    links.loop(2, j, per)
                step(j * 2, 0)
                step(j * 2 + 1, 1)
            if links:
                links.end(13)
            for k in range(30, NT + 2):
                step(k, k % 2)

        @block.sync
        def _(sp):
            sp.dma_start(pnext[:], path_next).then_inc(path_in, 16)
            sp.dma_start(pnow[:], path_now).then_inc(path_in, 16)
            sp.dma_start(pfirst[:], path_first).then_inc(path_in, 16)
            sp.dma_start(K[:], consts).then_inc(const_in, 16)
            for c in range(NCH + 1):
                if c >= 2:
                    sp.wait_ge(w_split, c - 1)
                sp.dma_start(WR[:, c % 2], wsig[:, c]).then_inc([wsig_in0, wsig_in1][c % 2], 16)
                if c == 1:
                    sp.dma_start(tokb[:], tok_b).then_inc(small_in, 16)
                    sp.dma_start(qkvb[:], qkv_b).then_inc(small_in, 16)
                    sp.dma_start(PV[:], vecs).then_inc(small_in, 16)
                    sp.dma_start(wqkv_s[:], wqkv).then_inc(small_in, 16)

            def step(k, u):
                if on(k - 2, 0, NT):
                    t = k - 2
                    sp.wait_ge(qs_ready, t + 1)
                    sp.dma_start(q_raw[bass.ds(t * TOK, TOK), :], QS[:, u, 0:F]).then_inc(qs_stored[u], 16)
                    sp.dma_start(k_raw[bass.ds(t * TOK, TOK), :], QS[:, u, F:F + DK]).then_inc(qs_stored[u], 16)
                    sp.dma_start(v_raw[bass.ds(t * TOK, TOK), :], QS[:, u, F + DK:QKV]).then_inc(qs_stored[u], 16)
                if on(k - 3, 0, NT):
                    load_q(k - 3, k)

            def load_q(t, k):
                if isinstance(t, int):
                    sp.wait_ge(qs_stored[t % 2], 48 * (t // 2 + 1))
                else:
                    sp.wait_ge(*k_of[0])
                src = q_raw.rearrange("(b s) f -> b (s f)", b=NB)[bass.ds(t * 2, 2), :].rearrange("b (p s) -> p b s", p=128)
                sp.dma_start(QR[:, bass.ds(t * 2, 2), 0:S], src).then_inc(q_loaded, 16)

            k_of = [None]
            for k in range(-1, 4):
                step(k, k % 2)
            with sp.Fori(2, 15) as j:
                k_of[0] = (qs_stored[1], (j - 1) * 48)
                step(j * 2, 0)
                k_of[0] = (qs_stored[0], j * 48)
                step(j * 2 + 1, 1)
            for k in range(30, NT + 2):
                step(k, k % 2)
            load_q(NT - 1, None)
            sp.wait_ge(q_loaded, 16 * NT)

        @block.gpsimd
        def _(pool):
            pool.memset(A2X[:, :, C2 + C:TAIL], 1.0).then_inc(consts_set, 1)
            pool.memset(eps[:], EPS).then_inc(consts_set, 1)
            pool.memset(QR[:, :, S:SP], 0.0).then_inc(consts_set, 1)
            pool.wait_ge(a2_ready, 2 * 4)

            def step(k, u):
                t = k + 1
                if on(t, 0, NT):
                    wait_from_one(pool, at_done, t - 1)
                    pool.tensor_tensor(
                        TOP[:, 1 - u].rearrange("p (a b) -> p a b", b=C),
                        A2T[:, bass.ds(t, 1)].rearrange("p t a b -> p (t a b)").unsqueeze(2).broadcast_to([TOK, C2, C]),
                        Vhalf[:, bass.ds(t, 1)].broadcast_to([TOK, C2, C]), ALU.mult).then_inc(top_ready, 1)
            run_steps(pool, step)

        @block.scalar
        def _(act):
            for c in range(NCH + 1):
                act.wait_ge([wsig_in0, wsig_in1][c % 2], 16 * (c // 2 + 1))
                act.activation(Wh[:, c], WR[:, c % 2], ACT.Copy).then_inc(w_hi, 1)
            act.wait_ge(a2_ready, 2 * 4)
            act.wait_ge(a2x_ready, 1)
            act.wait_ge(consts_set, 3)

            def step(k, u):
                if on(k + 1, 0, NT):
                    wait_from_one(act, at_done, k)
                    act.activation(AXs[:, 1 - u], A2X[:, bass.ds(k + 1, 1)].rearrange("p t c -> p (t c)"), ACT.Copy).then_inc(ax_ready, 1)
                if on(k - 1, 0, NT):
                    act.wait_ge(mv_ready, k)
                    act.activation(SD[:, 1 - u, 0:1], MV[:, 1 - u, 1:2], ACT.Sqrt, bias=eps[0:TOK, :]).then_inc(sd_ready, 1)
                if on(k + 1, 0, NT):
                    act.wait_ge(at_done, k + 2)
                    wait_from_one(act, u1_done, k)
                    act.activation(Ah[:, 1 - u, 0:NCH], psA, ACT.Copy).then_inc(ah_ready, 1)
                    act.activation(Ah[0:TAIL, 1 - u, NCH], psB, ACT.Copy).then_inc(ah_ready, 1)
                if on(k - 1, 0, NT):
                    act.wait_ge(xt_done, k)
                    wait_from_one(act, qkv_done, k - 2)
                    act.activation(XT[:, 1 - u], psX, ACT.Copy).then_inc(xt_ready, 1)
            run_steps(act, step)

        @block.vector
        def _(dve):
            L = Links(dve, dve_link)
            dve.wait_ge(path_in, 48)
            L.made(dve.tensor_tensor(V[:], pnext[:], pnow[:], ALU.subtract))
            L.link(dve.tensor_tensor(S1[:], pnow[:], pfirst[:], ALU.subtract))
            L.made(dve.tensor_scalar(Vhalf[:], V[:], 0.5, None, ALU.mult))
            L.made(dve.tensor_scalar(Vthird[:], V[:], 1.0 / 3.0, None, ALU.mult))
            L.made(dve.scalar_tensor_tensor(C2h[:], V[:], 0.5, S1[:], ALU.mult, ALU.add))
            L.made(dve.scalar_tensor_tensor(C3h[:], V[:], 1.0 / 3.0, S1[:], ALU.mult, ALU.add))
            L.link(dve.scalar_tensor_tensor(C4h[:], V[:], 0.25, S1[:], ALU.mult, ALU.add))

            def outer(o, a, b):
                return dve.tensor_tensor(o[:], a[:].unsqueeze(3).broadcast_to([TOK, NT, C, C]),
                                         b[:].unsqueeze(2).broadcast_to([TOK, NT, C, C]), ALU.mult)
            outer(E2, C2h, V).then_inc(e2_ready, 1)
            L.made(outer(E3, C3h, Vhalf))
            L.link(outer(A2T, C4h, Vthird))
            dve.tensor_copy(A2X[:, :, C2:C2 + C], C2h[:]).then_inc(a2x_ready, 1)
            for q in range(4):
                ts = slice(8 * q, 8 * q + 8)
                dve.wait_ge(s2_done, q + 1)
                s2 = PS[2 + q][0:TOK, :].rearrange("p (t c) -> p t c", t=8)
                dve.tensor_tensor(A2X[:, ts, 0:C2], s2, E3[:, ts].rearrange("p t a b -> p t (a b)"), ALU.add).then_inc(a2_ready, 1)
                a2 = A2T[:, ts].rearrange("p t a b -> p t (a b)")
                dve.tensor_tensor(a2, s2, a2, ALU.add).then_inc(a2_ready, 1)
            for c in range(NCH + 1):
                dve.wait_ge(w_hi, c + 1)
                dve.tensor_tensor(Wl[:, c], WR[:, c % 2], Wh[:, c].bitcast(f32), ALU.subtract).then_inc(w_split, 1)
            dve.wait_ge(a2_ready, 8)
            dve.wait_ge(small_in, 64)

            def combine(u, h, first, last):
                for d in range(4):
                    sc = Vt[:, u, 4 * h + d:4 * h + d + 1]
                    if first and d == 0:
                        ins = dve.tensor_scalar(Z[:, u], psU[u][h][:, d], sc, None, ALU.mult)
                    else:
                        ins = dve.scalar_tensor_tensor(Z[:, u], psU[u][h][:, d], sc, Z[:, u], ALU.mult, ALU.add)
                    if d == 3:
                        ins.then_inc(last, 1)
                    else:
                        L.link(ins)

            def step(k, u):
                w = 1 - u
                if on(k + 1, 0, NT):
                    t = k + 1
                    wait_from_one(dve, at_done, k)
                    dve.tensor_tensor(INC[:, w].rearrange("p (a b) -> p a b", b=C),
                                      A2X[:, bass.ds(t, 1), 0:C2].rearrange("p t c -> p (t c)").unsqueeze(2).broadcast_to([TOK, C2, C]),
                                      V[:, bass.ds(t, 1)].broadcast_to([TOK, C2, C]), ALU.mult).then_inc(inc_ready, 1)
                if on(k - 1, 0, NT):
                    dve.wait_ge(u1_done, k)
                    dve.wait_ge(c0_done, k)
                    combine(w, 1, False, z_ready)
                if on(k - 2, 0, NT):
                    t = k - 2
                    dve.wait_ge(qkv_done, k - 1)
                    if isinstance(k, int):
                        if t >= 2:
                            dve.wait_ge(qs_stored[u], 48 * (t // 2))
                    else:
                        dve.wait_ge(qs_stored[u], stored[0])
                    dve.tensor_tensor(QS[:, u], psQKV, qkvb[:], ALU.add).then_inc(qs_ready, 1)
                    L.made(dve.bn_stats(stQ[:, bass.ds(t, 1)].rearrange("p t c -> p (t c)"), psQT))
                    dve.bn_stats(stV[:, bass.ds(t, 1)].rearrange("p t c -> p (t c)"), psVT).then_inc(stats_done, 1)
                if on(k - 1, 0, NT):
                    t = k - 1
                    dve.wait_ge(h_done, k)
                    ht = H[:, bass.ds(t, 1)].rearrange("p t c -> p (t c)")
                    dve.tensor_tensor(ht, psH, tokb[:], ALU.add).then_inc(h_ready, 1)
                    dve.wait_ge(h_ready, k)
                    dve.memset(carrier[:], 0.0)
                    L.link(dve.bn_stats(ST[:, w], ht))
                    dve.memset(carrier[:], 0.0)
                    dve.bn_aggr(MV[:, w], ST[:, w]).then_inc(mv_ready, 1)
                if on(k, 0, NT):
                    L.link(dve.tensor_copy(Vt[:, u], V[:, bass.ds(k, 1)].rearrange("p t c -> p (t c)")))
                    dve.wait_ge(u0_done, k + 1)
                    combine(u, 0, True, c0_done)
                if on(k - 1, 0, NT):
                    dve.wait_ge(sd_ready, k)
                    L.link(dve.reciprocal(SD[:, w, 1:2], SD[:, w, 0:1]))
                    wait_from_one(dve, xt_done, k - 2)
                    dve.tensor_scalar(XN[:, w], ht, MV[:, w, 0:1], SD[:, w, 1:2], ALU.subtract, ALU.mult).then_inc(xn_ready, 1)
                if on(k + 1, 0, NT):
                    dve.wait_ge(ah_ready, 2 * (k + 2))
                    L.made(dve.tensor_tensor(Al[:, w, 0:NCH], psA, Ah[:, w, 0:NCH].bitcast(f32), ALU.subtract))
                    dve.tensor_tensor(Al[0:TAIL, w, NCH], psB, Ah[0:TAIL, w, NCH].bitcast(f32), ALU.subtract).then_inc(al_ready, 1)

            stored = [None]
            for k in range(-1, 4):
                step(k, k % 2)
            with dve.Fori(2, 15) as j:
                L.loop(2, j, 22)
                stored[0] = (j - 1) * 48
                step(j * 2, 0)
                step(j * 2 + 1, 1)
            L.end(13)
            for k in range(30, NT + 2):
                step(k, k % 2)

        @block.tensor
        def _(pe):
            pe.wait_ge(const_in, 16)
            pe.wait_ge(e2_ready, 1)
            for q in range(4):
                pe.matmul(PS[2 + q][0:TOK, :], before, E2[:, 8 * q:8 * q + 8].rearrange("p t a b -> p (t a b)"),
                          start=True, stop=True).then_inc(s2_done, 1)
            pe.wait_ge(a2_ready, 8)

            def half(k, u, h, done):
                for n, (a, w) in enumerate(((Ah, Wh), (Ah, Wl), (Al, Wh))):
                    if n == 2:
                        pe.wait_ge(al_ready, k + 1)
                    for c in range(NCH + 1):
                        rows = 128 if c < NCH else TAIL
                        ins = pe.matmul(psU[u][h].rearrange("p d o -> p (d o)"), a[0:rows, u, c], w[0:rows, c, h],
                                        start=(n == 0 and c == 0), stop=(n == 2 and c == NCH))
                ins.then_inc(done, 1)

            def step(k, u):
                w = 1 - u
                if on(k, 0, NT):
                    if isinstance(k, int) and k == 0:
                        pe.wait_ge(w_split, NCH + 1)
                    pe.wait_ge(ah_ready, 2 * (k + 1))
                    wait_from_one(pe, c0_done, k - 1)
                    half(k, u, 0, u0_done)
                if on(k - 2, 0, NT):
                    if isinstance(k, int) and k == 2:
                        pe.wait_ge(small_in, 64)
                    pe.wait_ge(xt_ready, k - 1)
                    wait_from_one(pe, stats_done, k - 2)
                    pe.matmul(psQKV, XT[:, u], wqkv_s[:], start=True, stop=True)
                    pe.matmul(psQT, wqkv_s[:, 0:F], XT[:, u], start=True, stop=True)
                    pe.matmul(psVT, wqkv_s[:, F + DK:QKV], XT[:, u], start=True, stop=True).then_inc(qkv_done, 1)
                if on(k - 1, 0, NT):
                    pe.wait_ge(z_ready, k)
                    wait_from_one(pe, h_ready, k - 1)
                    pe.matmul(psH, upto_now, Z[:, w], start=True, stop=True).then_inc(h_done, 1)
                if on(k + 1, 0, NT):
                    pe.wait_ge(inc_ready, k + 2)
                    pe.wait_ge(top_ready, k + 2)
                    pe.wait_ge(ax_ready, k + 2)
                    wait_from_one(pe, al_ready, k + 1)
                    for c in range(NCH):
                        cs = slice(128 * c, 128 * c + 128)
                        pe.matmul(psA[:, c], INC[:, w, cs], before, start=True, stop=False)
                        pe.matmul(psA[:, c], TOP[:, w, cs], ident_t, start=False, stop=True)
                    pe.transpose(psB, AXs[:, w], ident_t).then_inc(at_done, 1)
                if on(k, 0, NT):
                    wait_from_one(pe, z_ready, k - 1)
                    half(k, u, 1, u1_done)
                if on(k - 1, 0, NT):
                    pe.wait_ge(xn_ready, k)
                    wait_from_one(pe, stats_done, k - 1)
                    pe.transpose(psX, XN[:, w], ident_t).then_inc(xt_done, 1)
            run_steps(pe, step)


def attention(nc, m):
    K, ident, ident_t, H, PV, eps, carrier, LG, X2h, X2l = (
        m[n] for n in "K ident ident_t H PV eps carrier LG X2h X2l".split())
    stQ, stV, PS, QR, k_raw, v_raw, v_pad, pat_q, pat_v, x_rows, routed = (
        m[n] for n in "stQ stV PS QR k_raw v_raw v_pad pat_q pat_v x_rows routed".split())
    token_ids, wpos, wout_v, wout, gate_w = (m[n] for n in "token_ids wpos wout_v wout gate_w".split())
    with ExitStack() as ctx:
        def sb(name, shape, dt=f32):
            return ctx.enter_context(nc.sbuf_tensor(name, shape, dt))

        def sem(name):
            return ctx.enter_context(nc.semaphore(name))

        G8 = NB // 8
        KR, VR, KS, VN = (sb(n, [128, G8, S]) for n in ("KR", "VR", "KS", "VN"))
        Vh, Vl = (sb(n, [128, G8, SP], f32r) for n in ("Vh", "Vl"))
        kmax, ksum, krec = (sb(n, [128, G8]) for n in ("kmax", "ksum", "krec"))
        mvq, mvv = sb("mvq", [128, 2]), sb("mvv", [DK, 2])
        BNP, BNR = sb("BNP", [128, 4]), sb("BNR", [4, 128])
        bnt = sb("bnt", [128, 4])
        PQ, PVt = sb("PQ", [128, 2, S]), sb("PVt", [128, 2, S])
        KT, VT = sb("KT", [S, NB, DK]), sb("VT", [S, NB, DK])
        KH = sb("KH", [S, 2, GB, NH, DK])
        WP, WPh, WPm, W36 = sb("WP", [36, 128]), sb("WPh", [36, 128], f32r), sb("WPm", [36, 128]), sb("W36", [36, 128], f32r)
        WV, WO, GW = sb("WV", [128, DK, F]), sb("WO", [128, F]), sb("GW", [F, E])
        zero, nobody = sb("zero", [128, 128]), sb("nobody", [128, ROW])
        IM = sb("IM", [36, 2, GB, DK * SP], f32r)
        QN = sb("QN", [128, 2, GB, SP])
        P = sb("P", [128, 2, GB, DK, SP])
        LC = sb("LC", [128, 2, GB, NH, DK])
        YC = sb("YC", [128, 2, GB * SP])
        OTs = sb("OTs", [128, 2, GB, S])
        H1 = sb("H1", [TOK, 2, 2, F])
        ST, MV, SD = sb("ST2", [TOK, 2, 2, 6]), sb("MV2", [TOK, 2, 2, 2]), sb("SD2", [TOK, 2, 2, 2])
        XR = sb("XR", [TOK, 2, 2, ROW])
        XG = sb("XTg", [128, 2, 2 * TOK])
        IDS = sb("IDS", [TOK, NT], i32)

        loads, kv_in, wv_in, zeros_set, zeroed = sem("b_loads"), sem("kv_in"), sem("wv_in"), sem("zeros_set"), sem("zeroed")
        bn_ready, sdv_ready, bnp_ready, bnt_done, bnr_ready = sem("bn_ready"), sem("sdv_ready"), sem("bnp_ready"), sem("bnt_done"), sem("bnr_ready")
        pat_stored, pat_in, w36_ready = sem("pat_stored"), sem("pat_in"), sem("w36_ready")
        ks_ready, exp_done, k_ready, v_ready, vn_ready = sem("ks_ready"), sem("exp_done"), sem("k_ready"), sem("v_ready"), sem("vn_ready")
        v_stored, kt_done, vt_done, kvt_ready, lam_c_done, kh_ready = (
            sem("v_stored"), sem("kt_done"), sem("vt_done"), sem("kvt_ready"), sem("lam_c_done"), sem("kh_ready"))
        im_in = [sem("im_in0"), sem("im_in1")]
        conv_done, p_ready, qn_ready, lc_ready = sem("conv_done"), sem("p_ready"), sem("qn_ready"), sem("lc_ready")
        yc_done, yc_ready, ot_done, ot_ready = sem("yc_done"), sem("yc_ready"), sem("ot_done"), sem("ot_ready")
        ht_done, h1_ready, h1_kept, mv_ready, sd_ready, xn_ready = (
            sem("ht_done"), sem("h1_ready"), sem("h1_kept"), sem("mv2_ready"), sem("sd2_ready"), sem("xn2_ready"))
        ids_ready, xr_stored = sem("ids_ready"), [sem("xr_stored0"), sem("xr_stored1")]
        xt_done, xt_ready, xlo_ready, gate_done, lg_ready = sem("xt2_done"), sem("xt2_ready"), sem("xlo_ready"), sem("gate_done"), sem("lg_ready")
        dve_link, pool_link, act_link = sem("dve_link2"), sem("pool_link2"), sem("act_link2")

        psC = [[PS[2 * u + h][:, :].rearrange("p (v s) -> p v s", v=8) for h in range(2)] for u in range(2)]
        psO, psY = PS[4][:, 0:GB * SP], PS[5][:, 0:GB * SP]
        psH = PS[6][0:TOK, 0:2 * F].rearrange("p (t f) -> p t f", t=2)
        psL = PS[6][:, 256:256 + GB * DK].rearrange("p (b v) -> p b v", b=GB)
        psX = PS[7][:, 0:2 * TOK]
        psG = PS[7][0:TOK, 256:256 + 2 * E].rearrange("p (t e) -> p t e", t=2)

        block = ctx.enter_context(nc.Block())

        @block.sync
        def _(sp):
            sp.dma_start(KR[:], k_raw.rearrange("n k -> (n k)").rearrange("(g p s) -> p g s", g=G8, p=128)).then_inc(kv_in, 16)
            sp.dma_start(VR[:], v_raw.rearrange("n k -> (n k)").rearrange("(g p s) -> p g s", g=G8, p=128)).then_inc(kv_in, 16)
            sp.dma_start(WP[:], wpos).then_inc(loads, 16)
            sp.dma_start(GW[:], gate_w).then_inc(loads, 16)
            sp.dma_start(IDS[:], token_ids).then_inc(loads, 16)
            sp.dma_start(WV[:], wout_v).then_inc(wv_in, 16)
            sp.dma_start(WO[:], wout).then_inc(wv_in, 16)
            sp.wait_ge(zeros_set, 2)
            rows = v_pad.rearrange("c b n -> (c b) n")
            sp.dma_start(rows[:, 0:SP], zero[:, 0:SP]).then_inc(zeroed, 16)
            sp.dma_start(rows[:, 17 * SP:VB], zero[:, 0:VB - 17 * SP]).then_inc(zeroed, 16)
            sp.dma_start(routed.rearrange("(t p) c -> p t c", p=128), nobody[:].unsqueeze(1).broadcast_to([128, SLOTS, ROW])).then_inc(zeroed, 16)
            sp.wait_ge(bnr_ready, 1)
            sp.dma_start(pat_q, BNR[0:2, :].unsqueeze(1).broadcast_to([2, S, F])).then_inc(pat_stored, 16)
            sp.dma_start(pat_v, BNR[2:4, 0:DK].unsqueeze(1).broadcast_to([2, S, DK])).then_inc(pat_stored, 16)
            sp.wait_ge(pat_stored, 32)
            for c in range(2):
                sp.dma_start(PVt[:, c], bass.AP(pat_v.tensor, c * S * DK, [[0, 8], [S, DK], [1, S]])).then_inc(pat_in, 16)
            sp.dma_start(PQ[:], bass.AP(pat_q.tensor, 0, [[S, 128], [S * F, 2], [1, S]])).then_inc(pat_in, 16)
            sp.wait_ge(v_ready, 2)
            for c, half in enumerate((Vh, Vl)):
                for g in range(G8):
                    sp.dma_start(bass.AP(v_pad.tensor, (c * NB + 8 * g) * VB + SP, [[VB, 8], [SP, DK], [1, SP]]),
                                 half[:, g].bitcast(f32)).then_inc(v_stored, 16)
            sp.wait_ge(v_stored, 32 * G8)
            sp.wait_ge(zeroed, 48)

            def load_im(t, u):
                for c in range(4):
                    src = v_pad[c % 2, bass.ds(t * GB, GB), :]
                    for i in range(3):
                        sp.dma_start(IM[9 * c + 3 * i:9 * c + 3 * i + 3, u].bitcast(f32),
                                     bass.AP(src.tensor, src.offset + i * SP, [[1, 3], [VB, GB], [1, DK * SP]])).then_inc(im_in[u], 16)

            def step(g, u):
                if on(g + 1, 0, NG):
                    wait_from_one(sp, conv_done, g * GB)
                    load_im(g + 1, 1 - u)
                if on(g - 2, 0, NG):
                    sp.wait_ge(xn_ready, g - 1)
                    sp.wait_ge(ids_ready, g - 1)
                    sp.dma_start(x_rows[bass.ds((g - 2) * 2 * TOK, 2 * TOK), :].rearrange("(t p) c -> p t c", p=TOK),
                                 XR[:, u]).then_inc(xr_stored[u], 16)
            for g in range(-1, 4):
                step(g, g % 2)
            with sp.Fori(2, 7) as j:
                step(j * 2, 0)
                step(j * 2 + 1, 1)
            for g in range(14, NG + 3):
                step(g, g % 2)
            for u in range(2):
                sp.wait_ge(xr_stored[u], 16 * NG // 2)

        @block.gpsimd
        def _(pool):
            L = Links(pool, pool_link)
            pool.memset(zero[:], 0.0).then_inc(zeros_set, 1)
            L.link(pool.memset(nobody[:], 0.0))
            pool.memset(nobody[:, F:F + 1].bitcast(i32), NOBODY).then_inc(zeros_set, 1)
            L.made(pool.memset(QN[:, :, :, S:SP], 0.0))
            L.link(pool.memset(XR[:, :, :, F:ROW], 0.0))
            pool.wait_ge(loads, 48)
            pool.wait_ge(pat_in, 48)

            def step(g, u):
                w = 1 - u
                if on(g + 1, 0, NG):
                    wait_from_one(pool, p_ready, g * GB)
                    wait_from_one(pool, yc_done, g)
                    L.link(pool.tensor_tensor(QN[:, w, :, 0:S], QR[:, bass.ds((g + 1) * GB, GB), 0:S],
                                              PQ[:, 0:1].broadcast_to([128, GB, S]), ALU.mult))
                    pool.tensor_tensor(QN[:, w, :, 0:S], QN[:, w, :, 0:S],
                                       PQ[:, 1:2].broadcast_to([128, GB, S]), ALU.add).then_inc(qn_ready, 1)
                if on(g - 2, 0, NG):
                    if isinstance(g, int):
                        if g >= 4:
                            pool.wait_ge(xr_stored[u], 16 * ((g - 2) // 2))
                    else:
                        pool.wait_ge(xr_stored[u], freed[0])
                    pool.tensor_copy(XR[:, u, :, F].bitcast(i32), IDS[:, bass.ds((g - 2) * 2, 2)]).then_inc(ids_ready, 1)
                if on(g - 3, 0, NG):
                    pool.wait_ge(xt_ready, 2 * (g - 2))
                    ts = bass.ds((g - 3) * 2 * TOK, 2 * TOK)
                    pool.tensor_tensor(X2l[:, ts], XG[:, w], X2h[:, ts].bitcast(f32), ALU.subtract).then_inc(xlo_ready, 1)

            freed = [None]
            for g in range(-1, 4):
                step(g, g % 2)
            with pool.Fori(2, 7) as j:
                L.loop(2, j, 2)
                freed[0] = (j - 1) * 16
                step(j * 2, 0)
                step(j * 2 + 1, 1)
            L.end(5)
            for g in range(14, NG + 3):
                step(g, g % 2)

        @block.scalar
        def _(act):
            act.wait_ge(bn_ready, 2)
            act.activation(bnt[:, 0:1], mvq[:, 1:2], ACT.Sqrt, bias=eps[:]).then_inc(sdv_ready, 1)
            act.activation(bnt[0:DK, 1:2], mvv[:, 1:2], ACT.Sqrt, bias=eps[0:DK]).then_inc(sdv_ready, 1)
            act.wait_ge(bnt_done, 1)
            act.activation(BNR[:], PS[6][0:4, 0:128], ACT.Copy).then_inc(bnr_ready, 1)
            act.wait_ge(ks_ready, 1)
            act.activation(KS[:], KS[:], ACT.Exp).then_inc(exp_done, 1)
            for n, (to, done) in enumerate(((KT, kt_done), (VT, vt_done))):
                act.wait_ge(done, 1)
                for h in range(2):
                    act.activation(to[:, 32 * h:32 * h + 32].rearrange("p b k -> p (b k)"), PS[2 * n + h][0:S, :], ACT.Copy).then_inc(kvt_ready, 1)
            act.wait_ge(kvt_ready, 4)

            def step(g, u):
                w = 1 - u
                if on(g + 1, 0, NG):
                    wait_from_one(act, lam_c_done, g)
                    act.activation(KH[:, w], KT[:, bass.ds((g + 1) * GB, GB)].unsqueeze(2).broadcast_to([S, GB, NH, DK]),
                                   ACT.Copy).then_inc(kh_ready, 1)
                if on(g - 2, 0, NG):
                    act.wait_ge(mv_ready, 2 * (g - 1))
                    act.activation(SD[:, u, :, 0], MV[:, u, :, 1], ACT.Sqrt, bias=eps[0:TOK, :]).then_inc(sd_ready, 1)
                    act.activation(H[:, bass.ds((g - 2) * 2, 2)], H1[:, u], ACT.Copy).then_inc(h1_kept, 1)
                if on(g - 1, 0, NG):
                    act.wait_ge(ot_done, g)
                    wait_from_one(act, ht_done, g - 2)
                    act.activation(OTs[:, w], psO.rearrange("p (b s) -> p b s", b=GB)[:, :, 0:S], ACT.Identity,
                                   bias=PV[:, P_BOUT:P_BOUT + 1]).then_inc(ot_ready, 1)
                if on(g, 0, NG):
                    act.wait_ge(yc_done, g + 1)
                    wait_from_one(act, ot_done, g - 1)
                    act.activation(YC[:, u], psY, ACT.Copy).then_inc(yc_ready, 1)
                if on(g - 2, 0, NG):
                    act.wait_ge(xt_done, g - 1)
                    wait_from_one(act, xlo_ready, g - 3)
                    wait_from_one(act, gate_done, g - 3)
                    act.activation(XG[:, u], psX, ACT.Copy).then_inc(xt_ready, 1)
                    act.activation(X2h[:, bass.ds((g - 2) * 2 * TOK, 2 * TOK)], psX, ACT.Copy).then_inc(xt_ready, 1)
            for g in range(-1, 4):
                step(g, g % 2)
            with act.Fori(2, 7) as j:
                step(j * 2, 0)
                step(j * 2 + 1, 1)
            for g in range(14, NG + 3):
                step(g, g % 2)

        @block.vector
        def _(dve):
            L = Links(dve, dve_link)
            dve.bn_aggr(mvq[:], stQ[:].rearrange("p t c -> p (t c)")).then_inc(bn_ready, 1)
            dve.bn_aggr(mvv[:], stV[:].rearrange("p t c -> p (t c)")).then_inc(bn_ready, 1)
            L.link(dve.memset(BNP[:], 0.0))
            dve.wait_ge(bn_ready, 2)
            L.made(dve.tensor_tensor(bnt[:, 2:3], mvq[:, 0:1], PV[:, P_BQ:P_BQ + 1], ALU.add))
            L.made(dve.tensor_tensor(bnt[0:DK, 3:4], mvv[:, 0:1], PV[0:DK, P_BV:P_BV + 1], ALU.add))
            dve.wait_ge(sdv_ready, 2)
            L.made(dve.reciprocal(bnt[:, 0:1], bnt[:, 0:1]))
            L.link(dve.reciprocal(bnt[0:DK, 1:2], bnt[0:DK, 1:2]))
            L.made(dve.tensor_tensor(BNP[:, 0:1], bnt[:, 0:1], PV[:, P_GQ:P_GQ + 1], ALU.mult))
            L.link(dve.tensor_tensor(BNP[0:DK, 2:3], bnt[0:DK, 1:2], PV[0:DK, P_GV:P_GV + 1], ALU.mult))
            L.made(dve.tensor_tensor(bnt[:, 2:3], bnt[:, 2:3], BNP[:, 0:1], ALU.mult))
            L.link(dve.tensor_tensor(bnt[0:DK, 3:4], bnt[0:DK, 3:4], BNP[0:DK, 2:3], ALU.mult))
            L.made(dve.tensor_tensor(BNP[:, 1:2], PV[:, P_BETAQ:P_BETAQ + 1], bnt[:, 2:3], ALU.subtract))
            L.link(dve.tensor_tensor(BNP[0:DK, 3:4], PV[0:DK, P_BETAV:P_BETAV + 1], bnt[0:DK, 3:4], ALU.subtract))
            L.link(dve.tensor_copy(bnt[:, 0:4], BNP[:]))
            dve.sem_inc(bnp_ready, 1)
            dve.wait_ge(kv_in, 32)
            L.link(dve.tensor_reduce(kmax[:], KR[:], AX.X, ALU.max))
            dve.tensor_tensor(KS[:], KR[:], kmax[:].unsqueeze(2).broadcast_to([128, G8, S]), ALU.subtract).then_inc(ks_ready, 1)
            dve.wait_ge(loads, 48)
            L.link(dve.tensor_copy(WPh[:], WP[:]))
            L.link(dve.tensor_scalar(WPm[:], WP[:], K[0:36, K_CV + 1:K_CV + 2], None, ALU.mult))
            dve.scalar_tensor_tensor(W36[:], WPh[:].bitcast(f32), K[0:36, K_CV:K_CV + 1], WPm[:], ALU.mult, ALU.add).then_inc(w36_ready, 1)
            dve.wait_ge(exp_done, 1)
            L.link(dve.tensor_reduce(ksum[:], KS[:], AX.X, ALU.add))
            L.link(dve.reciprocal(krec[:], ksum[:]))
            dve.tensor_tensor(KS[:], KS[:], krec[:].unsqueeze(2).broadcast_to([128, G8, S]), ALU.mult).then_inc(k_ready, 1)
            dve.wait_ge(pat_in, 48)
            L.link(dve.tensor_tensor(VN[:], VR[:], PVt[:, 0:1].broadcast_to([128, G8, S]), ALU.mult))
            dve.tensor_tensor(VN[:], VN[:], PVt[:, 1:2].broadcast_to([128, G8, S]), ALU.add).then_inc(vn_ready, 1)
            dve.wait_ge(vn_ready, 1)
            L.made(dve.memset(Vh[:, :, 0:1].bitcast(f32), 0.0))
            L.made(dve.memset(Vl[:, :, 0:1].bitcast(f32), 0.0))
            dve.tensor_copy(Vh[:, :, 1:SP], VN[:]).then_inc(v_ready, 1)
            dve.wait_ge(v_ready, 1)
            L.wait()
            dve.tensor_tensor(Vl[:, :, 1:SP], VN[:], Vh[:, :, 1:SP].bitcast(f32), ALU.subtract).then_inc(v_ready, 1)

            def step(g, u):
                w = 1 - u

                def products(b):
                    n = g * GB + b
                    dve.wait_ge(conv_done, n + 1)
                    for h in range(2):
                        ins = dve.scalar_tensor_tensor(P[:, u, b, 8 * h:8 * h + 8], psC[b % 2][h], 0.0,
                                                       QN[:, u, b:b + 1].broadcast_to([128, 8, SP]), ALU.max, ALU.mult)
                    ins.then_inc(p_ready, 1)
                if on(g, 0, NG):
                    dve.wait_ge(qn_ready, g + 1)
                    wait_from_one(dve, ot_done, g - 1)
                    products(0)
                    products(1)
                if on(g - 2, 0, NG):
                    dve.wait_ge(ht_done, g - 1)
                    wait_from_one(dve, h1_kept, g - 3)
                    dve.tensor_tensor(H1[:, u], psH, H[:, bass.ds((g - 2) * 2, 2)], ALU.add).then_inc(h1_ready, 1)
                    dve.wait_ge(h1_ready, g - 1)
                    for t in range(2):
                        L.made(dve.bn_stats(ST[:, u, t], H1[:, u, t]))
                    L.wait()
                    dve.memset(carrier[:], 0.0)
                    for t in range(2):
                        dve.bn_aggr(MV[:, u, t], ST[:, u, t]).then_inc(mv_ready, 1)
                if on(g, 0, NG):
                    products(2)
                    products(3)
                if on(g - 2, 0, NG):
                    dve.wait_ge(sd_ready, g - 1)
                    L.link(dve.reciprocal(SD[:, u, :, 1], SD[:, u, :, 0]))
                    if isinstance(g, int):
                        if g >= 4:
                            dve.wait_ge(xr_stored[u], 16 * ((g - 2) // 2))
                    else:
                        dve.wait_ge(xr_stored[u], freed[0])
                    wait_from_one(dve, xt_done, g - 3)
                    for t in range(2):
                        ins = dve.tensor_scalar(XR[:, u, t, 0:F], H1[:, u, t], MV[:, u, t, 0:1], SD[:, u, t, 1:2], ALU.subtract, ALU.mult)
                        if t == 0:
                            L.made(ins)
                    ins.then_inc(xn_ready, 1)
                if on(g + 1, 0, NG):
                    dve.wait_ge(lam_c_done, g + 2)
                    wait_from_one(dve, yc_done, g)
                    dve.tensor_tensor(LC[:, w], psL.unsqueeze(2).broadcast_to([128, GB, NH, DK]),
                                      K[:, K_MB:K_MB + NH].unsqueeze(1).unsqueeze(3).broadcast_to([128, GB, NH, DK]),
                                      ALU.mult).then_inc(lc_ready, 1)
                if on(g - 3, 0, NG):
                    dve.wait_ge(gate_done, g - 2)
                    dve.tensor_copy(LG[:, bass.ds((g - 3) * 2, 2)], psG).then_inc(lg_ready, 1)

            freed = [None]
            for g in range(-1, 4):
                step(g, g % 2)
            with dve.Fori(2, 7) as j:
                L.loop(2, j, 8)
                freed[0] = (j - 1) * 16
                step(j * 2, 0)
                step(j * 2 + 1, 1)
            L.end(5)
            for g in range(14, NG + 3):
                step(g, g % 2)

        @block.tensor
        def _(pe):
            pe.wait_ge(bnp_ready, 1)
            pe.transpose(PS[6][0:4, 0:128], bnt[:], ident).then_inc(bnt_done, 1)
            for n, (of, ready, done) in enumerate(((KS, k_ready, kt_done), (VN, vn_ready, vt_done))):
                pe.wait_ge(ready, 1)
                for q in range(G8):
                    ins = pe.transpose(PS[2 * n + q // 4][0:S, 128 * (q % 4):128 * (q % 4) + 128], of[:, q], ident)
                ins.then_inc(done, 1)
            pe.wait_ge(kvt_ready, 4)
            pe.wait_ge(w36_ready, 1)
            pe.wait_ge(loads, 48)
            pe.wait_ge(wv_in, 32)

            def step(g, u):
                w = 1 - u

                def conv(b):
                    n = g * GB + b
                    wait_from_one(pe, p_ready, n - 1)
                    for h in range(2):
                        ins = pe.matmul(psC[b % 2][h].rearrange("p v s -> p (v s)"), W36[:], IM[:, u, b, 512 * h:512 * h + 512], start=True, stop=True)
                    ins.then_inc(conv_done, 1)

                def project(v0, v1):
                    for v in range(v0, v1):
                        pe.matmul(psO.rearrange("p (b s) -> p b s", b=GB), WV[:, v], P[:, w, :, v], start=(v == 0), stop=False)
                if on(g, 0, NG):
                    if isinstance(g, int):
                        pe.wait_ge(im_in[u], 192 * (g // 2 + 1))
                    else:
                        pe.wait_ge(im_in[u], arrived[0])
                    conv(0)
                    conv(1)
                if on(g - 1, 0, NG):
                    pe.wait_ge(p_ready, g * GB)
                    wait_from_one(pe, ot_ready, g - 1)
                    project(0, 8)
                if on(g, 0, NG):
                    conv(2)
                    conv(3)
                if on(g - 3, 0, NG):
                    pe.wait_ge(xt_ready, 2 * (g - 2))
                    wait_from_one(pe, lg_ready, g - 3)
                    for t in range(2):
                        ins = pe.matmul(psG[:, t], XG[:, w, TOK * t:TOK * t + TOK], GW[:], start=True, stop=True)
                    ins.then_inc(gate_done, 1)
                if on(g + 1, 0, NG):
                    pe.wait_ge(kh_ready, g + 2)
                    wait_from_one(pe, h1_ready, g - 1)
                    for b in range(GB):
                        ins = pe.matmul(psL[:, b], KH[:, w, b].rearrange("p h k -> p (h k)"),
                                        VT[:, bass.ds((g + 1) * GB + b, 1)].rearrange("p b v -> p (b v)"), start=True, stop=True)
                    ins.then_inc(lam_c_done, 1)
                if on(g - 1, 0, NG):
                    project(8, DK)
                    pe.wait_ge(yc_ready, g)
                    pe.matmul(psO, WO[:], YC[:, w], start=False, stop=True).then_inc(ot_done, 1)
                if on(g, 0, NG):
                    pe.wait_ge(lc_ready, g + 1)
                    pe.wait_ge(qn_ready, g + 1)
                    wait_from_one(pe, yc_ready, g)
                    for b in range(GB):
                        ins = pe.matmul(psY[:, SP * b:SP * b + SP], LC[:, u, b].rearrange("p h v -> p (h v)"), QN[:, u, b], start=True, stop=True)
                    ins.then_inc(yc_done, 1)
                if on(g - 2, 0, NG):
                    pe.wait_ge(xn_ready, g - 1)
                    wait_from_one(pe, lg_ready, g - 2)
                    for t in range(2):
                        ins = pe.transpose(psX[:, TOK * t:TOK * t + TOK], XR[:, u, t, 0:F], ident_t)
                    ins.then_inc(xt_done, 1)
                if on(g - 1, 0, NG):
                    pe.wait_ge(ot_ready, g)
                    if on(g + 1, 0, NG):
                        pe.wait_ge(lc_ready, g + 2)
                    wait_from_one(pe, h1_ready, g - 1)
                    for t in range(2):
                        ins = pe.transpose(psH[:, t], OTs[:, w, 2 * t:2 * t + 2].rearrange("p b s -> p (b s)"), ident)
                    ins.then_inc(ht_done, 1)

            arrived = [None]
            for g in range(-1, 4):
                step(g, g % 2)
            with pe.Fori(2, 7) as j:
                arrived[0] = (j + 1) * 192
                step(j * 2, 0)
                step(j * 2 + 1, 1)
            for g in range(14, NG + 3):
                step(g, g % 2)


def ffn(nc, m):
    K, ident, ident_t, H, LG, X2h, X2l, PS = (m[n] for n in "K ident ident_t H LG X2h X2l PS".split())
    x_rows, routed, base, out_rows, sw1, sw2, w13, w2 = (m[n] for n in "x_rows routed base out_rows sw1 sw2 w13 w2".split())
    with ExitStack() as ctx:
        def sb(name, shape, dt=f32):
            return ctx.enter_context(nc.sbuf_tensor(name, shape, dt))

        def sem(name):
            return ctx.enter_context(nc.semaphore(name))

        CT = 2 * TOK
        NC = N // CT
        IC = I // 128
        of_slot, OF = sb("of_slot", [128, SLOTS]), sb("OF", [128, SLOTS], i32)
        W1h, W1l = (sb(n, [F, E, 2 * I], f32r) for n in ("W1h", "W1l"))
        W2 = sb("W2", [128, E, IC, 2, F], f32r)
        with ExitStack() as own:
            def sbo(name, shape, dt=f32):
                return own.enter_context(nc.sbuf_tensor(name, shape, dt))
            lmax, top = sbo("lmax", [TOK, NT]), sbo("top", [TOK, NT])
            OH, RK = sbo("OH", [TOK, E, NT]), sbo("RK", [TOK, E, NT])
            CNT, INCL, ones_s = sbo("CNT", [128, E, NT]), sbo("INCL", [128, E, NT]), sbo("ones_s", [128, E * NT])
            n_e, tiles_e, ends, starts, first = (sbo(n, [128, E]) for n in ("n_e", "tiles_e", "ends", "starts", "first"))
            n_i = sbo("n_int", [128, E], i32)
            posf, POS = sbo("posf", [TOK, NT]), sbo("POS", [TOK, NT], i32)
            pos_t = sbo("pos_t", [TOK, 8], i32)
            SR1, SR2 = sbo("SR1", [F, I]), sbo("SR2", [128, IC, F])
            S1h, S1l = (sbo(n, [F, I], f32r) for n in ("S1h", "S1l"))
            S2 = sbo("S2", [128, IC, 2, F], f32r)
            WR1, WR2 = sbo("WR1", [F, 2 * I]), sbo("WR2", [128, IC, F])
            GF = sbo("GF", [128, IC, CT])
            Gh, Gl = (sbo(n, [128, 2, IC, CT], f32r) for n in ("Gh", "Gl"))
            BS = sbo("BS", [TOK, 2, 2, F])
            RB = sbo("RB", [TOK, 2, 4, ROW])
            shared(nc, locals())
        XS = sb("XS", [128, 4, ROW])
        BG, TO = sb("BG", [128, 4, F]), sb("TO", [128, 4, 2], i32)
        Xh, Xl = (sb(n, [F, 2, 128], f32r) for n in ("Xh", "Xl"))
        SG, GX = sb("SG", [128, 2, I]), sb("GX", [128, 2, I])
        Gh, Gl = (sb(n, [128, 2, IC, 128], f32r) for n in ("GTh", "GTl"))
        OS = sb("OS", [128, 2, F])
        experts(nc, locals())


def shared(nc, m):
    K, ident, ident_t, H, LG, X2h, X2l, PS = (m[n] for n in "K ident ident_t H LG X2h X2l PS".split())
    x_rows, routed, base, sw1, sw2, w13, w2 = (m[n] for n in "x_rows routed base sw1 sw2 w13 w2".split())
    lmax, top, OH, RK, CNT, INCL, ones_s, n_e, n_i, tiles_e, ends, starts, first, posf, POS, pos_t, of_slot, OF = (
        m[n] for n in "lmax top OH RK CNT INCL ones_s n_e n_i tiles_e ends starts first posf POS pos_t of_slot OF".split())
    SR1, SR2, S1h, S1l, S2, WR1, WR2, W1h, W1l, W2, GF, Gh, Gl, BS, RB = (
        m[n] for n in "SR1 SR2 S1h S1l S2 WR1 WR2 W1h W1l W2 GF Gh Gl BS RB".split())
    CT, NC, IC = m["CT"], m["NC"], m["IC"]
    with ExitStack() as ctx:
        def sem(name):
            return ctx.enter_context(nc.semaphore(name))

        s_in, s_hi, s_ready = sem("s_in"), sem("s_hi"), sem("s_ready")
        w1_in, w2_in, w_hi, w_lo = sem("w1_in"), sem("w2_in"), sem("we_hi"), sem("we_lo")
        oh_ready, rank_done, pos_ready = sem("oh_ready"), sem("rank_done"), sem("pos_ready")
        rb_in, scattered, pos_copied = [sem(f"rb_in{n}") for n in range(2)], [sem(f"scattered{n}") for n in range(2)], sem("pos_copied")
        g_done, gelu_ready, gh_ready, gl_ready = sem("g_done"), sem("gelu_ready"), sem("gh_ready"), sem("gl_ready")
        y_done, bs_ready, base_stored = sem("y_done"), sem("bs_ready"), [sem("base_stored0"), sem("base_stored1")]
        dve_link, turn = sem("dve_link3"), sem("turn")

        psG = [[PS[2 * u + h][:, 0:2 * CT].rearrange("p (i s) -> p i s", i=2) for h in range(2)] for u in range(2)]
        psY = [PS[4 + u][0:TOK, :].rearrange("p (t h f) -> p t h f", t=2, h=2) for u in range(2)]
        psR, psN = PS[6][0:TOK, 0:E * NT], PS[7][:, 0:E * NT]
        block = ctx.enter_context(nc.Block())

        @block.sync
        def _(sp):
            sp.dma_start(SR1[:], sw1).then_inc(s_in, 16)
            sp.dma_start(SR2[:], sw2).then_inc(s_in, 16)

            def step(c, u):
                if on(c, 0, NC) and u == 0:
                    e = c // 2 if isinstance(c, int) else expert[0]
                    wait_from_one(sp, w_lo, e)
                    sp.dma_start(WR1[:], w13[:, bass.ds(e, 1)].rearrange("p e i -> p (e i)")).then_inc(w1_in, 16)
                    sp.dma_start(WR2[:], w2[:, bass.ds(e, 1)].rearrange("p e i f -> p (e i f)")).then_inc(w2_in, 16)
                if on(c - 2, 0, NC):
                    sp.wait_ge(bs_ready, c - 1)
                    sp.dma_start(base[bass.ds((c - 2) * CT, CT), :].rearrange("(t p) f -> p t f", p=TOK), BS[:, u]).then_inc(base_stored[u], 16)
            expert = [None]
            for c in range(0, 4):
                step(c, c % 2)
            with sp.Fori(2, 8) as j:
                expert[0] = j
                step(j * 2, 0)
                step(j * 2 + 1, 1)
            for c in range(NC, NC + 2):
                step(c, c % 2)
            for u in range(2):
                sp.wait_ge(base_stored[u], 16 * NC // 2)

        @block.gpsimd
        def _(pool):
            pool.wait_ge(pos_ready, 1)

            def load(i, h):
                pool.dma_start(RB[:, h], x_rows[bass.ds(i * 4 * TOK, 4 * TOK), :].rearrange("(t p) c -> p t c", p=TOK)).then_inc(rb_in[h], 16)

            def group(j, h, first, last):
                i = 2 * j + h
                if not first:
                    pool.wait_ge(scattered[h], j * 64)
                pool.wait_ge(rb_in[h], j * 16 + 16)
                pool.tensor_copy(pos_t[:, 4 * h:4 * h + 4], POS[:, bass.ds(i * 4, 4)]).then_inc(pos_copied, 1)
                pool.wait_ge(pos_copied, i + 1)
                hold_waits(pool, turn)
                for n in range(4):
                    pool.indirect_dma_start(routed, bass.IndirectOffsetOnAxis(pos_t[:, 4 * h + n:4 * h + n + 1], 0), RB[:, h, n], None).then_inc(scattered[h], 16)
                if not last:
                    if not (first and h == 0):
                        pool.wait_ge(scattered[1 - h], (j + h) * 64)
                    load(i + 1, 1 - h)
            load(0, 0)
            group(0, 0, True, False)
            group(0, 1, True, False)
            with pool.Fori(1, NT // 8 - 1) as j:
                group(j, 0, False, False)
                group(j, 1, False, False)
            group(NT // 8 - 1, 0, False, False)
            group(NT // 8 - 1, 1, False, True)
            for h in range(2):
                pool.wait_ge(scattered[h], 16 * NT // 2)

        @block.scalar
        def _(act):
            act.wait_ge(s_in, 32)
            act.activation(S1h[:], SR1[:], ACT.Copy).then_inc(s_hi, 1)
            act.activation(S2[:, :, 0], SR2[:], ACT.Copy).then_inc(s_hi, 1)

            def step(c, u, e):
                act.wait_ge(g_done, c + 1)
                wait_from_one(act, gl_ready, c)
                for h in range(2):
                    act.activation(GF[:, 2 * h:2 * h + 2], psG[u][h], ACT.Gelu).then_inc(gelu_ready, 1)
                if u == 0:
                    act.wait_ge(w1_in, 16 * (e + 1))
                    act.activation(W1h[:, bass.ds(e, 1)].rearrange("p e i -> p (e i)"), WR1[:], ACT.Copy).then_inc(w_hi, 1)
                else:
                    act.wait_ge(w2_in, 16 * (e + 1))
                    act.activation(W2[:, bass.ds(e, 1), :, 0].rearrange("p e i f -> p (e i) f"), WR2[:], ACT.Copy).then_inc(w_hi, 1)
            for c in range(0, 4):
                step(c, c % 2, c // 2)
            with act.Fori(2, 8) as j:
                step(j * 2, 0, j)
                step(j * 2 + 1, 1, j)

        @block.vector
        def _(dve):
            L = Links(dve, dve_link)
            dve.wait_ge(s_hi, 2)
            dve.tensor_tensor(S1l[:], SR1[:], S1h[:].bitcast(f32), ALU.subtract).then_inc(s_ready, 1)
            dve.tensor_tensor(S2[:, :, 1], SR2[:], S2[:, :, 0].bitcast(f32), ALU.subtract).then_inc(s_ready, 1)
            rev = K[0:TOK, K_REV:K_REV + E].unsqueeze(1).broadcast_to([TOK, NT, E])
            L.made(dve.memset(ones_s[:], 1.0))
            L.link(dve.tensor_reduce(lmax[:], LG[:], AX.X, ALU.max))
            L.link(dve.tensor_tensor(LG[:], LG[:], lmax[:].unsqueeze(2).broadcast_to([TOK, NT, E]), ALU.is_equal))
            L.link(dve.tensor_tensor(LG[:], LG[:], rev, ALU.mult))
            L.link(dve.tensor_reduce(top[:], LG[:], AX.X, ALU.max))
            dve.tensor_tensor(OH[:].rearrange("p e t -> p t e"), rev, top[:].unsqueeze(2).broadcast_to([TOK, NT, E]),
                              ALU.is_equal).then_inc(oh_ready, 1)
            dve.wait_ge(rank_done, 2)
            flat = "p e t -> p (e t)"
            L.link(dve.tensor_copy(CNT[:].rearrange(flat), psN))
            L.link(dve.tensor_tensor_scan(INCL[:].rearrange(flat), ones_s[:], CNT[:].rearrange(flat), 0.0, ALU.mult, ALU.add))
            L.link(dve.tensor_tensor(CNT[:], INCL[:], CNT[:], ALU.subtract))
            L.link(dve.tensor_tensor(n_e[:], INCL[:, :, NT - 1], CNT[:, :, 0], ALU.subtract))
            L.link(dve.tensor_scalar(n_i[:], n_e[:], 127.0, None, ALU.add))
            L.link(dve.tensor_scalar(n_i[:], n_i[:], 7, None, ALU.logical_shift_right))
            L.link(dve.tensor_copy(tiles_e[:], n_i[:]))
            L.link(dve.tensor_tensor_scan(ends[:], ones_s[:, 0:E], tiles_e[:], 0.0, ALU.mult, ALU.add))
            L.link(dve.tensor_tensor(starts[:], ends[:], tiles_e[:], ALU.subtract))
            L.link(dve.scalar_tensor_tensor(first[:], starts[:], 128.0, CNT[:, :, 0], ALU.mult, ALU.subtract))
            L.link(dve.tensor_tensor(RK[:].rearrange(flat), psR, CNT[0:TOK].rearrange(flat), ALU.add))
            L.link(dve.tensor_tensor(RK[:], RK[:], first[0:TOK].unsqueeze(2).broadcast_to([TOK, E, NT]), ALU.add))
            L.link(dve.tensor_tensor(RK[:], RK[:], OH[:], ALU.mult))
            L.link(dve.tensor_reduce(posf[:], RK[:].rearrange("p e t -> p t e"), AX.X, ALU.add))
            dve.tensor_copy(POS[:], posf[:]).then_inc(pos_ready, 1)
            L.link(dve.tensor_scalar(of_slot[:], K[:, K_IO:K_IO + SLOTS], starts[:, 1:2], None, ALU.is_ge))
            for e in range(2, E):
                L.link(dve.scalar_tensor_tensor(of_slot[:], K[:, K_IO:K_IO + SLOTS], starts[:, e:e + 1], of_slot[:], ALU.is_ge, ALU.add))
            L.link(dve.tensor_copy(OF[:], of_slot[:]))

            def step(c, u, e):
                w = 1 - u
                if on(c, 0, NC):
                    dve.wait_ge(gelu_ready, 2 * (c + 1))
                    wait_from_one(dve, y_done, c - 1)
                    dve.tensor_copy(Gh[:, u], GF[:]).then_inc(gh_ready, 1)
                    dve.wait_ge(gh_ready, c + 1)
                    dve.tensor_tensor(Gl[:, u], GF[:], Gh[:, u].bitcast(f32), ALU.subtract).then_inc(gl_ready, 1)
                    dve.wait_ge(w_hi, c + 1)
                    if u == 0:
                        L.made(dve.tensor_tensor(W1l[:, bass.ds(e, 1)].rearrange("p e i -> p (e i)"), WR1[:],
                                                 W1h[:, bass.ds(e, 1)].rearrange("p e i -> p (e i)").bitcast(f32), ALU.subtract))
                    else:
                        dve.tensor_tensor(W2[:, bass.ds(e, 1), :, 1].rearrange("p e i f -> p (e i) f"), WR2[:],
                                          W2[:, bass.ds(e, 1), :, 0].rearrange("p e i f -> p (e i) f").bitcast(f32), ALU.subtract).then_inc(w_lo, 1)
                if on(c - 1, 0, NC):
                    dve.wait_ge(y_done, c)
                    if isinstance(c, int):
                        if c >= 3:
                            dve.wait_ge(base_stored[w], 16 * ((c - 1) // 2))
                    else:
                        dve.wait_ge(base_stored[w], freed[0])
                    L.link(dve.tensor_tensor(BS[:, w], psY[w][:, :, 0], H[:, bass.ds((c - 1) * 2, 2)], ALU.add))
                    dve.tensor_tensor(BS[:, w], psY[w][:, :, 1], BS[:, w], ALU.add).then_inc(bs_ready, 1)
            freed = [None]
            for c in range(0, 4):
                step(c, c % 2, c // 2)
            with dve.Fori(2, 8) as j:
                L.loop(2, j, 3)
                freed[0] = (j - 1) * 16
                step(j * 2, 0, j)
                freed[0] = j * 16
                step(j * 2 + 1, 1, j)
            L.end(6)
            step(NC, 0, None)

        @block.tensor
        def _(pe):
            pe.wait_ge(s_ready, 2)

            def step(c, u):
                w = 1 - u
                if on(c, 0, NC):
                    wait_from_one(pe, gelu_ready, 2 * (c - 1))
                    ts = bass.ds(c * CT, CT)
                    for i in range(IC):
                        for n, (a, x) in enumerate(((S1h, X2h), (S1l, X2h), (S1h, X2l))):
                            ins = pe.matmul(psG[u][i // 2][:, i % 2], a[:, 128 * i:128 * i + 128], x[:, ts], start=(n == 0), stop=(n == 2))
                    ins.then_inc(g_done, 1)
                if on(c - 1, 0, NC):
                    pe.wait_ge(gl_ready, c)
                    wait_from_one(pe, bs_ready, c - 2)
                    for t in range(2):
                        for i in range(IC):
                            for n, a in enumerate((Gh, Gl)):
                                ins = pe.matmul(psY[w][:, t].rearrange("p h f -> p (h f)"), a[:, w, i, TOK * t:TOK * t + TOK],
                                                S2[:, i].rearrange("p h f -> p (h f)"), start=(i == 0 and n == 0), stop=(i == IC - 1 and n == 1))
                    ins.then_inc(y_done, 1)
            step(0, 0)
            pe.wait_ge(oh_ready, 1)
            flat = OH[:].rearrange("p e t -> p (e t)")
            pe.matmul(psR, K[0:TOK, K_LR:K_LR + TOK], flat, start=True, stop=True).then_inc(rank_done, 1)
            pe.matmul(psN, K[0:TOK, K_ONE:K_ONE + 128], flat, start=True, stop=True).then_inc(rank_done, 1)
            for c in range(1, 4):
                step(c, c % 2)
            with pe.Fori(2, 8) as j:
                step(j * 2, 0)
                step(j * 2 + 1, 1)
            step(NC, 0)


def experts(nc, m):
    K, ident, PS, OF = (m[n] for n in "K ident PS OF".split())
    routed, base, out_rows = m["routed"], m["base"], m["out_rows"]
    W1h, W1l, W2, XS, BG, TO, Xh, Xl, SG, GX, Gh, Gl, OS, IC = (
        m[n] for n in "W1h W1l W2 XS BG TO Xh Xl SG GX Gh Gl OS IC".split())
    with ExitStack() as ctx:
        def sem(name):
            return ctx.enter_context(nc.semaphore(name))

        xs_in, bg_in, stored = [sem(f"xs_in{n}") for n in range(4)], [sem(f"bg_in{n}") for n in range(4)], [sem("stored0"), sem("stored1")]
        bg_set, to_ready, dve_link, turn = sem("bg_set"), [sem("to_ready0"), sem("to_ready1")], sem("dve_link4"), sem("turn3")
        xt_done, xh_ready, xl_ready = sem("xt3_done"), sem("xh_ready"), sem("xl_ready")
        up_done, sg_ready, gx_ready, gt_done, gh_ready, gl_ready, y_done, os_ready = (
            sem(n) for n in ("up_done", "sg_ready", "gx_ready", "gt_done", "gth_ready", "gtl_ready", "y3_done", "os_ready"))
        psU = [[PS[2 * u + h][:, :] for h in range(2)] for u in range(2)]
        psX, psT = PS[4][:, 0:128], PS[5][:, :].rearrange("p (i s) -> p i s", i=IC)
        psY = [PS[6 + u][:, 0:2 * F] for u in range(2)]
        block = ctx.enter_context(nc.Block())

        LAST = SLOTS + 3

        def run(step, eng, links=None):
            for k in range(-2, 4):
                step(k, k % 4, None)
            with eng.Fori(1, 9) as j:
                if links is not None:
                    links.loop(1, j, 4)
                for n in range(4):
                    step(j * 4 + n, n, j)
            if links is not None:
                links.end(8)
            for k in range(36, LAST):
                step(k, k % 4, None)

        def wait_use(eng, sems, k, n, j, d):
            eng.wait_ge(sems[(n + d) % 4], 16 * ((k + d) // 4 + 1) if j is None else (j + (n + d) // 4) * 16 + 16)

        @block.sync
        def _(sp):
            def load(m, t):
                sp.dma_start(XS[:, t], routed[bass.ds(m * 128, 128), :]).then_inc(xs_in[t], 16)

            def step(k, n, j):
                if k is not None and on(k + 3, 0, SLOTS):
                    m = k + 3 if isinstance(k, int) else sp.snap(k + 3)
                    if not isinstance(k, int) or k > 0:
                        sp.wait_ge(xt_done, k)
                        sp.wait_ge(to_ready[1], k)
                    load(m, (n + 3) % 4)
            load(0, 0)
            run(step, sp)

        @block.gpsimd
        def _(pool):
            pool.memset(BG[:], 0.0).then_inc(bg_set, 1)
            pool.wait_ge(bg_set, 1)

            def step(k, n, j):
                t = (n + 2) % 4
                if on(k - 2, 0, SLOTS):
                    pool.wait_ge(os_ready, k - 1)
                    hold_waits(pool, turn)
                    pool.tensor_copy(TO[:, t, 0:1], TO[:, t, 1:2]).then_inc(to_ready[0], 1)
                    pool.wait_ge(to_ready[0], k - 1)
                if on(k + 2, 0, SLOTS):
                    wait_use(pool, xs_in, k, n, j, 2)
                    hold_waits(pool, turn)
                    pool.tensor_copy(TO[:, t, 1:2], XS[:, t, F:F + 1].bitcast(i32)).then_inc(to_ready[1], 1)
                if on(k - 2, 0, SLOTS):
                    hold_waits(pool, turn)
                    pool.indirect_dma_start(out_rows, bass.IndirectOffsetOnAxis(TO[:, t, 0:1], 0), OS[:, n % 2], None,
                                            bounds_check=N - 1, oob_is_err=False).then_inc(stored[n % 2], 16)
                if on(k + 2, 0, SLOTS):
                    pool.wait_ge(to_ready[1], k + 3)
                    hold_waits(pool, turn)
                    pool.indirect_dma_start(BG[:, t], None, base, bass.IndirectOffsetOnAxis(TO[:, t, 1:2], 0),
                                            bounds_check=N - 1, oob_is_err=False).then_inc(bg_in[t], 16)
            run(step, pool)
            pool.wait_ge(stored[0], 16 * ((SLOTS + 1) // 2))
            pool.wait_ge(stored[1], 16 * (SLOTS // 2))

        @block.scalar
        def _(act):
            def step(k, n, j):
                u, w = n % 2, 1 - n % 2
                if on(k, 0, SLOTS):
                    act.wait_ge(up_done, 2 * k + 1)
                    wait_from_one(act, gx_ready, k - 1)
                    act.activation(SG[:, u], psU[u][0], ACT.Silu).then_inc(sg_ready, 1)
                if on(k - 1, 0, SLOTS):
                    act.wait_ge(gt_done, k)
                    wait_from_one(act, y_done, k - 2)
                    act.activation(Gh[:, w], psT, ACT.Copy).then_inc(gh_ready, 1)
                if on(k + 1, 0, SLOTS):
                    act.wait_ge(xt_done, k + 2)
                    wait_from_one(act, up_done, 2 * k)
                    act.activation(Xh[:, w], psX, ACT.Copy).then_inc(xh_ready, 1)
            run(step, act)

        @block.vector
        def _(dve):
            L = Links(dve, dve_link)

            def step(k, n, j):
                u, w = n % 2, 1 - n % 2
                if on(k - 1, 0, SLOTS):
                    dve.wait_ge(gh_ready, k)
                    dve.tensor_tensor(Gl[:, w], psT, Gh[:, w].bitcast(f32), ALU.subtract).then_inc(gl_ready, 1)
                if on(k, 0, SLOTS):
                    dve.wait_ge(up_done, 2 * k + 2)
                    dve.wait_ge(sg_ready, k + 1)
                    wait_from_one(dve, gt_done, k - 1)
                    dve.tensor_tensor(GX[:, u], psU[u][1], SG[:, u], ALU.mult).then_inc(gx_ready, 1)
                if on(k + 1, 0, SLOTS):
                    dve.wait_ge(xh_ready, k + 2)
                    dve.tensor_tensor(Xl[:, w], psX, Xh[:, w].bitcast(f32), ALU.subtract).then_inc(xl_ready, 1)
                if on(k - 2, 0, SLOTS):
                    t = (n + 2) % 4
                    dve.wait_ge(y_done, k - 1)
                    if j is None:
                        dve.wait_ge(bg_in[t], 16 * ((k - 2) // 4 + 1))
                        if k - 4 >= 0:
                            dve.wait_ge(stored[u], 16 * ((k - 4) // 2 + 1))
                    else:
                        dve.wait_ge(bg_in[t], (j + (n - 2) // 4) * 16 + 16)
                        dve.wait_ge(stored[u], j * 32 + 16 * ((n - 4) // 2 + 1))
                    L.link(dve.tensor_tensor(OS[:, u], psY[u][:, 0:F], BG[:, t], ALU.add))
                    dve.tensor_tensor(OS[:, u], psY[u][:, F:2 * F], OS[:, u], ALU.add).then_inc(os_ready, 1)
            run(step, dve, L)

        @block.tensor
        def _(pe):
            def step(k, n, j):
                u, w = n % 2, 1 - n % 2
                if on(k, 0, SLOTS):
                    e = pe.value_load(OF[0:1, bass.ds(k, 1)], min_val=0, max_val=E - 1)
                    pe.wait_ge(xl_ready, k + 1)
                    wait_from_one(pe, gx_ready, k - 1)
                    for h in range(2):
                        for p, (a, b) in enumerate(((Xh, W1h), (Xh, W1l), (Xl, W1h))):
                            ins = pe.matmul(psU[u][h], a[:, u], b[:, bass.ds(e, 1), I * h:I * h + I].rearrange("p e i -> p (e i)"), start=(p == 0), stop=(p == 2))
                        ins.then_inc(up_done, 1)
                if on(k + 1, 0, SLOTS):
                    wait_use(pe, xs_in, k, n, j, 1)
                    wait_from_one(pe, xl_ready, k + 1)
                    pe.transpose(psX, XS[:, (n + 1) % 4, 0:F], ident).then_inc(xt_done, 1)
                if on(k - 1, 0, SLOTS):
                    pe.wait_ge(gx_ready, k)
                    wait_from_one(pe, gl_ready, k - 1)
                    for i in range(IC):
                        ins = pe.transpose(psT[:, i], GX[:, w, 128 * i:128 * i + 128], ident)
                    ins.then_inc(gt_done, 1)
                if on(k - 2, 0, SLOTS):
                    e = pe.value_load(OF[0:1, bass.ds(k - 2, 1)], min_val=0, max_val=E - 1)
                    pe.wait_ge(gl_ready, k - 1)
                    wait_from_one(pe, os_ready, k - 3)
                    for i in range(IC):
                        for p, a in enumerate((Gh, Gl)):
                            ins = pe.matmul(psY[u], a[:, u, i], W2[:, bass.ds(e, 1), i].rearrange("p e h f -> p (e h f)"),
                                            start=(i == 0 and p == 0), stop=(i == IC - 1 and p == 1))
                    ins.then_inc(y_done, 1)
            run(step, pe)


def lay_out(x, L0_tok_W, L0_tok_b, L0_attn_Wq, L0_attn_bq, L0_attn_Wk, L0_attn_bk, L0_attn_Wv, L0_attn_bv,
            L0_attn_gq, L0_attn_betaq, L0_attn_gv, L0_attn_betav, L0_attn_Wpos, L0_attn_Wout, L0_attn_bout,
            L0_ffn_gate_w, L0_ffn_w1, L0_ffn_w2, L0_ffn_w3, L0_ffn_sw1, L0_ffn_sw2):
    x = np.asarray(x)
    time = np.arange(S + 1, dtype=np.float32) / np.float32(S)
    path = np.empty((NB, S + 1, C), np.float32)
    path[:, :, 0] = time
    path[:, :, 1:] = x

    def tokens(a):
        return a.reshape(NT, TOK, C).transpose(1, 0, 2)
    W = np.asarray(L0_tok_W)
    o4 = C + C2 + C3
    wsig = np.zeros((128, NCH + 1, C, F), np.float32)
    wsig[:, :NCH] = W[:, o4:].reshape(F, NCH, 128, C).transpose(2, 1, 3, 0)
    wsig[0:C2, NCH] = W[:, C + C2:o4].reshape(F, C2, C).transpose(1, 2, 0)
    wsig[C2:C2 + C, NCH] = W[:, C:C + C2].reshape(F, C, C).transpose(1, 2, 0)
    wsig[C2 + C, NCH] = W[:, 0:C].T
    K = np.zeros((128, K_END), np.float32)
    K[:, K_ID:K_ID + 128] = np.eye(128)
    r, s = np.arange(TOK)[:, None], np.arange(TOK)[None, :]
    same = r // S == s // S
    K[0:TOK, K_LX:K_LX + TOK] = same & (r < s)
    K[0:TOK, K_LI:K_LI + TOK] = same & (r <= s)
    K[0:TOK, K_LR:K_LR + TOK] = r < s
    K[:, K_ONE:K_ONE + 128] = 1
    K[:, K_MB:K_MB + NH] = np.arange(128)[:, None] // DK == np.arange(NH)[None, :]
    K[:, K_REV:K_REV + E] = E - np.arange(E)
    K[:, K_IO:K_IO + SLOTS] = np.arange(SLOTS)
    K[0:18, K_CV], K[18:36, K_CV] = 1, -1
    K[18:36, K_CV + 1] = 1

    def rows(a, n):
        return np.broadcast_to(np.asarray(a)[None, :], (n, len(a)))
    vecs = np.zeros((128, 7), np.float32)
    for c, a in enumerate((L0_attn_gq, L0_attn_betaq, L0_attn_bq, L0_attn_bout)):
        vecs[:, c] = np.asarray(a)
    for c, a in enumerate((L0_attn_gv, L0_attn_betav, L0_attn_bv)):
        vecs[0:DK, P_GV + c] = np.asarray(a)
    return dict(
        path_now=tokens(path[:, :-1]), path_next=tokens(path[:, 1:]),
        path_first=tokens(np.broadcast_to(path[:, 0:1], (NB, S, C))),
        wsig=wsig.reshape(128, NCH + 1, 2, 512), consts=K,
        token_ids=(np.arange(NT)[None, :] * TOK + np.arange(TOK)[:, None]).astype(np.int32), tok_b=rows(L0_tok_b, TOK),
        qkv_b=rows(np.concatenate([np.asarray(a) for a in (L0_attn_bq, L0_attn_bk, L0_attn_bv)]), TOK),
        vecs=vecs, wqkv=np.concatenate([np.asarray(a) for a in (L0_attn_Wq, L0_attn_Wk, L0_attn_Wv)], axis=1),
        wpos=np.broadcast_to(np.asarray(L0_attn_Wpos).reshape(DK, 9).T[None, :, None, :], (4, 9, NH, DK)).reshape(36, 128),
        wout_v=np.broadcast_to(np.asarray(L0_attn_Wout).reshape(NH, 1, DK, F), (NH, DK, DK, F)).reshape(128, DK, F),
        wout=np.asarray(L0_attn_Wout), gate_w=np.asarray(L0_ffn_gate_w).T,
        sw1=np.asarray(L0_ffn_sw1).T, sw2=np.asarray(L0_ffn_sw2).T.reshape(4, 128, F).transpose(1, 0, 2),
        w13=np.concatenate([np.asarray(L0_ffn_w1), np.asarray(L0_ffn_w3)], axis=1).transpose(2, 0, 1),
        w2=np.asarray(L0_ffn_w2).transpose(0, 2, 1).reshape(E, 4, 128, F).transpose(2, 0, 1, 3),
    )


INPUTS = ("path_now", "path_next", "path_first", "wsig", "consts", "token_ids", "tok_b", "qkv_b", "vecs", "wqkv", "wpos",
          "wout_v", "wout", "gate_w", "sw1", "sw2", "w13", "w2")


def kernel(**inputs):
    import concourse.bacc as bacc
    from concourse.bass_utils import run_bass_kernel_spmd

    laid = lay_out(**inputs)
    nc = bacc.Bacc("TRN2", target_bir_lowering=False, num_devices=1)
    arrays, args = {}, []
    for name in INPUTS:
        a = np.ascontiguousarray(laid[name])
        arrays[f"in_{name}"] = a
        args.append(nc.dram_tensor(f"in_{name}", a.shape, mybir.dt.from_np(a.dtype), kind="ExternalInput").ap())
    args.append(nc.dram_tensor("out_h", (NB, S, F), f32, kind="ExternalOutput").ap())
    build(nc, *args)
    result = run_bass_kernel_spmd(nc, [arrays], core_ids=[0])
    return result.results[0]["out_h"]
```

```python
import concourse.bass as bass
from concourse import mybir
from contextlib import ExitStack
import numpy as np

f32 = mybir.dt.float32
f32r = mybir.dt.float32r
i32 = mybir.dt.int32
u32 = mybir.dt.uint32
ALU = mybir.AluOpType
ACT = mybir.ActivationFunctionType
AX = mybir.AxisListType

NB, S, F = 64, 63, 128
C = 8
NT, TOK = 32, 126
N = NB * S
DK, NH = 16, 8
QKV = F + 2 * DK
C3, C2 = C ** 3, C ** 2
TAIL = C2 + C + 1
NCH = C3 // 128
EPS = 1e-5
SP = 64
VB = 18 * SP + SP
GB = 4
NG = NB // GB
E, I = 8, 512
SLOTS = 39
ROW = 132
NOBODY = 1 << 20

K_ID, K_LX, K_LI, K_LR, K_ONE, K_MB, K_REV, K_IO = 0, 128, 254, 380, 506, 634, 642, 650
K_CV = K_IO + SLOTS
K_END = K_CV + 2
P_GQ, P_BETAQ, P_BQ, P_BOUT, P_GV, P_BETAV, P_BV = range(7)


class Links:

    def __init__(self, eng, sem):
        self.eng, self.sem, self.base, self.n = eng, sem, 0, 0

    def made(self, ins):
        ins.then_inc(self.sem, 1)
        self.n += 1

    def wait(self):
        self.eng.wait_ge(self.sem, self.base + self.n)

    def link(self, ins):
        self.made(ins)
        self.wait()

    def loop(self, first, i, per):
        self.start, self.per = self.n, per
        self.base = self.n + (i - first) * per
        self.n = 0

    def end(self, passes):
        assert self.n == self.per, (self.n, self.per)
        self.n = self.start + passes * self.per
        self.base = 0


def on(k, low, high):
    return not isinstance(k, int) or low <= k < high


def hold_waits(eng, turn):
    eng.nop().then_inc(turn, 1)


def wait_from_one(eng, sem, value):
    if not isinstance(value, int) or value > 0:
        eng.wait_ge(sem, value)


def build(nc, path_now, path_next, path_first, wsig, consts, token_ids, tok_b, qkv_b, vecs, wqkv, wpos, wout_v, wout,
          gate_w, sw1, sw2, w13, w2, out):
    q_raw = nc.dram_tensor("q_raw", [N, F], f32, kind="Internal").ap()
    k_raw = nc.dram_tensor("k_raw", [N, DK], f32, kind="Internal").ap()
    v_raw = nc.dram_tensor("v_raw", [N, DK], f32, kind="Internal").ap()

    v_pad = nc.dram_tensor("v_pad", [2, NB, VB], f32, kind="Internal").ap()
    pat_q = nc.dram_tensor("pat_q", [2, S, F], f32, kind="Internal").ap()
    x_rows = nc.dram_tensor("x_rows", [N, ROW], f32, kind="Internal").ap()
    routed = nc.dram_tensor("routed", [SLOTS * 128, ROW], f32, kind="Internal").ap()
    base = nc.dram_tensor("base", [N, F], f32, kind="Internal").ap()
    out_rows = out.rearrange("b s f -> (b s) f")

    with ExitStack() as whole:
        def keep(name, shape, dt=f32):
            return whole.enter_context(nc.sbuf_tensor(name, shape, dt))

        K = keep("K", [128, K_END])
        ident, ident_t = K[:, K_ID:K_ID + 128], K[0:TOK, K_ID:K_ID + TOK]
        before, upto_now = K[0:TOK, K_LX:K_LX + TOK], K[0:TOK, K_LI:K_LI + TOK]
        H = keep("H", [TOK, NT, F])
        PV = keep("PV", [128, 7])
        eps = keep("eps", [128, 1])
        carrier = keep("carrier", [1, 1])
        stQ, stV = keep("stQ", [128, NT, 6]), keep("stV", [DK, NT, 6])
        LG = keep("LG", [TOK, NT, E])
        X2h, X2l = keep("X2h", [128, N], f32r), keep("X2l", [128, N], f32r)
        S1h, S1l = keep("S1h", [F, I], f32r), keep("S1l", [F, I], f32r)
        S2 = keep("S2", [128, I // 128, 2, F], f32r)
        PS = [whole.enter_context(nc.psum_tensor(f"PS{n}", [128, 512], f32)) for n in range(8)]
        with ExitStack() as attn:
            def early(name, shape, dt=f32):
                return attn.enter_context(nc.sbuf_tensor(name, shape, dt))
            QR = early("QR", [128, NB, SP])
            SR1, SR2 = early("SR1", [F, I]), early("SR2", [128, I // 128, F])
            WP, WV, WO, GW = early("WP", [36, 128]), early("WV", [128, DK, F]), early("WO", [128, F]), early("GW", [F, E])
            IDS, nobody = early("IDS", [TOK, NT], i32), early("nobody", [128, ROW])
            early_in, routed_set, q_loaded = (attn.enter_context(nc.semaphore(n)) for n in ("early_in", "routed_set", "q_loaded"))
            signatures(nc, locals())
            attention(nc, locals())
        ffn(nc, locals())


def signatures(nc, m):
    K, ident_t, before, upto_now, H, PV, eps, carrier = (m[n] for n in "K ident_t before upto_now H PV eps carrier".split())
    stQ, stV, PS, QR, q_raw, k_raw, v_raw = (m[n] for n in "stQ stV PS QR q_raw k_raw v_raw".split())
    path_now, path_next, path_first, wsig, consts, tok_b, qkv_b, vecs, wqkv = (
        m[n] for n in "path_now path_next path_first wsig consts tok_b qkv_b vecs wqkv".split())
    wpos, gate_w, token_ids, wout_v, wout, sw1, sw2, routed = (m[n] for n in "wpos gate_w token_ids wout_v wout sw1 sw2 routed".split())
    WP, GW, IDS, WV, WO, SR1, SR2, nobody, early_in, routed_set, q_loaded = (
        m[n] for n in "WP GW IDS WV WO SR1 SR2 nobody early_in routed_set q_loaded".split())
    with ExitStack() as ctx:
        def sb(name, shape, dt=f32):
            return ctx.enter_context(nc.sbuf_tensor(name, shape, dt))

        def sem(name):
            return ctx.enter_context(nc.semaphore(name))

        pnow, pnext, pfirst = (sb(n, [TOK, NT, C]) for n in ("pnow", "pnext", "pfirst"))
        V, Vhalf, Vthird, S1, C2h, C3h, C4h = (sb(n, [TOK, NT, C]) for n in ("V", "Vhalf", "Vthird", "S1", "C2h", "C3h", "C4h"))
        E2, E3, A2T = (sb(n, [TOK, NT, C, C]) for n in ("E2", "E3", "A2T"))
        A2X = sb("A2X", [TOK, NT, TAIL])
        INC, TOP = (sb(n, [TOK, 2, C3]) for n in ("INC", "TOP"))
        AXs = sb("AXs", [TOK, 2, TAIL])
        Ah, Al = (sb(n, [128, 2, NCH + 1, TOK], f32r) for n in ("Ah", "Al"))
        WR = sb("WR", [128, 2, 2, 512])
        Wh, Wl = (sb(n, [128, NCH + 1, 2, 512], f32r) for n in ("Wh", "Wl"))
        Vt = sb("Vt", [TOK, 2, C])
        Z = sb("Z", [TOK, 2, F])
        tokb = sb("tokb", [TOK, F])
        qkvb = sb("qkvb", [TOK, QKV])
        wqkv_s = sb("wqkv_s", [128, QKV])
        ST, MV, SD = sb("ST", [TOK, 2, 6]), sb("MV", [TOK, 2, 2]), sb("SD", [TOK, 2, 2])
        XN = sb("XN", [TOK, 2, F])
        XT = sb("XT", [128, 2, TOK])
        QS = sb("QS", [TOK, 2, QKV])

        psA = PS[0][:, 0:NCH * TOK].rearrange("p (c s) -> p c s", c=NCH)
        psB = PS[1][0:TAIL, 0:TOK]
        psU = [[PS[2 + 2 * u + h][0:TOK, :].rearrange("p (d o) -> p d o", d=4) for h in range(2)] for u in range(2)]
        psH = PS[6][0:TOK, 0:F]
        psX = PS[7][:, 0:TOK]
        psQKV, psQT, psVT = PS[7][0:TOK, 0:QKV], PS[7][:, QKV:QKV + TOK], PS[7][0:DK, 288:288 + TOK]

        path_in, const_in, wsig_in0, wsig_in1 = sem("path_in"), sem("const_in"), sem("wsig_in0"), sem("wsig_in1")
        small_in = sem("small_in")
        consts_set, nobody_set = sem("consts_set"), sem("nobody_set")
        w_hi, w_split = sem("w_hi"), sem("w_split")
        e2_ready, s2_done, a2_ready, a2x_ready = sem("e2_ready"), sem("s2_done"), sem("a2_ready"), sem("a2x_ready")
        inc_ready, top_ready, ax_ready, at_done = sem("inc_ready"), sem("top_ready"), sem("ax_ready"), sem("at_done")
        ah_ready, al_ready = sem("ah_ready"), sem("al_ready")
        u0_done, u1_done, c0_done, z_ready = sem("u0_done"), sem("u1_done"), sem("c0_done"), sem("z_ready")
        h_done, h_ready, mv_ready, sd_ready, xn_ready = sem("h_done"), sem("h_ready"), sem("mv_ready"), sem("sd_ready"), sem("xn_ready")
        xt_done, xt_ready, qkv_done, qs_ready, stats_done = sem("xt_done"), sem("xt_ready"), sem("qkv_done"), sem("qs_ready"), sem("stats_done")
        qs_stored = [sem("qs_stored0"), sem("qs_stored1")]
        dve_link = sem("dve_link")

        block = ctx.enter_context(nc.Block())

        def run_steps(eng, step, links=None, per=0):
            for k in range(-1, 4):
                step(k, k % 2)
            with eng.Fori(2, 15) as j:
                if links:
                    links.loop(2, j, per)
                step(j * 2, 0)
                step(j * 2 + 1, 1)
            if links:
                links.end(13)
            for k in range(30, NT + 2):
                step(k, k % 2)

        @block.sync
        def _(sp):
            sp.dma_start(pnext[:], path_next).then_inc(path_in, 16)
            sp.dma_start(pnow[:], path_now).then_inc(path_in, 16)
            sp.dma_start(pfirst[:], path_first).then_inc(path_in, 16)
            sp.dma_start(K[:], consts).then_inc(const_in, 16)
            for c in range(NCH + 1):
                if c >= 2:
                    sp.wait_ge(w_split, c - 1)
                sp.dma_start(WR[:, c % 2], wsig[:, c]).then_inc([wsig_in0, wsig_in1][c % 2], 16)
                if c == 1:
                    sp.dma_start(tokb[:], tok_b).then_inc(small_in, 16)
                    sp.dma_start(qkvb[:], qkv_b).then_inc(small_in, 16)
                    sp.dma_start(PV[:], vecs).then_inc(small_in, 16)
                    sp.dma_start(wqkv_s[:], wqkv).then_inc(small_in, 16)

            for to, src in ((WP, wpos), (GW, gate_w), (IDS, token_ids), (WV, wout_v), (WO, wout), (SR1, sw1), (SR2, sw2)):
                sp.dma_start(to[:], src).then_inc(early_in, 16)
            sp.wait_ge(nobody_set, 2)
            sp.dma_start(routed.rearrange("(t p) c -> p t c", p=128), nobody[:].unsqueeze(1).broadcast_to([128, SLOTS, ROW])).then_inc(routed_set, 16)

            def step(k, u):
                if on(k - 2, 0, NT):
                    t = k - 2
                    sp.wait_ge(qs_ready, t + 1)
                    sp.dma_start(q_raw[bass.ds(t * TOK, TOK), :], QS[:, u, 0:F]).then_inc(qs_stored[u], 16)
                    sp.dma_start(k_raw[bass.ds(t * TOK, TOK), :], QS[:, u, F:F + DK]).then_inc(qs_stored[u], 16)
                    sp.dma_start(v_raw[bass.ds(t * TOK, TOK), :], QS[:, u, F + DK:QKV]).then_inc(qs_stored[u], 16)
                if on(k - 3, 0, NT):
                    load_q(k - 3, k)

            def load_q(t, k):
                if isinstance(t, int):
                    sp.wait_ge(qs_stored[t % 2], 48 * (t // 2 + 1))
                else:
                    sp.wait_ge(*k_of[0])
                src = q_raw.rearrange("(b s) f -> b (s f)", b=NB)[bass.ds(t * 2, 2), :].rearrange("b (p s) -> p b s", p=128)
                sp.dma_start(QR[:, bass.ds(t * 2, 2), 0:S], src).then_inc(q_loaded, 16)

            k_of = [None]
            for k in range(-1, 4):
                step(k, k % 2)
            with sp.Fori(2, 15) as j:
                k_of[0] = (qs_stored[1], (j - 1) * 48)
                step(j * 2, 0)
                k_of[0] = (qs_stored[0], j * 48)
                step(j * 2 + 1, 1)
            for k in range(30, NT + 2):
                step(k, k % 2)
            load_q(NT - 1, None)

        @block.gpsimd
        def _(pool):
            pool.memset(A2X[:, :, C2 + C:TAIL], 1.0).then_inc(consts_set, 1)
            pool.memset(eps[:], EPS).then_inc(consts_set, 1)
            pool.memset(nobody[:], 0.0).then_inc(nobody_set, 1)
            pool.wait_ge(nobody_set, 1)
            pool.memset(nobody[:, F:F + 1].bitcast(i32), NOBODY).then_inc(nobody_set, 1)
            pool.memset(QR[:, :, S:SP], 0.0).then_inc(consts_set, 1)
            pool.wait_ge(a2_ready, 2 * 4)

            def step(k, u):
                t = k + 1
                if on(t, 0, NT):
                    wait_from_one(pool, at_done, t - 1)
                    pool.tensor_tensor(
                        TOP[:, 1 - u].rearrange("p (a b) -> p a b", b=C),
                        A2T[:, bass.ds(t, 1)].rearrange("p t a b -> p (t a b)").unsqueeze(2).broadcast_to([TOK, C2, C]),
                        Vhalf[:, bass.ds(t, 1)].broadcast_to([TOK, C2, C]), ALU.mult).then_inc(top_ready, 1)
            run_steps(pool, step)

        @block.scalar
        def _(act):
            for c in range(NCH + 1):
                act.wait_ge([wsig_in0, wsig_in1][c % 2], 16 * (c // 2 + 1))
                act.activation(Wh[:, c], WR[:, c % 2], ACT.Copy).then_inc(w_hi, 1)
            act.wait_ge(a2_ready, 2 * 4)
            act.wait_ge(a2x_ready, 1)
            act.wait_ge(consts_set, 3)

            def step(k, u):
                if on(k + 1, 0, NT):
                    wait_from_one(act, at_done, k)
                    act.activation(AXs[:, 1 - u], A2X[:, bass.ds(k + 1, 1)].rearrange("p t c -> p (t c)"), ACT.Copy).then_inc(ax_ready, 1)
                if on(k - 1, 0, NT):
                    act.wait_ge(mv_ready, k)
                    act.activation(SD[:, 1 - u, 0:1], MV[:, 1 - u, 1:2], ACT.Sqrt, bias=eps[0:TOK, :]).then_inc(sd_ready, 1)
                if on(k + 1, 0, NT):
                    act.wait_ge(at_done, k + 2)
                    wait_from_one(act, u1_done, k)
                    act.activation(Ah[:, 1 - u, 0:NCH], psA, ACT.Copy).then_inc(ah_ready, 1)
                    act.activation(Ah[0:TAIL, 1 - u, NCH], psB, ACT.Copy).then_inc(ah_ready, 1)
                if on(k - 1, 0, NT):
                    act.wait_ge(xt_done, k)
                    wait_from_one(act, qkv_done, k - 2)
                    act.activation(XT[:, 1 - u], psX, ACT.Copy).then_inc(xt_ready, 1)
            run_steps(act, step)

        @block.vector
        def _(dve):
            L = Links(dve, dve_link)
            dve.wait_ge(path_in, 48)
            L.made(dve.tensor_tensor(V[:], pnext[:], pnow[:], ALU.subtract))
            L.link(dve.tensor_tensor(S1[:], pnow[:], pfirst[:], ALU.subtract))
            L.made(dve.tensor_scalar(Vhalf[:], V[:], 0.5, None, ALU.mult))
            L.made(dve.tensor_scalar(Vthird[:], V[:], 1.0 / 3.0, None, ALU.mult))
            L.made(dve.scalar_tensor_tensor(C2h[:], V[:], 0.5, S1[:], ALU.mult, ALU.add))
            L.made(dve.scalar_tensor_tensor(C3h[:], V[:], 1.0 / 3.0, S1[:], ALU.mult, ALU.add))
            L.link(dve.scalar_tensor_tensor(C4h[:], V[:], 0.25, S1[:], ALU.mult, ALU.add))

            def outer(o, a, b):
                return dve.tensor_tensor(o[:], a[:].unsqueeze(3).broadcast_to([TOK, NT, C, C]),
                                         b[:].unsqueeze(2).broadcast_to([TOK, NT, C, C]), ALU.mult)
            outer(E2, C2h, V).then_inc(e2_ready, 1)
            L.made(outer(E3, C3h, Vhalf))
            L.link(outer(A2T, C4h, Vthird))
            dve.tensor_copy(A2X[:, :, C2:C2 + C], C2h[:]).then_inc(a2x_ready, 1)
            for q in range(4):
                ts = slice(8 * q, 8 * q + 8)
                dve.wait_ge(s2_done, q + 1)
                s2 = PS[2 + q][0:TOK, :].rearrange("p (t c) -> p t c", t=8)
                dve.tensor_tensor(A2X[:, ts, 0:C2], s2, E3[:, ts].rearrange("p t a b -> p t (a b)"), ALU.add).then_inc(a2_ready, 1)
                a2 = A2T[:, ts].rearrange("p t a b -> p t (a b)")
                dve.tensor_tensor(a2, s2, a2, ALU.add).then_inc(a2_ready, 1)
            for c in range(NCH + 1):
                dve.wait_ge(w_hi, c + 1)
                dve.tensor_tensor(Wl[:, c], WR[:, c % 2], Wh[:, c].bitcast(f32), ALU.subtract).then_inc(w_split, 1)
            dve.wait_ge(a2_ready, 8)
            dve.wait_ge(small_in, 64)

            def combine(u, h, first, last):
                for d in range(4):
                    sc = Vt[:, u, 4 * h + d:4 * h + d + 1]
                    if first and d == 0:
                        ins = dve.tensor_scalar(Z[:, u], psU[u][h][:, d], sc, None, ALU.mult)
                    else:
                        ins = dve.scalar_tensor_tensor(Z[:, u], psU[u][h][:, d], sc, Z[:, u], ALU.mult, ALU.add)
                    if d == 3:
                        ins.then_inc(last, 1)
                    else:
                        L.link(ins)

            def step(k, u):
                w = 1 - u
                if on(k + 1, 0, NT):
                    t = k + 1
                    wait_from_one(dve, at_done, k)
                    dve.tensor_tensor(INC[:, w].rearrange("p (a b) -> p a b", b=C),
                                      A2X[:, bass.ds(t, 1), 0:C2].rearrange("p t c -> p (t c)").unsqueeze(2).broadcast_to([TOK, C2, C]),
                                      V[:, bass.ds(t, 1)].broadcast_to([TOK, C2, C]), ALU.mult).then_inc(inc_ready, 1)
                if on(k - 1, 0, NT):
                    dve.wait_ge(u1_done, k)
                    dve.wait_ge(c0_done, k)
                    combine(w, 1, False, z_ready)
                if on(k - 2, 0, NT):
                    t = k - 2
                    dve.wait_ge(qkv_done, k - 1)
                    if isinstance(k, int):
                        if t >= 2:
                            dve.wait_ge(qs_stored[u], 48 * (t // 2))
                    else:
                        dve.wait_ge(qs_stored[u], stored[0])
                    dve.tensor_tensor(QS[:, u], psQKV, qkvb[:], ALU.add).then_inc(qs_ready, 1)
                    L.made(dve.bn_stats(stQ[:, bass.ds(t, 1)].rearrange("p t c -> p (t c)"), psQT))
                    dve.bn_stats(stV[:, bass.ds(t, 1)].rearrange("p t c -> p (t c)"), psVT).then_inc(stats_done, 1)
                if on(k - 1, 0, NT):
                    t = k - 1
                    dve.wait_ge(h_done, k)
                    ht = H[:, bass.ds(t, 1)].rearrange("p t c -> p (t c)")
                    dve.tensor_tensor(ht, psH, tokb[:], ALU.add).then_inc(h_ready, 1)
                    dve.wait_ge(h_ready, k)
                    dve.memset(carrier[:], 0.0)
                    L.link(dve.bn_stats(ST[:, w], ht))
                    dve.memset(carrier[:], 0.0)
                    dve.bn_aggr(MV[:, w], ST[:, w]).then_inc(mv_ready, 1)
                if on(k, 0, NT):
                    L.link(dve.tensor_copy(Vt[:, u], V[:, bass.ds(k, 1)].rearrange("p t c -> p (t c)")))
                    dve.wait_ge(u0_done, k + 1)
                    combine(u, 0, True, c0_done)
                if on(k - 1, 0, NT):
                    dve.wait_ge(sd_ready, k)
                    L.link(dve.reciprocal(SD[:, w, 1:2], SD[:, w, 0:1]))
                    wait_from_one(dve, xt_done, k - 2)
                    dve.tensor_scalar(XN[:, w], ht, MV[:, w, 0:1], SD[:, w, 1:2], ALU.subtract, ALU.mult).then_inc(xn_ready, 1)
                if on(k + 1, 0, NT):
                    dve.wait_ge(ah_ready, 2 * (k + 2))
                    L.made(dve.tensor_tensor(Al[:, w, 0:NCH], psA, Ah[:, w, 0:NCH].bitcast(f32), ALU.subtract))
                    dve.tensor_tensor(Al[0:TAIL, w, NCH], psB, Ah[0:TAIL, w, NCH].bitcast(f32), ALU.subtract).then_inc(al_ready, 1)

            stored = [None]
            for k in range(-1, 4):
                step(k, k % 2)
            with dve.Fori(2, 15) as j:
                L.loop(2, j, 22)
                stored[0] = (j - 1) * 48
                step(j * 2, 0)
                step(j * 2 + 1, 1)
            L.end(13)
            for k in range(30, NT + 2):
                step(k, k % 2)

        @block.tensor
        def _(pe):
            pe.wait_ge(const_in, 16)
            pe.wait_ge(e2_ready, 1)
            for q in range(4):
                pe.matmul(PS[2 + q][0:TOK, :], before, E2[:, 8 * q:8 * q + 8].rearrange("p t a b -> p (t a b)"),
                          start=True, stop=True).then_inc(s2_done, 1)
            pe.wait_ge(a2_ready, 8)

            def half(k, u, h, done):
                for n, (a, w) in enumerate(((Ah, Wh), (Ah, Wl), (Al, Wh))):
                    if n == 2:
                        pe.wait_ge(al_ready, k + 1)
                    for c in range(NCH + 1):
                        rows = 128 if c < NCH else TAIL
                        ins = pe.matmul(psU[u][h].rearrange("p d o -> p (d o)"), a[0:rows, u, c], w[0:rows, c, h],
                                        start=(n == 0 and c == 0), stop=(n == 2 and c == NCH))
                ins.then_inc(done, 1)

            def step(k, u):
                w = 1 - u
                if on(k, 0, NT):
                    if isinstance(k, int) and k == 0:
                        pe.wait_ge(w_split, NCH + 1)
                    pe.wait_ge(ah_ready, 2 * (k + 1))
                    wait_from_one(pe, c0_done, k - 1)
                    half(k, u, 0, u0_done)
                if on(k - 2, 0, NT):
                    if isinstance(k, int) and k == 2:
                        pe.wait_ge(small_in, 64)
                    pe.wait_ge(xt_ready, k - 1)
                    wait_from_one(pe, stats_done, k - 2)
                    pe.matmul(psQKV, XT[:, u], wqkv_s[:], start=True, stop=True)
                    pe.matmul(psQT, wqkv_s[:, 0:F], XT[:, u], start=True, stop=True)
                    pe.matmul(psVT, wqkv_s[:, F + DK:QKV], XT[:, u], start=True, stop=True).then_inc(qkv_done, 1)
                if on(k - 1, 0, NT):
                    pe.wait_ge(z_ready, k)
                    wait_from_one(pe, h_ready, k - 1)
                    pe.matmul(psH, upto_now, Z[:, w], start=True, stop=True).then_inc(h_done, 1)
                if on(k + 1, 0, NT):
                    pe.wait_ge(inc_ready, k + 2)
                    pe.wait_ge(top_ready, k + 2)
                    pe.wait_ge(ax_ready, k + 2)
                    wait_from_one(pe, al_ready, k + 1)
                    for c in range(NCH):
                        cs = slice(128 * c, 128 * c + 128)
                        pe.matmul(psA[:, c], INC[:, w, cs], before, start=True, stop=False)
                        pe.matmul(psA[:, c], TOP[:, w, cs], ident_t, start=False, stop=True)
                    pe.transpose(psB, AXs[:, w], ident_t).then_inc(at_done, 1)
                if on(k, 0, NT):
                    wait_from_one(pe, z_ready, k - 1)
                    half(k, u, 1, u1_done)
                if on(k - 1, 0, NT):
                    pe.wait_ge(xn_ready, k)
                    wait_from_one(pe, stats_done, k - 1)
                    pe.transpose(psX, XN[:, w], ident_t).then_inc(xt_done, 1)
            run_steps(pe, step)


def attention(nc, m):
    K, ident, ident_t, H, PV, eps, carrier, LG, X2h, X2l = (
        m[n] for n in "K ident ident_t H PV eps carrier LG X2h X2l".split())
    stQ, stV, PS, QR, k_raw, v_raw, v_pad, pat_q, x_rows = (
        m[n] for n in "stQ stV PS QR k_raw v_raw v_pad pat_q x_rows".split())
    WP, GW, IDS, WV, WO, SR1, SR2, early_in, routed_set, q_loaded = (m[n] for n in "WP GW IDS WV WO SR1 SR2 early_in routed_set q_loaded".split())
    S1h, S1l, S2 = (m[n] for n in "S1h S1l S2".split())
    with ExitStack() as ctx:
        def sb(name, shape, dt=f32):
            return ctx.enter_context(nc.sbuf_tensor(name, shape, dt))

        def sem(name):
            return ctx.enter_context(nc.semaphore(name))

        G8 = NB // 8
        KR, KS = (sb(n, [128, G8, S]) for n in ("KR", "KS"))
        VR, VN = (sb(n, [2 * NB, S, DK]) for n in ("VR", "VN"))
        VP = sb("VP", [2 * NB, VB], f32r)
        by_key = "b s k -> b (s k)"
        kmax, ksum, krec = (sb(n, [128, G8]) for n in ("kmax", "ksum", "krec"))
        mvq, mvv = sb("mvq", [128, 2]), sb("mvv", [DK, 2])
        BNP, BNR = sb("BNP", [128, 4]), sb("BNR", [2, 128])
        bnt = sb("bnt", [128, 4])
        PQ = sb("PQ", [128, 2, S])
        KT, VT = sb("KT", [S, NB, DK]), sb("VT", [S, NB, DK])
        KH = sb("KH", [S, 2, GB, NH, DK])
        WPh, WPm, W36 = sb("WPh", [36, 128], f32r), sb("WPm", [36, 128]), sb("W36", [36, 128], f32r)
        RUN = (GB - 1) * VB + DK * SP
        IM = sb("IM", [36, 2, RUN], f32r)
        QN = sb("QN", [128, 2, GB, SP])
        P = sb("P", [128, 2, GB, DK, SP])
        LC = sb("LC", [128, 2, GB, NH, DK])
        YC = sb("YC", [128, 2, GB * SP])
        OTs = sb("OTs", [128, 2, GB, S])
        H1 = sb("H1", [TOK, 2, 2, F])
        ST, MV, SD = sb("ST2", [TOK, 2, 2, 6]), sb("MV2", [TOK, 2, 2, 2]), sb("SD2", [TOK, 2, 2, 2])
        XR = sb("XR", [TOK, 2, 2, ROW])
        XG = sb("XTg", [128, 2, 2 * TOK])

        k_in, v_in, vp_set, bv_done = sem("k_in"), sem("v_in"), sem("vp_set"), sem("bv_done")
        bn_ready, sdv_ready, bnp_ready, bnt_done, bnr_ready = sem("bn_ready"), sem("sdv_ready"), sem("bnp_ready"), sem("bnt_done"), sem("bnr_ready")
        pat_stored, pat_in, w36_ready = sem("pat_stored"), sem("pat_in"), sem("w36_ready")
        ks_ready, exp_done, k_ready, v_ready, vn_ready = sem("ks_ready"), sem("exp_done"), sem("k_ready"), sem("v_ready"), sem("vn_ready")
        v_stored, kt_done, vt_done, kvt_ready, lam_c_done, kh_ready = (
            sem("v_stored"), sem("kt_done"), sem("vt_done"), sem("kvt_ready"), sem("lam_c_done"), sem("kh_ready"))
        s_hi, s_lo = sem("s_hi"), sem("s_lo")
        im_in = [sem("im_in0"), sem("im_in1")]
        conv_done, p_ready, qn_ready, lc_ready = sem("conv_done"), sem("p_ready"), sem("qn_ready"), sem("lc_ready")
        yc_done, yc_ready, ot_done, ot_ready = sem("yc_done"), sem("yc_ready"), sem("ot_done"), sem("ot_ready")
        ht_done, h1_ready, h1_kept, mv_ready, sd_ready, xn_ready = (
            sem("ht_done"), sem("h1_ready"), sem("h1_kept"), sem("mv2_ready"), sem("sd2_ready"), sem("xn2_ready"))
        ids_ready, xr_stored = sem("ids_ready"), [sem("xr_stored0"), sem("xr_stored1")]
        xt_done, xt_ready, xlo_ready, gate_done, lg_ready = sem("xt2_done"), sem("xt2_ready"), sem("xlo_ready"), sem("gate_done"), sem("lg_ready")
        dve_link, pool_link = sem("dve_link2"), sem("pool_link2")

        psC = [[PS[2 * u + h][:, :].rearrange("p (v s) -> p v s", v=8) for h in range(2)] for u in range(2)]
        psO, psY = PS[4][:, 0:GB * SP], PS[5][:, 0:GB * SP]
        psH = PS[6][0:TOK, 0:2 * F].rearrange("p (t f) -> p t f", t=2)
        psL = PS[6][:, 256:256 + GB * DK].rearrange("p (b v) -> p b v", b=GB)
        psV = PS[7][0:2 * NB, 0:2 * DK].rearrange("p (c k) -> p c k", c=2)
        psX = PS[7][:, 0:2 * TOK]
        psG = PS[7][0:TOK, 256:256 + 2 * E].rearrange("p (t e) -> p t e", t=2)

        block = ctx.enter_context(nc.Block())

        @block.sync
        def _(sp):
            sp.dma_start(KR[:], k_raw.rearrange("n k -> (n k)").rearrange("(g p s) -> p g s", g=G8, p=128)).then_inc(k_in, 16)
            for c in range(2):
                sp.dma_start(VR[NB * c:NB * c + NB], v_raw.rearrange("(b s) k -> b s k", b=NB)).then_inc(v_in, 16)
            sp.wait_ge(bnr_ready, 1)
            sp.dma_start(pat_q, BNR[0:2, :].unsqueeze(1).broadcast_to([2, S, F])).then_inc(pat_stored, 16)
            sp.wait_ge(pat_stored, 16)
            sp.dma_start(PQ[:], bass.AP(pat_q.tensor, 0, [[S, 128], [S * F, 2], [1, S]])).then_inc(pat_in, 16)
            sp.wait_ge(v_ready, 2)
            sp.dma_start(v_pad.rearrange("c b n -> (c b) n"), VP[:].bitcast(f32)).then_inc(v_stored, 16)
            sp.wait_ge(v_stored, 16)

            def load_im(t, u):
                for c in range(4):
                    src = v_pad[c % 2, bass.ds(t * GB, GB), :]
                    sp.dma_start(IM[9 * c:9 * c + 9, u].bitcast(f32),
                                 bass.AP(src.tensor, src.offset, [[SP, 3], [1, 3], [1, RUN]])).then_inc(im_in[u], 16)

            def step(g, u):
                if on(g + 1, 0, NG):
                    wait_from_one(sp, conv_done, g * GB)
                    load_im(g + 1, 1 - u)
                if on(g - 2, 0, NG):
                    sp.wait_ge(xn_ready, g - 1)
                    sp.wait_ge(ids_ready, g - 1)
                    sp.dma_start(x_rows[bass.ds((g - 2) * 2 * TOK, 2 * TOK), :].rearrange("(t p) c -> p t c", p=TOK),
                                 XR[:, u]).then_inc(xr_stored[u], 16)
            for g in range(-1, 4):
                step(g, g % 2)
            with sp.Fori(2, 7) as j:
                step(j * 2, 0)
                step(j * 2 + 1, 1)
            for g in range(14, NG + 3):
                step(g, g % 2)
            for u in range(2):
                sp.wait_ge(xr_stored[u], 16 * NG // 2)
            sp.wait_ge(routed_set, 16)

        @block.gpsimd
        def _(pool):
            L = Links(pool, pool_link)
            pool.memset(VP[:].bitcast(f32), 0.0).then_inc(vp_set, 1)
            L.made(pool.memset(QN[:, :, :, S:SP], 0.0))
            L.link(pool.memset(XR[:, :, :, F:ROW], 0.0))
            pool.wait_ge(early_in, 16 * 7)
            pool.wait_ge(q_loaded, 16 * NT)
            pool.wait_ge(pat_in, 16)

            def step(g, u):
                w = 1 - u
                if on(g + 1, 0, NG):
                    wait_from_one(pool, p_ready, g * GB)
                    wait_from_one(pool, yc_done, g)
                    L.link(pool.tensor_tensor(QN[:, w, :, 0:S], QR[:, bass.ds((g + 1) * GB, GB), 0:S],
                                              PQ[:, 0:1].broadcast_to([128, GB, S]), ALU.mult))
                    pool.tensor_tensor(QN[:, w, :, 0:S], QN[:, w, :, 0:S],
                                       PQ[:, 1:2].broadcast_to([128, GB, S]), ALU.add).then_inc(qn_ready, 1)
                if on(g - 2, 0, NG):
                    if isinstance(g, int):
                        if g >= 4:
                            pool.wait_ge(xr_stored[u], 16 * ((g - 2) // 2))
                    else:
                        pool.wait_ge(xr_stored[u], freed[0])
                    pool.tensor_copy(XR[:, u, :, F].bitcast(i32), IDS[:, bass.ds((g - 2) * 2, 2)]).then_inc(ids_ready, 1)
                if on(g - 3, 0, NG):
                    pool.wait_ge(xt_ready, 2 * (g - 2))
                    ts = bass.ds((g - 3) * 2 * TOK, 2 * TOK)
                    pool.tensor_tensor(X2l[:, ts], XG[:, w], X2h[:, ts].bitcast(f32), ALU.subtract).then_inc(xlo_ready, 1)

            freed = [None]
            for g in range(-1, 4):
                step(g, g % 2)
            with pool.Fori(2, 7) as j:
                L.loop(2, j, 2)
                freed[0] = (j - 1) * 16
                step(j * 2, 0)
                step(j * 2 + 1, 1)
            L.end(5)
            for g in range(14, NG + 3):
                step(g, g % 2)

        @block.scalar
        def _(act):
            act.wait_ge(bn_ready, 2)
            act.activation(bnt[:, 0:1], mvq[:, 1:2], ACT.Sqrt, bias=eps[:]).then_inc(sdv_ready, 1)
            act.activation(bnt[0:DK, 1:2], mvv[:, 1:2], ACT.Sqrt, bias=eps[0:DK]).then_inc(sdv_ready, 1)
            act.wait_ge(bnt_done, 1)
            act.activation(BNR[:], PS[6][0:2, 0:128], ACT.Copy).then_inc(bnr_ready, 1)
            act.wait_ge(ks_ready, 1)
            act.activation(KS[:], KS[:], ACT.Exp).then_inc(exp_done, 1)
            act.wait_ge(kt_done, 1)
            for h in range(2):
                act.activation(KT[:, 32 * h:32 * h + 32].rearrange("p b k -> p (b k)"), PS[h][0:S, :], ACT.Copy).then_inc(kvt_ready, 1)
            act.wait_ge(vt_done, 1)
            for h in range(2):
                act.activation(VT[:, :, 8 * h:8 * h + 8].rearrange("p b k -> p k b"), PS[2 + h][0:S, :].rearrange("p (k b) -> p k b", b=NB),
                               ACT.Copy).then_inc(kvt_ready, 1)
            act.wait_ge(kvt_ready, 4)

            def step(g, u):
                w = 1 - u
                if on(g + 1, 0, NG):
                    wait_from_one(act, lam_c_done, g)
                    act.activation(KH[:, w], KT[:, bass.ds((g + 1) * GB, GB)].unsqueeze(2).broadcast_to([S, GB, NH, DK]),
                                   ACT.Copy).then_inc(kh_ready, 1)
                if on(g - 2, 0, NG):
                    act.wait_ge(mv_ready, 2 * (g - 1))
                    act.activation(SD[:, u, :, 0], MV[:, u, :, 1], ACT.Sqrt, bias=eps[0:TOK, :]).then_inc(sd_ready, 1)
                    act.activation(H[:, bass.ds((g - 2) * 2, 2)], H1[:, u], ACT.Copy).then_inc(h1_kept, 1)
                if on(g - 1, 0, NG):
                    act.wait_ge(ot_done, g)
                    wait_from_one(act, ht_done, g - 2)
                    act.activation(OTs[:, w], psO.rearrange("p (b s) -> p b s", b=GB)[:, :, 0:S], ACT.Identity,
                                   bias=PV[:, P_BOUT:P_BOUT + 1]).then_inc(ot_ready, 1)
                if on(g, 0, NG):
                    act.wait_ge(yc_done, g + 1)
                    wait_from_one(act, ot_done, g - 1)
                    act.activation(YC[:, u], psY, ACT.Copy).then_inc(yc_ready, 1)
                if on(g - 2, 0, NG):
                    act.wait_ge(xt_done, g - 1)
                    wait_from_one(act, xlo_ready, g - 3)
                    wait_from_one(act, gate_done, g - 3)
                    act.activation(XG[:, u], psX, ACT.Copy).then_inc(xt_ready, 1)
                    act.activation(X2h[:, bass.ds((g - 2) * 2 * TOK, 2 * TOK)], psX, ACT.Copy).then_inc(xt_ready, 1)
            for g in range(-1, 4):
                step(g, g % 2)
                if g == 0:
                    act.activation(S1h[:], SR1[:], ACT.Copy).then_inc(s_hi, 1)
                    act.activation(S2[:, :, 0], SR2[:], ACT.Copy).then_inc(s_hi, 1)
            with act.Fori(2, 7) as j:
                step(j * 2, 0)
                step(j * 2 + 1, 1)
            for g in range(14, NG + 3):
                step(g, g % 2)

        @block.vector
        def _(dve):
            L = Links(dve, dve_link)
            dve.bn_aggr(mvq[:], stQ[:].rearrange("p t c -> p (t c)")).then_inc(bn_ready, 1)
            dve.bn_aggr(mvv[:], stV[:].rearrange("p t c -> p (t c)")).then_inc(bn_ready, 1)
            L.link(dve.memset(BNP[:], 0.0))
            dve.wait_ge(bn_ready, 2)
            L.made(dve.tensor_tensor(bnt[:, 2:3], mvq[:, 0:1], PV[:, P_BQ:P_BQ + 1], ALU.add))
            L.made(dve.tensor_tensor(bnt[0:DK, 3:4], mvv[:, 0:1], PV[0:DK, P_BV:P_BV + 1], ALU.add))
            dve.wait_ge(sdv_ready, 2)
            L.made(dve.reciprocal(bnt[:, 0:1], bnt[:, 0:1]))
            L.link(dve.reciprocal(bnt[0:DK, 1:2], bnt[0:DK, 1:2]))
            L.made(dve.tensor_tensor(BNP[:, 0:1], bnt[:, 0:1], PV[:, P_GQ:P_GQ + 1], ALU.mult))
            L.link(dve.tensor_tensor(BNP[0:DK, 2:3], bnt[0:DK, 1:2], PV[0:DK, P_GV:P_GV + 1], ALU.mult))
            L.made(dve.tensor_tensor(bnt[:, 2:3], bnt[:, 2:3], BNP[:, 0:1], ALU.mult))
            L.link(dve.tensor_tensor(bnt[0:DK, 3:4], bnt[0:DK, 3:4], BNP[0:DK, 2:3], ALU.mult))
            L.made(dve.tensor_tensor(BNP[:, 1:2], PV[:, P_BETAQ:P_BETAQ + 1], bnt[:, 2:3], ALU.subtract))
            L.link(dve.tensor_tensor(BNP[0:DK, 3:4], PV[0:DK, P_BETAV:P_BETAV + 1], bnt[0:DK, 3:4], ALU.subtract))
            L.link(dve.tensor_copy(bnt[:, 0:4], BNP[:]))
            dve.sem_inc(bnp_ready, 1)
            dve.wait_ge(k_in, 16)
            L.link(dve.tensor_reduce(kmax[:], KR[:], AX.X, ALU.max))
            dve.tensor_tensor(KS[:], KR[:], kmax[:].unsqueeze(2).broadcast_to([128, G8, S]), ALU.subtract).then_inc(ks_ready, 1)
            dve.wait_ge(bv_done, 1)
            dve.wait_ge(v_in, 32)
            L.link(dve.tensor_tensor(VN[:], VR[:], psV[:, 0:1].broadcast_to([2 * NB, S, DK]), ALU.mult))
            dve.tensor_tensor(VN[:], VN[:], psV[:, 1:2].broadcast_to([2 * NB, S, DK]), ALU.add).then_inc(vn_ready, 1)
            dve.wait_ge(vn_ready, 1)
            dve.wait_ge(vp_set, 1)
            values = VP[:, SP:SP + DK * SP].rearrange("b (k s) -> b k s", k=DK)[:, :, 1:SP]
            by_step = VN[:].rearrange(by_key).rearrange("b (k s) -> b k s", k=DK)
            dve.tensor_copy(values, by_step).then_inc(v_ready, 1)
            dve.wait_ge(v_ready, 1)
            dve.tensor_tensor(values[NB:2 * NB], by_step[NB:2 * NB], values[NB:2 * NB].bitcast(f32), ALU.subtract).then_inc(v_ready, 1)
            dve.wait_ge(early_in, 16 * 7)
            L.link(dve.tensor_copy(WPh[:], WP[:]))
            L.link(dve.tensor_scalar(WPm[:], WP[:], K[0:36, K_CV + 1:K_CV + 2], None, ALU.mult))
            dve.scalar_tensor_tensor(W36[:], WPh[:].bitcast(f32), K[0:36, K_CV:K_CV + 1], WPm[:], ALU.mult, ALU.add).then_inc(w36_ready, 1)
            dve.wait_ge(exp_done, 1)
            L.link(dve.tensor_reduce(ksum[:], KS[:], AX.X, ALU.add))
            L.link(dve.reciprocal(krec[:], ksum[:]))
            dve.tensor_tensor(KS[:], KS[:], krec[:].unsqueeze(2).broadcast_to([128, G8, S]), ALU.mult).then_inc(k_ready, 1)
            def step(g, u):
                w = 1 - u

                def products(b):
                    n = g * GB + b
                    dve.wait_ge(conv_done, n + 1)
                    for h in range(2):
                        ins = dve.scalar_tensor_tensor(P[:, u, b, 8 * h:8 * h + 8], psC[b % 2][h], 0.0,
                                                       QN[:, u, b:b + 1].broadcast_to([128, 8, SP]), ALU.max, ALU.mult)
                    ins.then_inc(p_ready, 1)
                if on(g, 0, NG):
                    dve.wait_ge(qn_ready, g + 1)
                    wait_from_one(dve, ot_done, g - 1)
                    products(0)
                    products(1)
                if on(g - 2, 0, NG):
                    dve.wait_ge(ht_done, g - 1)
                    wait_from_one(dve, h1_kept, g - 3)
                    dve.tensor_tensor(H1[:, u], psH, H[:, bass.ds((g - 2) * 2, 2)], ALU.add).then_inc(h1_ready, 1)
                    dve.wait_ge(h1_ready, g - 1)
                    for t in range(2):
                        L.made(dve.bn_stats(ST[:, u, t], H1[:, u, t]))
                    L.wait()
                    dve.memset(carrier[:], 0.0)
                    for t in range(2):
                        dve.bn_aggr(MV[:, u, t], ST[:, u, t]).then_inc(mv_ready, 1)
                if on(g, 0, NG):
                    products(2)
                    products(3)
                if on(g - 2, 0, NG):
                    dve.wait_ge(sd_ready, g - 1)
                    L.link(dve.reciprocal(SD[:, u, :, 1], SD[:, u, :, 0]))
                    if isinstance(g, int):
                        if g >= 4:
                            dve.wait_ge(xr_stored[u], 16 * ((g - 2) // 2))
                    else:
                        dve.wait_ge(xr_stored[u], freed[0])
                    wait_from_one(dve, xt_done, g - 3)
                    for t in range(2):
                        ins = dve.tensor_scalar(XR[:, u, t, 0:F], H1[:, u, t], MV[:, u, t, 0:1], SD[:, u, t, 1:2], ALU.subtract, ALU.mult)
                        if t == 0:
                            L.made(ins)
                    ins.then_inc(xn_ready, 1)
                if on(g + 1, 0, NG):
                    dve.wait_ge(lam_c_done, g + 2)
                    wait_from_one(dve, yc_done, g)
                    dve.tensor_tensor(LC[:, w], psL.unsqueeze(2).broadcast_to([128, GB, NH, DK]),
                                      K[:, K_MB:K_MB + NH].unsqueeze(1).unsqueeze(3).broadcast_to([128, GB, NH, DK]),
                                      ALU.mult).then_inc(lc_ready, 1)
                if on(g - 3, 0, NG):
                    dve.wait_ge(gate_done, g - 2)
                    dve.tensor_copy(LG[:, bass.ds((g - 3) * 2, 2)], psG).then_inc(lg_ready, 1)

            freed = [None]
            for g in range(-1, 4):
                step(g, g % 2)
                if g == 1:
                    dve.wait_ge(s_hi, 2)
                    dve.tensor_tensor(S1l[:], SR1[:], S1h[:].bitcast(f32), ALU.subtract).then_inc(s_lo, 1)
                    dve.tensor_tensor(S2[:, :, 1], SR2[:], S2[:, :, 0].bitcast(f32), ALU.subtract).then_inc(s_lo, 1)
            with dve.Fori(2, 7) as j:
                L.loop(2, j, 8)
                freed[0] = (j - 1) * 16
                step(j * 2, 0)
                step(j * 2 + 1, 1)
            L.end(5)
            for g in range(14, NG + 3):
                step(g, g % 2)

        @block.tensor
        def _(pe):
            pe.wait_ge(bnp_ready, 1)
            for c in range(2):
                ins = pe.matmul(psV[:, c], bnt[0:DK, 2 + c:3 + c].broadcast_to([DK, 2 * NB]), K[0:DK, K_ID:K_ID + DK], start=True, stop=True)
            ins.then_inc(bv_done, 1)
            pe.transpose(PS[6][0:2, 0:128], bnt[:, 0:2], ident).then_inc(bnt_done, 1)
            pe.wait_ge(vn_ready, 1)
            by_step = VN[0:NB].rearrange(by_key).rearrange("b (k s) -> b k s", k=DK)
            for k in range(DK):
                ins = pe.transpose(PS[2 + k // 8][0:S, NB * (k % 8):NB * (k % 8) + NB], by_step[:, k], K[0:NB, K_ID:K_ID + NB])
            ins.then_inc(vt_done, 1)
            pe.wait_ge(k_ready, 1)
            for q in range(G8):
                ins = pe.transpose(PS[q // 4][0:S, 128 * (q % 4):128 * (q % 4) + 128], KS[:, q], ident)
            ins.then_inc(kt_done, 1)
            pe.wait_ge(kvt_ready, 4)
            pe.wait_ge(w36_ready, 1)
            pe.wait_ge(early_in, 16 * 7)

            def step(g, u):
                w = 1 - u

                def conv(b):
                    n = g * GB + b
                    wait_from_one(pe, p_ready, n - 1)
                    for h in range(2):
                        ins = pe.matmul(psC[b % 2][h].rearrange("p v s -> p (v s)"), W36[:], IM[:, u, b * VB + 512 * h:b * VB + 512 * h + 512], start=True, stop=True)
                    ins.then_inc(conv_done, 1)

                def project(v0, v1):
                    for v in range(v0, v1):
                        pe.matmul(psO.rearrange("p (b s) -> p b s", b=GB), WV[:, v], P[:, w, :, v], start=(v == 0), stop=False)
                if on(g, 0, NG):
                    if isinstance(g, int):
                        pe.wait_ge(im_in[u], 64 * (g // 2 + 1))
                    else:
                        pe.wait_ge(im_in[u], arrived[0])
                    conv(0)
                    conv(1)
                if on(g - 1, 0, NG):
                    pe.wait_ge(p_ready, g * GB)
                    wait_from_one(pe, ot_ready, g - 1)
                    project(0, 8)
                if on(g, 0, NG):
                    conv(2)
                    conv(3)
                if on(g - 3, 0, NG):
                    pe.wait_ge(xt_ready, 2 * (g - 2))
                    wait_from_one(pe, lg_ready, g - 3)
                    for t in range(2):
                        ins = pe.matmul(psG[:, t], XG[:, w, TOK * t:TOK * t + TOK], GW[:], start=True, stop=True)
                    ins.then_inc(gate_done, 1)
                if on(g + 1, 0, NG):
                    pe.wait_ge(kh_ready, g + 2)
                    wait_from_one(pe, h1_ready, g - 1)
                    for b in range(GB):
                        ins = pe.matmul(psL[:, b], KH[:, w, b].rearrange("p h k -> p (h k)"),
                                        VT[:, bass.ds((g + 1) * GB + b, 1)].rearrange("p b v -> p (b v)"), start=True, stop=True)
                    ins.then_inc(lam_c_done, 1)
                if on(g - 1, 0, NG):
                    project(8, DK)
                    pe.wait_ge(yc_ready, g)
                    pe.matmul(psO, WO[:], YC[:, w], start=False, stop=True).then_inc(ot_done, 1)
                if on(g, 0, NG):
                    pe.wait_ge(lc_ready, g + 1)
                    pe.wait_ge(qn_ready, g + 1)
                    wait_from_one(pe, yc_ready, g)
                    for b in range(GB):
                        ins = pe.matmul(psY[:, SP * b:SP * b + SP], LC[:, u, b].rearrange("p h v -> p (h v)"), QN[:, u, b], start=True, stop=True)
                    ins.then_inc(yc_done, 1)
                if on(g - 2, 0, NG):
                    pe.wait_ge(xn_ready, g - 1)
                    wait_from_one(pe, lg_ready, g - 2)
                    for t in range(2):
                        ins = pe.transpose(psX[:, TOK * t:TOK * t + TOK], XR[:, u, t, 0:F], ident_t)
                    ins.then_inc(xt_done, 1)
                if on(g - 1, 0, NG):
                    pe.wait_ge(ot_ready, g)
                    if on(g + 1, 0, NG):
                        pe.wait_ge(lc_ready, g + 2)
                    wait_from_one(pe, h1_ready, g - 1)
                    for t in range(2):
                        ins = pe.transpose(psH[:, t], OTs[:, w, 2 * t:2 * t + 2].rearrange("p b s -> p (b s)"), ident)
                    ins.then_inc(ht_done, 1)

            arrived = [None]
            for g in range(-1, 4):
                step(g, g % 2)
            with pe.Fori(2, 7) as j:
                arrived[0] = (j + 1) * 64
                step(j * 2, 0)
                step(j * 2 + 1, 1)
            for g in range(14, NG + 3):
                step(g, g % 2)


def ffn(nc, m):
    K, ident, ident_t, H, LG, X2h, X2l, PS = (m[n] for n in "K ident ident_t H LG X2h X2l PS".split())
    x_rows, routed, base, out_rows, w13, w2 = (m[n] for n in "x_rows routed base out_rows w13 w2".split())
    S1h, S1l, S2 = m["S1h"], m["S1l"], m["S2"]
    with ExitStack() as ctx:
        def sb(name, shape, dt=f32):
            return ctx.enter_context(nc.sbuf_tensor(name, shape, dt))

        def sem(name):
            return ctx.enter_context(nc.semaphore(name))

        CT = 2 * TOK
        NC = N // CT
        IC = I // 128
        of_slot, OF = sb("of_slot", [128, SLOTS]), sb("OF", [128, SLOTS], i32)
        W1h, W1l = (sb(n, [F, E, 2 * I], f32r) for n in ("W1h", "W1l"))
        W2 = sb("W2", [128, E, IC, 2, F], f32r)
        with ExitStack() as own:
            def sbo(name, shape, dt=f32):
                return own.enter_context(nc.sbuf_tensor(name, shape, dt))
            lmax, top = sbo("lmax", [TOK, NT]), sbo("top", [TOK, NT])
            OH, RK = sbo("OH", [TOK, E, NT]), sbo("RK", [TOK, E, NT])
            CNT, INCL, ones_s = sbo("CNT", [128, E, NT]), sbo("INCL", [128, E, NT]), sbo("ones_s", [128, E * NT])
            n_e, tiles_e, ends, starts, first = (sbo(n, [128, E]) for n in ("n_e", "tiles_e", "ends", "starts", "first"))
            n_i = sbo("n_int", [128, E], i32)
            posf, POS = sbo("posf", [TOK, NT]), sbo("POS", [TOK, NT], i32)
            WR1, WR2 = sbo("WR1", [F, 2 * I]), sbo("WR2", [128, IC, F])
            GF = sbo("GF", [128, 2, IC, CT])
            Gh, Gl = (sbo(n, [128, 2, IC, CT], f32r) for n in ("Gh", "Gl"))
            BS = sbo("BS", [TOK, 2, 2, F])
            RB = sbo("RB", [TOK, 3, 8, ROW])
            shared(nc, locals())
        XS = sb("XS", [128, 4, ROW])
        BG, TO = sb("BG", [128, 4, F]), sb("TO", [128, 4, 2], i32)
        Xh, Xl = (sb(n, [F, 2, 128], f32r) for n in ("Xh", "Xl"))
        SG, GX = sb("SG", [128, 2, I]), sb("GX", [128, 2, I])
        Gh, Gl = (sb(n, [128, 2, IC, 128], f32r) for n in ("GTh", "GTl"))
        OS = sb("OS", [128, 2, F])
        experts(nc, locals())


def shared(nc, m):
    K, ident, ident_t, H, LG, X2h, X2l, PS = (m[n] for n in "K ident ident_t H LG X2h X2l PS".split())
    x_rows, routed, base, w13, w2 = (m[n] for n in "x_rows routed base w13 w2".split())
    lmax, top, OH, RK, CNT, INCL, ones_s, n_e, n_i, tiles_e, ends, starts, first, posf, POS, of_slot, OF = (
        m[n] for n in "lmax top OH RK CNT INCL ones_s n_e n_i tiles_e ends starts first posf POS of_slot OF".split())
    S1h, S1l, S2, WR1, WR2, W1h, W1l, W2, GF, Gh, Gl, BS, RB = (
        m[n] for n in "S1h S1l S2 WR1 WR2 W1h W1l W2 GF Gh Gl BS RB".split())
    CT, NC, IC = m["CT"], m["NC"], m["IC"]
    with ExitStack() as ctx:
        def sem(name):
            return ctx.enter_context(nc.semaphore(name))

        w1_in, w2_in, w_hi, w1_split, w2_split = sem("w1_in"), sem("w2_in"), sem("we_hi"), sem("w1_split"), sem("w2_split")
        oh_ready, rank_done, pos_ready = sem("oh_ready"), sem("rank_done"), sem("pos_ready")
        rb_in, scattered = [sem(f"rb_in{n}") for n in range(4)], [sem(f"scattered{n}") for n in range(4)]
        g_done, gelu_ready, gh_ready, gl_ready = sem("g_done"), sem("gelu_ready"), sem("gh_ready"), sem("gl_ready")
        y_done, bs_ready, base_stored = sem("y_done"), sem("bs_ready"), [sem("base_stored0"), sem("base_stored1")]
        dve_link = sem("dve_link3")

        psG = [[PS[2 * u + h][:, 0:2 * CT].rearrange("p (i s) -> p i s", i=2) for h in range(2)] for u in range(2)]
        psY = [PS[4 + u][0:TOK, :].rearrange("p (t h f) -> p t h f", t=2, h=2) for u in range(2)]
        psR, psN = PS[6][0:TOK, 0:E * NT], PS[7][:, 0:E * NT]
        block = ctx.enter_context(nc.Block())

        @block.sync
        def _(sp):
            def weights(n, e):
                to, src, arrived = ((WR1, w13, w1_in), (WR2, w2, w2_in))[n]
                if n == 0:
                    sp.dma_start(to[:], src[:, bass.ds(e, 1)].rearrange("p e i -> p (e i)")).then_inc(arrived, 16)
                else:
                    sp.dma_start(to[:], src[:, bass.ds(e, 1)].rearrange("p e i f -> p (e i f)")).then_inc(arrived, 16)
            weights(0, 0)
            for q in range(3):
                sp.dma_start(RB[:, q], x_rows[8 * q * TOK:(8 * q + 8) * TOK, :].rearrange("(t p) c -> p t c", p=TOK)).then_inc(rb_in[q], 16)
                if q == 0:
                    weights(1, 0)

            def step(c, u):
                if u == 1 and on(c, 1, NC - 2):
                    e = c // 2 if isinstance(c, int) else expert[0]
                    sp.wait_ge(w1_split, e + 1)
                    weights(0, e + 1)
                if u == 0 and on(c, 2, NC):
                    e = c // 2 if isinstance(c, int) else expert[0]
                    sp.wait_ge(w2_split, e)
                    weights(1, e)
                if on(c - 2, 0, NC):
                    sp.wait_ge(bs_ready, c - 1)
                    sp.dma_start(base[bass.ds((c - 2) * CT, CT), :].rearrange("(t p) f -> p t f", p=TOK), BS[:, u]).then_inc(base_stored[u], 16)
            expert = [None]
            for c in range(0, 4):
                step(c, c % 2)
            with sp.Fori(2, 7) as j:
                expert[0] = j
                step(j * 2, 0)
                step(j * 2 + 1, 1)
            for c in range(NC - 2, NC + 2):
                step(c, c % 2)
            for u in range(2):
                sp.wait_ge(base_stored[u], 16 * NC // 2)

        @block.gpsimd
        def _(pool):
            pool.wait_ge(pos_ready, 1)
            for t in range(NT):
                q = t // 8
                if t % 8 == 0:
                    pool.wait_ge(rb_in[q], 16)
                pool.indirect_dma_start(routed, bass.IndirectOffsetOnAxis(POS[:, t:t + 1], 0), RB[:, q % 3, t % 8], None).then_inc(scattered[q], 16)
                if t == 15:
                    pool.wait_ge(scattered[0], 16 * 8)
                    pool.dma_start(RB[:, 0], x_rows[24 * TOK:32 * TOK, :].rearrange("(t p) c -> p t c", p=TOK)).then_inc(rb_in[3], 16)
            for n in range(4):
                pool.wait_ge(scattered[n], 16 * 8)

        @block.scalar
        def _(act):
            def step(c, u, e):
                wait_from_one(act, gl_ready, c - 1)
                wait_from_one(act, y_done, c - 1)
                for h in range(2):
                    act.wait_ge(g_done, 2 * c + h + 1)
                    act.activation(Gh[:, u, 2 * h:2 * h + 2], psG[u][h], ACT.Gelu).then_inc(gh_ready, 1)
                    act.activation(GF[:, u, 2 * h:2 * h + 2], psG[u][h], ACT.Gelu).then_inc(gelu_ready, 1)
                if u == 0:
                    act.wait_ge(w1_in, 16 * (e + 1))
                    act.activation(W1h[:, bass.ds(e, 1)].rearrange("p e i -> p (e i)"), WR1[:], ACT.Copy).then_inc(w_hi, 1)
                else:
                    act.wait_ge(w2_in, 16 * (e + 1))
                    act.activation(W2[:, bass.ds(e, 1), :, 0].rearrange("p e i f -> p (e i) f"), WR2[:], ACT.Copy).then_inc(w_hi, 1)
            for c in range(0, 4):
                step(c, c % 2, c // 2)
            with act.Fori(2, 8) as j:
                step(j * 2, 0, j)
                step(j * 2 + 1, 1, j)

        @block.vector
        def _(dve):
            L = Links(dve, dve_link)
            rev = K[0:TOK, K_REV:K_REV + E].unsqueeze(1).broadcast_to([TOK, NT, E])
            L.made(dve.memset(ones_s[:], 1.0))
            L.link(dve.tensor_reduce(lmax[:], LG[:], AX.X, ALU.max))
            L.link(dve.tensor_tensor(LG[:], LG[:], lmax[:].unsqueeze(2).broadcast_to([TOK, NT, E]), ALU.is_equal))
            L.link(dve.tensor_tensor(LG[:], LG[:], rev, ALU.mult))
            L.link(dve.tensor_reduce(top[:], LG[:], AX.X, ALU.max))
            dve.tensor_tensor(OH[:].rearrange("p e t -> p t e"), rev, top[:].unsqueeze(2).broadcast_to([TOK, NT, E]),
                              ALU.is_equal).then_inc(oh_ready, 1)
            dve.wait_ge(rank_done, 2)
            flat = "p e t -> p (e t)"
            L.link(dve.tensor_copy(CNT[:].rearrange(flat), psN))
            L.link(dve.tensor_tensor_scan(INCL[:].rearrange(flat), ones_s[:], CNT[:].rearrange(flat), 0.0, ALU.mult, ALU.add))
            L.link(dve.tensor_tensor(CNT[:], INCL[:], CNT[:], ALU.subtract))
            L.link(dve.tensor_tensor(n_e[:], INCL[:, :, NT - 1], CNT[:, :, 0], ALU.subtract))
            L.link(dve.tensor_scalar(n_i[:], n_e[:], 127.0, None, ALU.add))
            L.link(dve.tensor_scalar(n_i[:], n_i[:], 7, None, ALU.logical_shift_right))
            L.link(dve.tensor_copy(tiles_e[:], n_i[:]))
            L.link(dve.tensor_tensor_scan(ends[:], ones_s[:, 0:E], tiles_e[:], 0.0, ALU.mult, ALU.add))
            L.link(dve.tensor_tensor(starts[:], ends[:], tiles_e[:], ALU.subtract))
            L.link(dve.scalar_tensor_tensor(first[:], starts[:], 128.0, CNT[:, :, 0], ALU.mult, ALU.subtract))
            L.link(dve.tensor_tensor(RK[:].rearrange(flat), psR, CNT[0:TOK].rearrange(flat), ALU.add))
            L.link(dve.tensor_tensor(RK[:], RK[:], first[0:TOK].unsqueeze(2).broadcast_to([TOK, E, NT]), ALU.add))
            L.link(dve.tensor_tensor(RK[:], RK[:], OH[:], ALU.mult))
            L.link(dve.tensor_reduce(posf[:], RK[:].rearrange("p e t -> p t e"), AX.X, ALU.add))
            dve.tensor_copy(POS[:], posf[:]).then_inc(pos_ready, 1)
            L.link(dve.tensor_scalar(of_slot[:], K[:, K_IO:K_IO + SLOTS], starts[:, 1:2], None, ALU.is_ge))
            for e in range(2, E):
                L.link(dve.scalar_tensor_tensor(of_slot[:], K[:, K_IO:K_IO + SLOTS], starts[:, e:e + 1], of_slot[:], ALU.is_ge, ALU.add))
            L.link(dve.tensor_copy(OF[:], of_slot[:]))

            def step(c, u, e):
                w = 1 - u
                if on(c, 0, NC):
                    for h in range(2):
                        hs = slice(2 * h, 2 * h + 2)
                        dve.wait_ge(gelu_ready, 2 * c + h + 1)
                        if h == 0:
                            wait_from_one(dve, y_done, c - 1)
                        dve.wait_ge(gh_ready, 2 * c + h + 1)
                        ins = dve.tensor_tensor(Gl[:, u, hs], GF[:, u, hs], Gh[:, u, hs].bitcast(f32), ALU.subtract)
                    ins.then_inc(gl_ready, 1)
                    dve.wait_ge(w_hi, c + 1)
                    if u == 0:
                        dve.tensor_tensor(W1l[:, bass.ds(e, 1)].rearrange("p e i -> p (e i)"), WR1[:],
                                          W1h[:, bass.ds(e, 1)].rearrange("p e i -> p (e i)").bitcast(f32), ALU.subtract).then_inc(w1_split, 1)
                    else:
                        dve.tensor_tensor(W2[:, bass.ds(e, 1), :, 1].rearrange("p e i f -> p (e i) f"), WR2[:],
                                          W2[:, bass.ds(e, 1), :, 0].rearrange("p e i f -> p (e i) f").bitcast(f32), ALU.subtract).then_inc(w2_split, 1)
                if on(c - 1, 0, NC):
                    dve.wait_ge(y_done, c)
                    if isinstance(c, int):
                        if c >= 3:
                            dve.wait_ge(base_stored[w], 16 * ((c - 1) // 2))
                    else:
                        dve.wait_ge(base_stored[w], freed[0])
                    L.link(dve.tensor_tensor(BS[:, w], psY[w][:, :, 0], H[:, bass.ds((c - 1) * 2, 2)], ALU.add))
                    dve.tensor_tensor(BS[:, w], psY[w][:, :, 1], BS[:, w], ALU.add).then_inc(bs_ready, 1)
            freed = [None]
            for c in range(0, 4):
                step(c, c % 2, c // 2)
            with dve.Fori(2, 8) as j:
                L.loop(2, j, 2)
                freed[0] = (j - 1) * 16
                step(j * 2, 0, j)
                freed[0] = j * 16
                step(j * 2 + 1, 1, j)
            L.end(6)
            step(NC, 0, None)

        @block.tensor
        def _(pe):
            def step(c, u):
                w = 1 - u
                if on(c, 0, NC):
                    wait_from_one(pe, gelu_ready, 2 * (c - 1))
                    ts = bass.ds(c * CT, CT)
                    for i in range(IC):
                        for n, (a, x) in enumerate(((S1h, X2h), (S1l, X2h), (S1h, X2l))):
                            ins = pe.matmul(psG[u][i // 2][:, i % 2], a[:, 128 * i:128 * i + 128], x[:, ts], start=(n == 0), stop=(n == 2))
                        if i % 2:
                            ins.then_inc(g_done, 1)
                if on(c - 1, 0, NC):
                    pe.wait_ge(gl_ready, c)
                    wait_from_one(pe, bs_ready, c - 2)
                    for t in range(2):
                        for i in range(IC):
                            for n, a in enumerate((Gh, Gl)):
                                ins = pe.matmul(psY[w][:, t].rearrange("p h f -> p (h f)"), a[:, w, i, TOK * t:TOK * t + TOK],
                                                S2[:, i].rearrange("p h f -> p (h f)"), start=(i == 0 and n == 0), stop=(i == IC - 1 and n == 1))
                    ins.then_inc(y_done, 1)
            step(0, 0)
            pe.wait_ge(oh_ready, 1)
            flat = OH[:].rearrange("p e t -> p (e t)")
            pe.matmul(psR, K[0:TOK, K_LR:K_LR + TOK], flat, start=True, stop=True).then_inc(rank_done, 1)
            pe.matmul(psN, K[0:TOK, K_ONE:K_ONE + 128], flat, start=True, stop=True).then_inc(rank_done, 1)
            for c in range(1, 4):
                step(c, c % 2)
            with pe.Fori(2, 8) as j:
                step(j * 2, 0)
                step(j * 2 + 1, 1)
            step(NC, 0)


def experts(nc, m):
    K, ident, PS, OF = (m[n] for n in "K ident PS OF".split())
    routed, base, out_rows = m["routed"], m["base"], m["out_rows"]
    W1h, W1l, W2, XS, BG, TO, Xh, Xl, SG, GX, Gh, Gl, OS, IC = (
        m[n] for n in "W1h W1l W2 XS BG TO Xh Xl SG GX Gh Gl OS IC".split())
    with ExitStack() as ctx:
        def sem(name):
            return ctx.enter_context(nc.semaphore(name))

        xs_in, bg_in, stored = [sem(f"xs_in{n}") for n in range(4)], [sem(f"bg_in{n}") for n in range(4)], [sem("stored0"), sem("stored1")]
        bg_set, to_ready, dve_link, turn = sem("bg_set"), [sem("to_ready0"), sem("to_ready1")], sem("dve_link4"), sem("turn3")
        xt_done, xh_ready, xl_ready = sem("xt3_done"), sem("xh_ready"), sem("xl_ready")
        up_done, sg_ready, gx_ready, gt_done, gh_ready, gl_ready, y_done, os_ready = (
            sem(n) for n in ("up_done", "sg_ready", "gx_ready", "gt_done", "gth_ready", "gtl_ready", "y3_done", "os_ready"))
        psU = [[PS[2 * u + h][:, :] for h in range(2)] for u in range(2)]
        psX, psT = PS[4][:, 0:128], PS[5][:, :].rearrange("p (i s) -> p i s", i=IC)
        psY = [PS[6 + u][:, 0:2 * F] for u in range(2)]
        block = ctx.enter_context(nc.Block())

        LAST = SLOTS + 3

        def run(step, eng, links=None):
            for k in range(-2, 4):
                step(k, k % 4, None)
            with eng.Fori(1, 9) as j:
                if links is not None:
                    links.loop(1, j, 4)
                for n in range(4):
                    step(j * 4 + n, n, j)
            if links is not None:
                links.end(8)
            for k in range(36, LAST):
                step(k, k % 4, None)

        def wait_use(eng, sems, k, n, j, d):
            eng.wait_ge(sems[(n + d) % 4], 16 * ((k + d) // 4 + 1) if j is None else (j + (n + d) // 4) * 16 + 16)

        @block.sync
        def _(sp):
            def load(m, t):
                sp.dma_start(XS[:, t], routed[bass.ds(m * 128, 128), :]).then_inc(xs_in[t], 16)

            def step(k, n, j):
                if k is not None and on(k + 3, 0, SLOTS):
                    m = k + 3 if isinstance(k, int) else sp.snap(k + 3)
                    if not isinstance(k, int) or k > 0:
                        sp.wait_ge(xt_done, k)
                        sp.wait_ge(to_ready[1], k)
                    load(m, (n + 3) % 4)
            load(0, 0)
            run(step, sp)

        @block.gpsimd
        def _(pool):
            pool.memset(BG[:], 0.0).then_inc(bg_set, 1)
            pool.wait_ge(bg_set, 1)

            def step(k, n, j):
                t = (n + 2) % 4
                if on(k - 2, 0, SLOTS):
                    pool.wait_ge(os_ready, k - 1)
                    hold_waits(pool, turn)
                    pool.tensor_copy(TO[:, t, 0:1], TO[:, t, 1:2]).then_inc(to_ready[0], 1)
                    pool.wait_ge(to_ready[0], k - 1)
                if on(k + 2, 0, SLOTS):
                    wait_use(pool, xs_in, k, n, j, 2)
                    hold_waits(pool, turn)
                    pool.tensor_copy(TO[:, t, 1:2], XS[:, t, F:F + 1].bitcast(i32)).then_inc(to_ready[1], 1)
                if on(k - 2, 0, SLOTS):
                    hold_waits(pool, turn)
                    pool.indirect_dma_start(out_rows, bass.IndirectOffsetOnAxis(TO[:, t, 0:1], 0), OS[:, n % 2], None,
                                            bounds_check=N - 1, oob_is_err=False).then_inc(stored[n % 2], 16)
                if on(k + 2, 0, SLOTS):
                    pool.wait_ge(to_ready[1], k + 3)
                    hold_waits(pool, turn)
                    pool.indirect_dma_start(BG[:, t], None, base, bass.IndirectOffsetOnAxis(TO[:, t, 1:2], 0),
                                            bounds_check=N - 1, oob_is_err=False).then_inc(bg_in[t], 16)
            run(step, pool)
            pool.wait_ge(stored[0], 16 * ((SLOTS + 1) // 2))
            pool.wait_ge(stored[1], 16 * (SLOTS // 2))

        @block.scalar
        def _(act):
            def step(k, n, j):
                u, w = n % 2, 1 - n % 2
                if on(k + 1, 0, SLOTS):
                    act.wait_ge(xt_done, k + 2)
                    wait_from_one(act, up_done, 2 * k)
                    act.activation(Xh[:, w], psX, ACT.Copy).then_inc(xh_ready, 1)
                if on(k, 0, SLOTS):
                    act.wait_ge(up_done, 2 * k + 1)
                    wait_from_one(act, gx_ready, k - 1)
                    act.activation(SG[:, u], psU[u][0], ACT.Silu).then_inc(sg_ready, 1)
                if on(k - 1, 0, SLOTS):
                    act.wait_ge(gt_done, k)
                    wait_from_one(act, y_done, k - 2)
                    act.activation(Gh[:, w], psT, ACT.Copy).then_inc(gh_ready, 1)
            run(step, act)

        @block.vector
        def _(dve):
            L = Links(dve, dve_link)

            def step(k, n, j):
                u, w = n % 2, 1 - n % 2
                if on(k + 1, 0, SLOTS):
                    dve.wait_ge(xh_ready, k + 2)
                    dve.tensor_tensor(Xl[:, w], psX, Xh[:, w].bitcast(f32), ALU.subtract).then_inc(xl_ready, 1)
                if on(k, 0, SLOTS):
                    dve.wait_ge(up_done, 2 * k + 2)
                    dve.wait_ge(sg_ready, k + 1)
                    wait_from_one(dve, gt_done, k - 1)
                    dve.tensor_tensor(GX[:, u], psU[u][1], SG[:, u], ALU.mult).then_inc(gx_ready, 1)
                if on(k - 1, 0, SLOTS):
                    dve.wait_ge(gh_ready, k)
                    dve.tensor_tensor(Gl[:, w], psT, Gh[:, w].bitcast(f32), ALU.subtract).then_inc(gl_ready, 1)
                if on(k - 2, 0, SLOTS):
                    t = (n + 2) % 4
                    dve.wait_ge(y_done, k - 1)
                    if j is None:
                        dve.wait_ge(bg_in[t], 16 * ((k - 2) // 4 + 1))
                        if k - 4 >= 0:
                            dve.wait_ge(stored[u], 16 * ((k - 4) // 2 + 1))
                    else:
                        dve.wait_ge(bg_in[t], (j + (n - 2) // 4) * 16 + 16)
                        dve.wait_ge(stored[u], j * 32 + 16 * ((n - 4) // 2 + 1))
                    L.link(dve.tensor_tensor(OS[:, u], psY[u][:, 0:F], BG[:, t], ALU.add))
                    dve.tensor_tensor(OS[:, u], psY[u][:, F:2 * F], OS[:, u], ALU.add).then_inc(os_ready, 1)
            run(step, dve, L)

        @block.tensor
        def _(pe):
            def step(k, n, j):
                u, w = n % 2, 1 - n % 2
                if on(k + 1, 0, SLOTS):
                    wait_use(pe, xs_in, k, n, j, 1)
                    wait_from_one(pe, xl_ready, k + 1)
                    pe.transpose(psX, XS[:, (n + 1) % 4, 0:F], ident).then_inc(xt_done, 1)
                if on(k, 0, SLOTS):
                    e = pe.value_load(OF[0:1, bass.ds(k, 1)], min_val=0, max_val=E - 1)
                    pe.wait_ge(xl_ready, k + 1)
                    wait_from_one(pe, gx_ready, k - 1)
                    for h in range(2):
                        for p, (a, b) in enumerate(((Xh, W1h), (Xh, W1l), (Xl, W1h))):
                            ins = pe.matmul(psU[u][h], a[:, u], b[:, bass.ds(e, 1), I * h:I * h + I].rearrange("p e i -> p (e i)"), start=(p == 0), stop=(p == 2))
                        ins.then_inc(up_done, 1)
                if on(k - 1, 0, SLOTS):
                    pe.wait_ge(gx_ready, k)
                    wait_from_one(pe, gl_ready, k - 1)
                    for i in range(IC):
                        ins = pe.transpose(psT[:, i], GX[:, w, 128 * i:128 * i + 128], ident)
                    ins.then_inc(gt_done, 1)
                if on(k - 2, 0, SLOTS):
                    e = pe.value_load(OF[0:1, bass.ds(k - 2, 1)], min_val=0, max_val=E - 1)
                    pe.wait_ge(gl_ready, k - 1)
                    wait_from_one(pe, os_ready, k - 3)
                    for i in range(IC):
                        for p, a in enumerate((Gh, Gl)):
                            ins = pe.matmul(psY[u], a[:, u, i], W2[:, bass.ds(e, 1), i].rearrange("p e h f -> p (e h f)"),
                                            start=(i == 0 and p == 0), stop=(i == IC - 1 and p == 1))
                    ins.then_inc(y_done, 1)
            run(step, pe)


def lay_out(x, L0_tok_W, L0_tok_b, L0_attn_Wq, L0_attn_bq, L0_attn_Wk, L0_attn_bk, L0_attn_Wv, L0_attn_bv,
            L0_attn_gq, L0_attn_betaq, L0_attn_gv, L0_attn_betav, L0_attn_Wpos, L0_attn_Wout, L0_attn_bout,
            L0_ffn_gate_w, L0_ffn_w1, L0_ffn_w2, L0_ffn_w3, L0_ffn_sw1, L0_ffn_sw2):
    x = np.asarray(x)
    time = np.arange(S + 1, dtype=np.float32) / np.float32(S)
    path = np.empty((NB, S + 1, C), np.float32)
    path[:, :, 0] = time
    path[:, :, 1:] = x

    def tokens(a):
        return a.reshape(NT, TOK, C).transpose(1, 0, 2)
    W = np.asarray(L0_tok_W)
    o4 = C + C2 + C3
    wsig = np.zeros((128, NCH + 1, C, F), np.float32)
    wsig[:, :NCH] = W[:, o4:].reshape(F, NCH, 128, C).transpose(2, 1, 3, 0)
    wsig[0:C2, NCH] = W[:, C + C2:o4].reshape(F, C2, C).transpose(1, 2, 0)
    wsig[C2:C2 + C, NCH] = W[:, C:C + C2].reshape(F, C, C).transpose(1, 2, 0)
    wsig[C2 + C, NCH] = W[:, 0:C].T
    K = np.zeros((128, K_END), np.float32)
    K[:, K_ID:K_ID + 128] = np.eye(128)
    r, s = np.arange(TOK)[:, None], np.arange(TOK)[None, :]
    same = r // S == s // S
    K[0:TOK, K_LX:K_LX + TOK] = same & (r < s)
    K[0:TOK, K_LI:K_LI + TOK] = same & (r <= s)
    K[0:TOK, K_LR:K_LR + TOK] = r < s
    K[:, K_ONE:K_ONE + 128] = 1
    K[:, K_MB:K_MB + NH] = np.arange(128)[:, None] // DK == np.arange(NH)[None, :]
    K[:, K_REV:K_REV + E] = E - np.arange(E)
    K[:, K_IO:K_IO + SLOTS] = np.arange(SLOTS)
    K[0:18, K_CV], K[18:36, K_CV] = 1, -1
    K[18:36, K_CV + 1] = 1

    def rows(a, n):
        return np.broadcast_to(np.asarray(a)[None, :], (n, len(a)))
    vecs = np.zeros((128, 7), np.float32)
    for c, a in enumerate((L0_attn_gq, L0_attn_betaq, L0_attn_bq, L0_attn_bout)):
        vecs[:, c] = np.asarray(a)
    for c, a in enumerate((L0_attn_gv, L0_attn_betav, L0_attn_bv)):
        vecs[0:DK, P_GV + c] = np.asarray(a)
    return dict(
        path_now=tokens(path[:, :-1]), path_next=tokens(path[:, 1:]),
        path_first=tokens(np.broadcast_to(path[:, 0:1], (NB, S, C))),
        wsig=wsig.reshape(128, NCH + 1, 2, 512), consts=K,
        token_ids=(np.arange(NT)[None, :] * TOK + np.arange(TOK)[:, None]).astype(np.int32), tok_b=rows(L0_tok_b, TOK),
        qkv_b=rows(np.concatenate([np.asarray(a) for a in (L0_attn_bq, L0_attn_bk, L0_attn_bv)]), TOK),
        vecs=vecs, wqkv=np.concatenate([np.asarray(a) for a in (L0_attn_Wq, L0_attn_Wk, L0_attn_Wv)], axis=1),
        wpos=np.broadcast_to(np.asarray(L0_attn_Wpos).reshape(DK, 9).T[None, :, None, :], (4, 9, NH, DK)).reshape(36, 128),
        wout_v=np.broadcast_to(np.asarray(L0_attn_Wout).reshape(NH, 1, DK, F), (NH, DK, DK, F)).reshape(128, DK, F),
        wout=np.asarray(L0_attn_Wout), gate_w=np.asarray(L0_ffn_gate_w).T,
        sw1=np.asarray(L0_ffn_sw1).T, sw2=np.asarray(L0_ffn_sw2).T.reshape(4, 128, F).transpose(1, 0, 2),
        w13=np.concatenate([np.asarray(L0_ffn_w1), np.asarray(L0_ffn_w3)], axis=1).transpose(2, 0, 1),
        w2=np.asarray(L0_ffn_w2).transpose(0, 2, 1).reshape(E, 4, 128, F).transpose(2, 0, 1, 3),
    )


INPUTS = ("path_now", "path_next", "path_first", "wsig", "consts", "token_ids", "tok_b", "qkv_b", "vecs", "wqkv", "wpos",
          "wout_v", "wout", "gate_w", "sw1", "sw2", "w13", "w2")


def kernel(**inputs):
    import concourse.bacc as bacc
    from concourse.bass_utils import run_bass_kernel_spmd

    laid = lay_out(**inputs)
    nc = bacc.Bacc("TRN2", target_bir_lowering=False, num_devices=1)
    arrays, args = {}, []
    for name in INPUTS:
        a = np.ascontiguousarray(laid[name])
        arrays[f"in_{name}"] = a
        args.append(nc.dram_tensor(f"in_{name}", a.shape, mybir.dt.from_np(a.dtype), kind="ExternalInput").ap())
    args.append(nc.dram_tensor("out_h", (NB, S, F), f32, kind="ExternalOutput").ap())
    build(nc, *args)
    result = run_bass_kernel_spmd(nc, [arrays], core_ids=[0])
    return result.results[0]["out_h"]
```

```python
import concourse.bass as bass
from concourse import mybir
from contextlib import ExitStack
import numpy as np

f32 = mybir.dt.float32
f32r = mybir.dt.float32r
i32 = mybir.dt.int32
u32 = mybir.dt.uint32
ALU = mybir.AluOpType
ACT = mybir.ActivationFunctionType
AX = mybir.AxisListType

NB, S, F = 64, 63, 128
C = 8
NT, TOK = 32, 126
N = NB * S
DK, NH = 16, 8
QKV = F + 2 * DK
C3, C2 = C ** 3, C ** 2
TAIL = C2 + C + 1
NCH = C3 // 128
EPS = 1e-5
SP = 64
VB = 18 * SP + SP
GB = 4
NG = NB // GB
E, I = 8, 512
SLOTS = 39
ROW = 132
NOBODY = 1 << 20

K_ID, K_LX, K_LI, K_LR, K_ONE, K_MB, K_REV, K_IO = 0, 128, 254, 380, 506, 634, 642, 650
K_CV = K_IO + SLOTS
K_BD = K_CV + 2
K_END = K_BD + F + DK
P_GQ, P_BETAQ, P_BQ, P_BOUT, P_GV, P_BETAV, P_BV = range(7)


class Links:

    def __init__(self, eng, sem):
        self.eng, self.sem, self.base, self.n = eng, sem, 0, 0

    def made(self, ins):
        ins.then_inc(self.sem, 1)
        self.n += 1

    def wait(self):
        self.eng.wait_ge(self.sem, self.base + self.n)

    def link(self, ins):
        self.made(ins)
        self.wait()

    def loop(self, first, i, per):
        self.start, self.per = self.n, per
        self.base = self.n + (i - first) * per
        self.n = 0

    def end(self, passes):
        assert self.n == self.per, (self.n, self.per)
        self.n = self.start + passes * self.per
        self.base = 0


def on(k, low, high):
    return not isinstance(k, int) or low <= k < high


def hold_waits(eng, turn):
    eng.nop().then_inc(turn, 1)


def wait_from_one(eng, sem, value):
    if not isinstance(value, int) or value > 0:
        eng.wait_ge(sem, value)


def build(nc, path_now, path_next, path_first, wsig, consts, token_ids, tok_b, qkv_b, vecs, wqkv, wpos, wout,
          gate_w, sw1, sw2, w13, w2, out):
    q_raw = nc.dram_tensor("q_raw", [N, F], f32, kind="Internal").ap()
    k_raw = nc.dram_tensor("k_raw", [N, DK], f32, kind="Internal").ap()
    v_raw = nc.dram_tensor("v_raw", [N, DK], f32, kind="Internal").ap()

    v_pad = nc.dram_tensor("v_pad", [2, NB, VB], f32, kind="Internal").ap()
    pat_q = nc.dram_tensor("pat_q", [2, S, F], f32, kind="Internal").ap()
    x_rows = nc.dram_tensor("x_rows", [N, ROW], f32, kind="Internal").ap()
    routed = nc.dram_tensor("routed", [SLOTS * 128, ROW], f32, kind="Internal").ap()
    base = nc.dram_tensor("base", [N, F], f32, kind="Internal").ap()
    out_rows = out.rearrange("b s f -> (b s) f")

    with ExitStack() as whole:
        def keep(name, shape, dt=f32):
            return whole.enter_context(nc.sbuf_tensor(name, shape, dt))

        K = keep("K", [128, K_END])
        ident, ident_t = K[:, K_ID:K_ID + 128], K[0:TOK, K_ID:K_ID + TOK]
        before, upto_now = K[0:TOK, K_LX:K_LX + TOK], K[0:TOK, K_LI:K_LI + TOK]
        H = keep("H", [TOK, NT, F])
        PV = keep("PV", [128, 7])
        eps = keep("eps", [128, 1])
        carrier = keep("carrier", [1, 1])
        stQ, stV = keep("stQ", [128, NT, 6]), keep("stV", [DK, NT, 6])
        LG = keep("LG", [TOK, NT, E])
        X2h, X2l = keep("X2h", [128, N], f32r), keep("X2l", [128, N], f32r)
        S1h, S1l = keep("S1h", [F, I], f32r), keep("S1l", [F, I], f32r)
        S2 = keep("S2", [128, I // 128, 2, F], f32r)
        PS = [whole.enter_context(nc.psum_tensor(f"PS{n}", [128, 512], f32)) for n in range(8)]
        with ExitStack() as attn:
            def early(name, shape, dt=f32):
                return attn.enter_context(nc.sbuf_tensor(name, shape, dt))
            QR = early("QR", [128, NB, SP])
            SR1, SR2 = early("SR1", [F, I]), early("SR2", [128, I // 128, F])
            WP, WO, GW = early("WP", [36, 128]), early("WO", [128, F]), early("GW", [F, E])
            IDS, nobody = early("IDS", [TOK, NT], i32), early("nobody", [128, ROW])
            early_in, routed_set, q_loaded = (attn.enter_context(nc.semaphore(n)) for n in ("early_in", "routed_set", "q_loaded"))
            signatures(nc, locals())
            attention(nc, locals())
        ffn(nc, locals())


def signatures(nc, m):
    K, ident_t, before, upto_now, H, PV, eps, carrier = (m[n] for n in "K ident_t before upto_now H PV eps carrier".split())
    stQ, stV, PS, QR, q_raw, k_raw, v_raw = (m[n] for n in "stQ stV PS QR q_raw k_raw v_raw".split())
    path_now, path_next, path_first, wsig, consts, tok_b, qkv_b, vecs, wqkv = (
        m[n] for n in "path_now path_next path_first wsig consts tok_b qkv_b vecs wqkv".split())
    wpos, gate_w, token_ids, wout, sw1, sw2, routed = (m[n] for n in "wpos gate_w token_ids wout sw1 sw2 routed".split())
    WP, GW, IDS, WO, SR1, SR2, nobody, early_in, routed_set, q_loaded = (
        m[n] for n in "WP GW IDS WO SR1 SR2 nobody early_in routed_set q_loaded".split())
    with ExitStack() as ctx:
        def sb(name, shape, dt=f32):
            return ctx.enter_context(nc.sbuf_tensor(name, shape, dt))

        def sem(name):
            return ctx.enter_context(nc.semaphore(name))

        pnow, pnext, pfirst = (sb(n, [TOK, NT, C]) for n in ("pnow", "pnext", "pfirst"))
        V, Vhalf, Vthird, S1, C2h, C3h, C4h = (sb(n, [TOK, NT, C]) for n in ("V", "Vhalf", "Vthird", "S1", "C2h", "C3h", "C4h"))
        E2, E3, A2T = (sb(n, [TOK, NT, C, C]) for n in ("E2", "E3", "A2T"))
        A2X = sb("A2X", [TOK, NT, TAIL])
        INC, TOP = (sb(n, [TOK, 2, C3]) for n in ("INC", "TOP"))
        AXs = sb("AXs", [TOK, 2, TAIL])
        AS = sb("AS", [128, NCH, TOK])
        Ah, Al = (sb(n, [128, 2, NCH + 1, TOK], f32r) for n in ("Ah", "Al"))
        WR = sb("WR", [128, 2, 2, 512])
        Wh, Wl = (sb(n, [128, NCH + 1, 2, 512], f32r) for n in ("Wh", "Wl"))
        Vt = sb("Vt", [TOK, 2, C])
        Z = sb("Z", [TOK, 2, F])
        tokb = sb("tokb", [TOK, F])
        qkvb = sb("qkvb", [TOK, QKV])
        wqkv_s = sb("wqkv_s", [128, QKV])
        ST, MV, SD = sb("ST", [TOK, 2, 6]), sb("MV", [TOK, 2, 2]), sb("SD", [TOK, 2, 2])
        XN = sb("XN", [TOK, 2, F])
        XT = sb("XT", [128, 2, TOK])
        QS = sb("QS", [TOK, 2, QKV])

        psA = PS[0][:, 0:NCH * TOK].rearrange("p (c s) -> p c s", c=NCH)
        psT = PS[1][:, 0:NCH * TOK].rearrange("p (c s) -> p c s", c=NCH)
        psB = PS[6][0:TAIL, F:F + TOK]
        psU = [[PS[2 + 2 * u + h][0:TOK, :].rearrange("p (d o) -> p d o", d=4) for h in range(2)] for u in range(2)]
        psH = PS[6][0:TOK, 0:F]
        psX = PS[7][:, 0:TOK]
        psQKV, psQT, psVT = PS[7][0:TOK, 0:QKV], PS[7][:, QKV:QKV + TOK], PS[7][0:DK, 288:288 + TOK]

        path_in, const_in, wsig_in = sem("path_in"), sem("const_in"), [sem(f"wsig_in{c}") for c in range(NCH + 1)]
        small_in = sem("small_in")
        consts_set, nobody_set = sem("consts_set"), sem("nobody_set")
        w_hi, w_lo_pool, w_lo_dve = sem("w_hi"), sem("w_lo_pool"), sem("w_lo_dve")
        horner_ready, a2t_ready = sem("horner_ready"), sem("a2t_ready")
        e2_ready, s2_done, a2_ready, a2x_ready = sem("e2_ready"), sem("s2_done"), sem("a2_ready"), sem("a2x_ready")
        inc_ready, top_ready, ax_ready, at_done = sem("inc_ready"), sem("top_ready"), sem("ax_ready"), sem("at_done")
        tt_done, tt_ready, as_ready, ah_ready, al_ready = sem("tt_done"), sem("tt_ready"), sem("as_ready"), sem("ah_ready"), sem("al_ready")
        u0_done, u1_done, c0_done, z_ready = sem("u0_done"), sem("u1_done"), sem("c0_done"), sem("z_ready")
        h_done, h_ready, mv_ready, sd_ready, xn_ready = sem("h_done"), sem("h_ready"), sem("mv_ready"), sem("sd_ready"), sem("xn_ready")
        xt_done, xt_ready, qkv_done, qs_ready, stats_done = sem("xt_done"), sem("xt_ready"), sem("qkv_done"), sem("qs_ready"), sem("stats_done")
        qs_stored = [sem("qs_stored0"), sem("qs_stored1")]
        dve_link = sem("dve_link")

        block = ctx.enter_context(nc.Block())

        raw_q = QR[:].rearrange("p b s -> p (b s)")
        raw = [WR[:, c] for c in range(2)] + [raw_q[:, 1024 * c:1024 * c + 1024].rearrange("p (h n) -> p h n", h=2) for c in range(NCH - 1)]
        BY_POOL = 2
        psS = [PS[n][0:TOK, :] for n in (7, 4, 5, 7)]

        def outer(eng, o, a, b, ts):
            n = ts.stop - ts.start
            return eng.tensor_tensor(o[:, ts], a[:, ts].unsqueeze(3).broadcast_to([TOK, n, C, C]),
                                     b[:, ts].unsqueeze(2).broadcast_to([TOK, n, C, C]), ALU.mult)

        def run_steps(eng, step, links=None, per=0, after={}):
            for k in range(-1, 4):
                step(k, k % 2)
                if k in after:
                    after[k]()
            with eng.Fori(2, 15) as j:
                if links:
                    links.loop(2, j, per)
                step(j * 2, 0)
                step(j * 2 + 1, 1)
            if links:
                links.end(13)
            for k in range(30, NT + 2):
                step(k, k % 2)

        @block.sync
        def _(sp):
            sp.dma_start(pnext[:], path_next).then_inc(path_in, 16)
            sp.dma_start(pnow[:], path_now).then_inc(path_in, 16)
            sp.dma_start(pfirst[:], path_first).then_inc(path_in, 16)
            sp.dma_start(K[:], consts).then_inc(const_in, 16)
            for c in range(NCH + 1):
                sp.dma_start(raw[c], wsig[:, c]).then_inc(wsig_in[c], 16)
            for to, src in ((tokb, tok_b), (qkvb, qkv_b), (PV, vecs), (wqkv_s, wqkv)):
                sp.dma_start(to[:], src).then_inc(small_in, 16)
            for to, src in ((WP, wpos), (GW, gate_w), (IDS, token_ids), (WO, wout), (SR1, sw1), (SR2, sw2)):
                sp.dma_start(to[:], src).then_inc(early_in, 16)
            sp.wait_ge(nobody_set, 2)
            sp.dma_start(routed.rearrange("(t p) c -> p t c", p=128), nobody[:].unsqueeze(1).broadcast_to([128, SLOTS, ROW])).then_inc(routed_set, 16)

            def step(k, u):
                if on(k - 2, 0, NT):
                    t = k - 2
                    sp.wait_ge(qs_ready, t + 1)
                    sp.dma_start(q_raw[bass.ds(t * TOK, TOK), :], QS[:, u, 0:F]).then_inc(qs_stored[u], 16)
                    sp.dma_start(k_raw[bass.ds(t * TOK, TOK), :], QS[:, u, F:F + DK]).then_inc(qs_stored[u], 16)
                    sp.dma_start(v_raw[bass.ds(t * TOK, TOK), :], QS[:, u, F + DK:QKV]).then_inc(qs_stored[u], 16)
                if on(k - 3, 0, NT):
                    load_q(k - 3, k)

            def load_q(t, k):
                if isinstance(t, int):
                    sp.wait_ge(qs_stored[t % 2], 48 * (t // 2 + 1))
                else:
                    sp.wait_ge(*k_of[0])
                src = q_raw.rearrange("(b s) f -> b (s f)", b=NB)[bass.ds(t * 2, 2), :].rearrange("b (p s) -> p b s", p=128)
                sp.dma_start(QR[:, bass.ds(t * 2, 2), 0:S], src).then_inc(q_loaded, 16)

            k_of = [None]
            for k in range(-1, 4):
                step(k, k % 2)
            with sp.Fori(2, 15) as j:
                k_of[0] = (qs_stored[1], (j - 1) * 48)
                step(j * 2, 0)
                k_of[0] = (qs_stored[0], j * 48)
                step(j * 2 + 1, 1)
            for k in range(30, NT + 2):
                step(k, k % 2)
            load_q(NT - 1, None)

        @block.gpsimd
        def _(pool):
            pool.memset(A2X[:, :, C2 + C:TAIL], 1.0).then_inc(consts_set, 1)
            pool.memset(eps[:], EPS).then_inc(consts_set, 1)
            pool.memset(nobody[:], 0.0).then_inc(nobody_set, 1)
            pool.wait_ge(nobody_set, 1)
            pool.memset(nobody[:, F:F + 1].bitcast(i32), NOBODY).then_inc(nobody_set, 1)

            def second_horner(ts):
                outer(pool, A2T, C4h, Vthird, ts).then_inc(a2t_ready, 1)
            pool.wait_ge(horner_ready, 1)
            second_horner(slice(0, 8))
            for c in range(BY_POOL):
                pool.wait_ge(w_hi, c + 1)
                pool.tensor_tensor(Wl[:, c], raw[c], Wh[:, c].bitcast(f32), ALU.subtract).then_inc(w_lo_pool, 1)
            pool.wait_ge(a2_ready, 2)

            def others():
                second_horner(slice(8, NT))

            def sums_ready():
                pool.wait_ge(a2_ready, 4)
                pool.wait_ge(w_lo_dve, NCH + 1 - BY_POOL)
                pool.memset(QR[:, :, S:SP], 0.0).then_inc(consts_set, 1)

            def step(k, u):
                t = k + 1
                if on(t, 0, NT):
                    wait_from_one(pool, at_done, t - 1)
                    pool.tensor_tensor(
                        TOP[:, 1 - u].rearrange("p (a b) -> p a b", b=C),
                        A2T[:, bass.ds(t, 1)].rearrange("p t a b -> p (t a b)").unsqueeze(2).broadcast_to([TOK, C2, C]),
                        Vhalf[:, bass.ds(t, 1)].broadcast_to([TOK, C2, C]), ALU.mult).then_inc(top_ready, 1)
            run_steps(pool, step, after={-1: others, 0: sums_ready})

        @block.scalar
        def _(act):
            for c in range(NCH + 1):
                act.wait_ge(wsig_in[c], 16)
                act.activation(Wh[:, c], raw[c], ACT.Copy).then_inc(w_hi, 1)
            act.wait_ge(a2_ready, 2)
            act.wait_ge(a2x_ready, 1)
            act.wait_ge(consts_set, 2)

            def step(k, u):
                if on(k + 1, 0, NT):
                    wait_from_one(act, at_done, k)
                    act.activation(AXs[:, 1 - u], A2X[:, bass.ds(k + 1, 1)].rearrange("p t c -> p (t c)"), ACT.Copy).then_inc(ax_ready, 1)
                if on(k + 1, 0, NT):
                    act.wait_ge(tt_done, k + 2)
                    wait_from_one(act, al_ready, k + 1)
                    act.activation(AS[:], psT, ACT.Copy).then_inc(tt_ready, 1)
                if on(k - 1, 0, NT):
                    act.wait_ge(mv_ready, k)
                    act.activation(SD[:, 1 - u, 0:1], MV[:, 1 - u, 1:2], ACT.Sqrt, bias=eps[0:TOK, :]).then_inc(sd_ready, 1)
                if on(k + 1, 0, NT):
                    act.wait_ge(at_done, k + 2)
                    wait_from_one(act, u1_done, k)
                    act.activation(Ah[0:TAIL, 1 - u, NCH], psB, ACT.Copy).then_inc(ah_ready, 1)
                    act.wait_ge(as_ready, k + 2)
                    act.activation(Ah[:, 1 - u, 0:NCH], AS[:], ACT.Copy).then_inc(ah_ready, 1)
                if on(k - 1, 0, NT):
                    act.wait_ge(xt_done, k)
                    wait_from_one(act, qkv_done, k - 2)
                    act.activation(XT[:, 1 - u], psX, ACT.Copy).then_inc(xt_ready, 1)
            run_steps(act, step, after={0: lambda: act.wait_ge(a2_ready, 4)})

        @block.vector
        def _(dve):
            L = Links(dve, dve_link)
            dve.wait_ge(path_in, 48)
            L.made(dve.tensor_tensor(V[:], pnext[:], pnow[:], ALU.subtract))
            L.link(dve.tensor_tensor(S1[:], pnow[:], pfirst[:], ALU.subtract))
            L.made(dve.tensor_scalar(Vthird[:], V[:], 1.0 / 3.0, None, ALU.mult))
            dve.scalar_tensor_tensor(C4h[:], V[:], 0.25, S1[:], ALU.mult, ALU.add).then_inc(horner_ready, 1)
            L.link(dve.scalar_tensor_tensor(C2h[:], V[:], 0.5, S1[:], ALU.mult, ALU.add))
            outer(dve, E2, C2h, V, slice(0, NT)).then_inc(e2_ready, 1)
            L.made(dve.tensor_scalar(Vhalf[:], V[:], 0.5, None, ALU.mult))
            L.link(dve.scalar_tensor_tensor(C3h[:], V[:], 1.0 / 3.0, S1[:], ALU.mult, ALU.add))
            dve.tensor_copy(A2X[:, :, C2:C2 + C], C2h[:]).then_inc(a2x_ready, 1)

            def first_horner(ts):
                L.link(outer(dve, E3, C3h, Vhalf, ts))

            def add_level2(q):
                ts = slice(8 * q, 8 * q + 8)
                dve.wait_ge(s2_done, q + 1)
                s2 = psS[q].rearrange("p (t c) -> p t c", t=8)
                dve.tensor_tensor(A2X[:, ts, 0:C2], s2, E3[:, ts].rearrange("p t a b -> p t (a b)"), ALU.add)
                a2 = A2T[:, ts].rearrange("p t a b -> p t (a b)")
                dve.wait_ge(a2t_ready, 1 if q == 0 else 2)
                return dve.tensor_tensor(a2, s2, a2, ALU.add)
            first_horner(slice(0, 8))
            add_level2(0).then_inc(a2_ready, 2)
            dve.wait_ge(a2_ready, 2)

            def weights_low():
                for c in range(BY_POOL, NCH + 1):
                    dve.wait_ge(w_hi, c + 1)
                    dve.tensor_tensor(Wl[:, c], raw[c], Wh[:, c].bitcast(f32), ALU.subtract).then_inc(w_lo_dve, 1)

            def others():
                first_horner(slice(8, NT))
                for q in range(1, 4):
                    ins = add_level2(q)
                ins.then_inc(a2_ready, 2)
                dve.wait_ge(a2_ready, 4)
                dve.wait_ge(small_in, 64)

            def combine(u, h, first, last):
                for d in range(4):
                    sc = Vt[:, u, 4 * h + d:4 * h + d + 1]
                    if first and d == 0:
                        ins = dve.tensor_scalar(Z[:, u], psU[u][h][:, d], sc, None, ALU.mult)
                    else:
                        ins = dve.scalar_tensor_tensor(Z[:, u], psU[u][h][:, d], sc, Z[:, u], ALU.mult, ALU.add)
                    if d == 3:
                        ins.then_inc(last, 1)
                    else:
                        L.link(ins)

            def step(k, u):
                w = 1 - u
                if on(k + 1, 0, NT):
                    t = k + 1
                    wait_from_one(dve, at_done, k)
                    dve.tensor_tensor(INC[:, w].rearrange("p (a b) -> p a b", b=C),
                                      A2X[:, bass.ds(t, 1), 0:C2].rearrange("p t c -> p (t c)").unsqueeze(2).broadcast_to([TOK, C2, C]),
                                      V[:, bass.ds(t, 1)].broadcast_to([TOK, C2, C]), ALU.mult).then_inc(inc_ready, 1)
                    if isinstance(k, int) and k == -1:
                        weights_low()
                if on(k - 1, 0, NT):
                    dve.wait_ge(u1_done, k)
                    dve.wait_ge(c0_done, k)
                    combine(w, 1, False, z_ready)
                if on(k - 2, 0, NT):
                    t = k - 2
                    dve.wait_ge(qkv_done, k - 1)
                    if isinstance(k, int):
                        if t >= 2:
                            dve.wait_ge(qs_stored[u], 48 * (t // 2))
                    else:
                        dve.wait_ge(qs_stored[u], stored[0])
                    dve.tensor_tensor(QS[:, u], psQKV, qkvb[:], ALU.add).then_inc(qs_ready, 1)
                    L.made(dve.bn_stats(stQ[:, bass.ds(t, 1)].rearrange("p t c -> p (t c)"), psQT))
                    dve.bn_stats(stV[:, bass.ds(t, 1)].rearrange("p t c -> p (t c)"), psVT).then_inc(stats_done, 1)
                if on(k - 1, 0, NT):
                    t = k - 1
                    dve.wait_ge(h_done, k)
                    ht = H[:, bass.ds(t, 1)].rearrange("p t c -> p (t c)")
                    dve.tensor_tensor(ht, psH, tokb[:], ALU.add).then_inc(h_ready, 1)
                    dve.wait_ge(h_ready, k)
                    dve.memset(carrier[:], 0.0)
                    L.link(dve.bn_stats(ST[:, w], ht))
                    dve.memset(carrier[:], 0.0)
                    dve.bn_aggr(MV[:, w], ST[:, w]).then_inc(mv_ready, 1)
                if on(k + 1, 0, NT):
                    dve.wait_ge(at_done, k + 2)
                    dve.wait_ge(tt_ready, k + 2)
                    dve.tensor_tensor(AS[:], psA, AS[:], ALU.add).then_inc(as_ready, 1)
                if on(k, 0, NT):
                    L.link(dve.tensor_copy(Vt[:, u], V[:, bass.ds(k, 1)].rearrange("p t c -> p (t c)")))
                    dve.wait_ge(u0_done, k + 1)
                    combine(u, 0, True, c0_done)
                if on(k - 1, 0, NT):
                    dve.wait_ge(sd_ready, k)
                    L.link(dve.reciprocal(SD[:, w, 1:2], SD[:, w, 0:1]))
                    wait_from_one(dve, xt_done, k - 2)
                    dve.tensor_scalar(XN[:, w], ht, MV[:, w, 0:1], SD[:, w, 1:2], ALU.subtract, ALU.mult).then_inc(xn_ready, 1)
                if on(k + 1, 0, NT):
                    dve.wait_ge(ah_ready, 2 * (k + 2))
                    L.made(dve.tensor_tensor(Al[:, w, 0:NCH], AS[:], Ah[:, w, 0:NCH].bitcast(f32), ALU.subtract))
                    dve.tensor_tensor(Al[0:TAIL, w, NCH], psB, Ah[0:TAIL, w, NCH].bitcast(f32), ALU.subtract).then_inc(al_ready, 1)

            stored = [None]
            for k in range(-1, 4):
                step(k, k % 2)
                if k == -1:
                    others()
            with dve.Fori(2, 15) as j:
                L.loop(2, j, 22)
                stored[0] = (j - 1) * 48
                step(j * 2, 0)
                step(j * 2 + 1, 1)
            L.end(13)
            for k in range(30, NT + 2):
                step(k, k % 2)

        @block.tensor
        def _(pe):
            pe.wait_ge(const_in, 16)
            pe.wait_ge(e2_ready, 1)

            def level2(q):
                pe.matmul(psS[q], before, E2[:, 8 * q:8 * q + 8].rearrange("p t a b -> p (t a b)"),
                          start=True, stop=True).then_inc(s2_done, 1)
            level2(0)
            pe.wait_ge(a2_ready, 2)

            def others():
                for q in range(1, 4):
                    level2(q)

            def half(k, u, h, done):
                for n, (a, w) in enumerate(((Ah, Wh), (Ah, Wl), (Al, Wh))):
                    if n == 2:
                        pe.wait_ge(al_ready, k + 1)
                    for c in range(NCH + 1):
                        rows = 128 if c < NCH else TAIL
                        ins = pe.matmul(psU[u][h].rearrange("p d o -> p (d o)"), a[0:rows, u, c], w[0:rows, c, h],
                                        start=(n == 0 and c == 0), stop=(n == 2 and c == NCH))
                ins.then_inc(done, 1)

            def step(k, u):
                w = 1 - u
                if on(k, 0, NT):
                    if isinstance(k, int) and k == 0:
                        pe.wait_ge(w_lo_pool, BY_POOL)
                        pe.wait_ge(w_lo_dve, NCH + 1 - BY_POOL)
                    pe.wait_ge(ah_ready, 2 * (k + 1))
                    wait_from_one(pe, c0_done, k - 1)
                    half(k, u, 0, u0_done)
                if on(k - 2, 0, NT):
                    if isinstance(k, int) and k == 2:
                        pe.wait_ge(small_in, 64)
                    pe.wait_ge(xt_ready, k - 1)
                    wait_from_one(pe, stats_done, k - 2)
                    pe.matmul(psQKV, XT[:, u], wqkv_s[:], start=True, stop=True)
                    pe.matmul(psQT, wqkv_s[:, 0:F], XT[:, u], start=True, stop=True)
                    pe.matmul(psVT, wqkv_s[:, F + DK:QKV], XT[:, u], start=True, stop=True).then_inc(qkv_done, 1)
                if on(k - 1, 0, NT):
                    pe.wait_ge(z_ready, k)
                    wait_from_one(pe, h_ready, k - 1)
                    pe.matmul(psH, upto_now, Z[:, w], start=True, stop=True).then_inc(h_done, 1)
                if on(k + 1, 0, NT):
                    pe.wait_ge(top_ready, k + 2)
                    wait_from_one(pe, al_ready, k + 1)
                    for c in range(NCH):
                        ins = pe.transpose(psT[:, c], TOP[:, w, 128 * c:128 * c + 128], ident_t)
                    ins.then_inc(tt_done, 1)
                    pe.wait_ge(inc_ready, k + 2)
                    pe.wait_ge(ax_ready, k + 2)
                    for c in range(NCH):
                        pe.matmul(psA[:, c], INC[:, w, 128 * c:128 * c + 128], before, start=True, stop=True)
                    if on(k - 1, 0, NT):
                        pe.wait_ge(h_ready, k)
                    pe.transpose(psB, AXs[:, w], ident_t).then_inc(at_done, 1)
                if on(k, 0, NT):
                    wait_from_one(pe, z_ready, k - 1)
                    half(k, u, 1, u1_done)
                if on(k - 1, 0, NT):
                    pe.wait_ge(xn_ready, k)
                    wait_from_one(pe, stats_done, k - 1)
                    pe.transpose(psX, XN[:, w], ident_t).then_inc(xt_done, 1)
            run_steps(pe, step, after={-1: others, 0: lambda: pe.wait_ge(a2_ready, 4)})


def attention(nc, m):
    K, ident, ident_t, H, PV, eps, carrier, LG, X2h, X2l = (
        m[n] for n in "K ident ident_t H PV eps carrier LG X2h X2l".split())
    stQ, stV, PS, QR, k_raw, v_raw, v_pad, pat_q, x_rows = (
        m[n] for n in "stQ stV PS QR k_raw v_raw v_pad pat_q x_rows".split())
    WP, GW, IDS, WO, SR1, SR2, early_in, routed_set, q_loaded = (m[n] for n in "WP GW IDS WO SR1 SR2 early_in routed_set q_loaded".split())
    S1h, S1l, S2 = (m[n] for n in "S1h S1l S2".split())
    with ExitStack() as ctx:
        def sb(name, shape, dt=f32):
            return ctx.enter_context(nc.sbuf_tensor(name, shape, dt))

        def sem(name):
            return ctx.enter_context(nc.semaphore(name))

        G8 = NB // 8
        HV = DK // 2
        EARLY = 5
        P0, PF = sb("P0", [128, 2, GB, HV, SP]), sb("PF", [128, GB, HV, SP])
        Ph, Pl = (sb(n, [128, 2, GB, HV, SP], f32r) for n in ("Ph", "Pl"))
        BD = sb("BD", [128, F + DK], f32r)
        flat, n_k, n_v = PF[:].rearrange("p b v s -> p (b v s)"), G8 * S, S * DK
        KR, KS = (flat[:, n * n_k:(n + 1) * n_k].rearrange("p (g s) -> p g s", g=G8) for n in range(2))
        VR = flat[:, 2 * n_k:2 * n_k + n_v].rearrange("p (s k) -> p s k", s=S)
        VN = P0[:].rearrange("p u b v s -> p (u b v s)")[:, 0:n_v].rearrange("p (s k) -> p s k", s=S)
        VP = Ph[:].rearrange("p u b v s -> p (u b v s)")[:, 0:VB]
        by_key = "b s k -> b (s k)"
        kmax, ksum, krec = (sb(n, [128, G8]) for n in ("kmax", "ksum", "krec"))
        mvq, mvv = sb("mvq", [128, 2]), sb("mvv", [DK, 2])
        BNP, BNR = sb("BNP", [128, 4]), sb("BNR", [2, 128])
        bnt = sb("bnt", [128, 4])
        PQ = sb("PQ", [128, 2, S])
        KT, VT = sb("KT", [S, NB, DK]), sb("VT", [S, NB, DK])
        KH = sb("KH", [S, 2, GB, NH, DK])
        WPh, WPm, W36 = sb("WPh", [36, 128], f32r), sb("WPm", [36, 128]), sb("W36", [36, 128], f32r)
        RUN = (GB - 1) * VB + DK * SP
        IM = sb("IM", [36, 2, RUN], f32r)
        QN = sb("QN", [128, 2, GB, SP])
        LC = sb("LC", [128, 2, GB, NH, DK])
        YC = sb("YC", [128, 2, GB * SP])
        OTs = sb("OTs", [128, 2, GB, S])
        H1 = sb("H1", [TOK, 2, 2, F])
        ST, MV, SD = sb("ST2", [TOK, 2, 2, 6]), sb("MV2", [TOK, 2, 2, 2]), sb("SD2", [TOK, 2, 2, 2])
        XR = sb("XR", [TOK, 2, 2, ROW])
        XG = sb("XTg", [128, 2, 2 * TOK])

        k_in, v_in, vp_set, bv_done = sem("k_in"), sem("v_in"), sem("vp_set"), sem("bv_done")
        bn_ready, sdv_ready, bnp_ready, bnt_done, bnr_ready = sem("bn_ready"), sem("sdv_ready"), sem("bnp_ready"), sem("bnt_done"), sem("bnr_ready")
        pat_stored, pat_in, w36_ready = sem("pat_stored"), sem("pat_in"), sem("w36_ready")
        ks_ready, exp_done, k_ready, v_ready, vn_ready = sem("ks_ready"), sem("exp_done"), sem("k_ready"), sem("v_ready"), sem("vn_ready")
        v_stored, kt_done, vt_done, kvt_ready, lam_c_done, kh_ready = (
            sem("v_stored"), sem("kt_done"), sem("vt_done"), sem("kvt_ready"), sem("lam_c_done"), sem("kh_ready"))
        s_hi, s_lo = sem("s_hi"), sem("s_lo")
        im_in = [sem("im_in0"), sem("im_in1")]
        conv_done, p_ready, qn_ready, lc_ready = sem("conv_done"), sem("p_ready"), sem("qn_ready"), sem("lc_ready")
        ph_ready, pl_ready, sum_done, bd_ready = sem("ph_ready"), sem("pl_ready"), sem("sum_done"), sem("bd_ready")
        yc_done, yc_ready, ot_done, ot_ready = sem("yc_done"), sem("yc_ready"), sem("ot_done"), sem("ot_ready")
        ht_done, h1_ready, h1_kept, mv_ready, sd_ready, xn_ready = (
            sem("ht_done"), sem("h1_ready"), sem("h1_kept"), sem("mv2_ready"), sem("sd2_ready"), sem("xn2_ready"))
        ids_ready, xr_stored = sem("ids_ready"), [sem("xr_stored0"), sem("xr_stored1")]
        xt_done, xt_ready, xlo_ready, gate_done, lg_ready = sem("xt2_done"), sem("xt2_ready"), sem("xlo_ready"), sem("gate_done"), sem("lg_ready")
        dve_link, pool_link = sem("dve_link2"), sem("pool_link2")

        psC = [[PS[2 * u + h][:, :].rearrange("p (v s) -> p v s", v=8) for h in range(2)] for u in range(2)]
        psY = PS[4][:, 0:GB * SP]
        psO = PS[5][:, 0:GB * SP]
        psH = PS[6][0:TOK, 0:2 * F].rearrange("p (t f) -> p t f", t=2)
        psL = PS[6][:, 256:256 + GB * DK].rearrange("p (b v) -> p b v", b=GB)
        psV = PS[7][0:2 * NB, 0:2 * DK].rearrange("p (c k) -> p c k", c=2)
        psX = PS[7][:, 0:2 * TOK]
        psG = PS[7][0:TOK, 256:256 + 2 * E].rearrange("p (t e) -> p t e", t=2)

        block = ctx.enter_context(nc.Block())

        @block.sync
        def _(sp):
            sp.dma_start(KR, k_raw.rearrange("n k -> (n k)").rearrange("(g p s) -> p g s", g=G8, p=128)).then_inc(k_in, 16)
            for c in range(2):
                sp.dma_start(VR[NB * c:NB * c + NB], v_raw.rearrange("(b s) k -> b s k", b=NB)).then_inc(v_in, 16)
            sp.wait_ge(bnr_ready, 1)
            sp.dma_start(pat_q, BNR[0:2, :].unsqueeze(1).broadcast_to([2, S, F])).then_inc(pat_stored, 16)
            sp.wait_ge(pat_stored, 16)
            sp.dma_start(PQ[:], bass.AP(pat_q.tensor, 0, [[S, 128], [S * F, 2], [1, S]])).then_inc(pat_in, 16)
            sp.wait_ge(v_ready, 2)
            sp.dma_start(v_pad.rearrange("c b n -> (c b) n"), VP.bitcast(f32)).then_inc(v_stored, 16)
            sp.wait_ge(v_stored, 16)

            def load_im(t, u):
                for c in range(4):
                    src = v_pad[c % 2, bass.ds(t * GB, GB), :]
                    sp.dma_start(IM[9 * c:9 * c + 9, u].bitcast(f32),
                                 bass.AP(src.tensor, src.offset, [[SP, 3], [1, 3], [1, RUN]])).then_inc(im_in[u], 16)

            def step(g, u):
                if on(g + 1, 0, NG):
                    wait_from_one(sp, conv_done, g * GB)
                    load_im(g + 1, 1 - u)
                if on(g - 2, 0, NG):
                    sp.wait_ge(xn_ready, g - 1)
                    sp.wait_ge(ids_ready, g - 1)
                    sp.dma_start(x_rows[bass.ds((g - 2) * 2 * TOK, 2 * TOK), :].rearrange("(t p) c -> p t c", p=TOK),
                                 XR[:, u]).then_inc(xr_stored[u], 16)
            for g in range(-1, 4):
                step(g, g % 2)
            with sp.Fori(2, 7) as j:
                step(j * 2, 0)
                step(j * 2 + 1, 1)
            for g in range(14, NG + 3):
                step(g, g % 2)
            for u in range(2):
                sp.wait_ge(xr_stored[u], 16 * NG // 2)
            sp.wait_ge(routed_set, 16)

        @block.gpsimd
        def _(pool):
            L = Links(pool, pool_link)
            pool.memset(VP.bitcast(f32), 0.0).then_inc(vp_set, 1)
            L.made(pool.memset(QN[:, :, :, S:SP], 0.0))
            L.link(pool.memset(XR[:, :, :, F:ROW], 0.0))
            pool.wait_ge(early_in, 16 * 6)
            pool.wait_ge(q_loaded, 16 * NT)
            pool.wait_ge(pat_in, 16)

            def low(g, u, b):
                pool.wait_ge(ph_ready, g * GB + b + 1)
                if b == 0:
                    wait_from_one(pool, sum_done, g - 1)
                pool.tensor_tensor(Pl[:, u, b], PF[:, b], Ph[:, u, b].bitcast(f32), ALU.subtract).then_inc(pl_ready, 1)

            def step(g, u):
                w = 1 - u
                if on(g + 1, 0, NG):
                    wait_from_one(pool, p_ready, g * GB)
                    wait_from_one(pool, yc_done, g)
                    L.link(pool.tensor_tensor(QN[:, w, :, 0:S], QR[:, bass.ds((g + 1) * GB, GB), 0:S],
                                              PQ[:, 0:1].broadcast_to([128, GB, S]), ALU.mult))
                    pool.tensor_tensor(QN[:, w, :, 0:S], QN[:, w, :, 0:S],
                                       PQ[:, 1:2].broadcast_to([128, GB, S]), ALU.add).then_inc(qn_ready, 1)
                if on(g, 0, NG):
                    low(g, u, 0)
                    low(g, u, 1)
                if on(g - 2, 0, NG):
                    if isinstance(g, int):
                        if g >= 4:
                            pool.wait_ge(xr_stored[u], 16 * ((g - 2) // 2))
                    else:
                        pool.wait_ge(xr_stored[u], freed[0])
                    pool.tensor_copy(XR[:, u, :, F].bitcast(i32), IDS[:, bass.ds((g - 2) * 2, 2)]).then_inc(ids_ready, 1)
                if on(g - 3, 0, NG):
                    pool.wait_ge(xt_ready, 2 * (g - 2))
                    ts = bass.ds((g - 3) * 2 * TOK, 2 * TOK)
                    pool.tensor_tensor(X2l[:, ts], XG[:, w], X2h[:, ts].bitcast(f32), ALU.subtract).then_inc(xlo_ready, 1)
                if on(g, 0, NG):
                    low(g, u, 2)
                    low(g, u, 3)

            freed = [None]
            for g in range(-1, 4):
                step(g, g % 2)
            with pool.Fori(2, 7) as j:
                L.loop(2, j, 2)
                freed[0] = (j - 1) * 16
                step(j * 2, 0)
                step(j * 2 + 1, 1)
            L.end(5)
            for g in range(14, NG + 3):
                step(g, g % 2)

        @block.scalar
        def _(act):
            act.wait_ge(bn_ready, 2)
            act.activation(bnt[:, 0:1], mvq[:, 1:2], ACT.Sqrt, bias=eps[:]).then_inc(sdv_ready, 1)
            act.activation(bnt[0:DK, 1:2], mvv[:, 1:2], ACT.Sqrt, bias=eps[0:DK]).then_inc(sdv_ready, 1)
            act.wait_ge(bnt_done, 1)
            act.activation(BNR[:], PS[6][0:2, 0:128], ACT.Copy).then_inc(bnr_ready, 1)
            act.wait_ge(ks_ready, 1)
            act.activation(KS, KS, ACT.Exp).then_inc(exp_done, 1)
            act.wait_ge(kt_done, 1)
            for h in range(2):
                act.activation(KT[:, 32 * h:32 * h + 32].rearrange("p b k -> p (b k)"), PS[h][0:S, :], ACT.Copy).then_inc(kvt_ready, 1)
            act.wait_ge(vt_done, 1)
            for h in range(2):
                act.activation(VT[:, :, 8 * h:8 * h + 8].rearrange("p b k -> p k b"), PS[2 + h][0:S, :].rearrange("p (k b) -> p k b", b=NB),
                               ACT.Copy).then_inc(kvt_ready, 1)
            act.wait_ge(kvt_ready, 4)

            def high(g, u, b):
                act.wait_ge(p_ready, g * GB + b + 1)
                if b == 0:
                    wait_from_one(act, sum_done, g - 1)
                act.activation(Ph[:, u, b], PF[:, b], ACT.Copy).then_inc(ph_ready, 1)

            def step(g, u):
                w = 1 - u
                if on(g + 1, 0, NG):
                    wait_from_one(act, lam_c_done, g)
                    act.activation(KH[:, w], KT[:, bass.ds((g + 1) * GB, GB)].unsqueeze(2).broadcast_to([S, GB, NH, DK]),
                                   ACT.Copy).then_inc(kh_ready, 1)
                if on(g, 0, NG):
                    high(g, u, 0)
                    high(g, u, 1)
                if on(g - 2, 0, NG):
                    act.wait_ge(mv_ready, 2 * (g - 1))
                    act.activation(SD[:, u, :, 0], MV[:, u, :, 1], ACT.Sqrt, bias=eps[0:TOK, :]).then_inc(sd_ready, 1)
                    act.activation(H[:, bass.ds((g - 2) * 2, 2)], H1[:, u], ACT.Copy).then_inc(h1_kept, 1)
                if on(g, 0, NG):
                    high(g, u, 2)
                    high(g, u, 3)
                if on(g - 1, 0, NG):
                    act.wait_ge(sum_done, g)
                    wait_from_one(act, ot_done, g - 2)
                    act.activation(YC[:, w], psY, ACT.Copy).then_inc(yc_ready, 1)
                if on(g - 2, 0, NG):
                    act.wait_ge(xt_done, g - 1)
                    wait_from_one(act, xlo_ready, g - 3)
                    wait_from_one(act, gate_done, g - 3)
                    act.activation(XG[:, u], psX, ACT.Copy).then_inc(xt_ready, 1)
                    act.activation(X2h[:, bass.ds((g - 2) * 2 * TOK, 2 * TOK)], psX, ACT.Copy).then_inc(xt_ready, 1)
                if on(g - 1, 0, NG):
                    act.wait_ge(ot_done, g)
                    wait_from_one(act, ht_done, g - 2)
                    act.activation(OTs[:, w], psO.rearrange("p (b s) -> p b s", b=GB)[:, :, 0:S], ACT.Identity,
                                   bias=PV[:, P_BOUT:P_BOUT + 1]).then_inc(ot_ready, 1)
            for g in range(-1, 4):
                step(g, g % 2)
                if g == 0:
                    act.activation(S1h[:], SR1[:], ACT.Copy).then_inc(s_hi, 1)
                    act.activation(S2[:, :, 0], SR2[:], ACT.Copy).then_inc(s_hi, 1)
            with act.Fori(2, 7) as j:
                step(j * 2, 0)
                step(j * 2 + 1, 1)
            for g in range(14, NG + 3):
                step(g, g % 2)

        @block.vector
        def _(dve):
            L = Links(dve, dve_link)
            dve.bn_aggr(mvq[:], stQ[:].rearrange("p t c -> p (t c)")).then_inc(bn_ready, 1)
            dve.bn_aggr(mvv[:], stV[:].rearrange("p t c -> p (t c)")).then_inc(bn_ready, 1)
            L.link(dve.memset(BNP[:], 0.0))
            dve.wait_ge(bn_ready, 2)
            L.made(dve.tensor_tensor(bnt[:, 2:3], mvq[:, 0:1], PV[:, P_BQ:P_BQ + 1], ALU.add))
            L.made(dve.tensor_tensor(bnt[0:DK, 3:4], mvv[:, 0:1], PV[0:DK, P_BV:P_BV + 1], ALU.add))
            dve.wait_ge(sdv_ready, 2)
            L.made(dve.reciprocal(bnt[:, 0:1], bnt[:, 0:1]))
            L.link(dve.reciprocal(bnt[0:DK, 1:2], bnt[0:DK, 1:2]))
            L.made(dve.tensor_tensor(BNP[:, 0:1], bnt[:, 0:1], PV[:, P_GQ:P_GQ + 1], ALU.mult))
            L.link(dve.tensor_tensor(BNP[0:DK, 2:3], bnt[0:DK, 1:2], PV[0:DK, P_GV:P_GV + 1], ALU.mult))
            L.made(dve.tensor_tensor(bnt[:, 2:3], bnt[:, 2:3], BNP[:, 0:1], ALU.mult))
            L.link(dve.tensor_tensor(bnt[0:DK, 3:4], bnt[0:DK, 3:4], BNP[0:DK, 2:3], ALU.mult))
            L.made(dve.tensor_tensor(BNP[:, 1:2], PV[:, P_BETAQ:P_BETAQ + 1], bnt[:, 2:3], ALU.subtract))
            L.link(dve.tensor_tensor(BNP[0:DK, 3:4], PV[0:DK, P_BETAV:P_BETAV + 1], bnt[0:DK, 3:4], ALU.subtract))
            L.link(dve.tensor_copy(bnt[:, 0:4], BNP[:]))
            dve.sem_inc(bnp_ready, 1)
            dve.wait_ge(k_in, 16)
            L.link(dve.tensor_reduce(kmax[:], KR, AX.X, ALU.max))
            dve.tensor_tensor(KS, KR, kmax[:].unsqueeze(2).broadcast_to([128, G8, S]), ALU.subtract).then_inc(ks_ready, 1)
            dve.wait_ge(bv_done, 1)
            dve.wait_ge(v_in, 32)
            L.link(dve.tensor_tensor(VN, VR, psV[:, 0:1].broadcast_to([2 * NB, S, DK]), ALU.mult))
            dve.tensor_tensor(VN, VN, psV[:, 1:2].broadcast_to([2 * NB, S, DK]), ALU.add).then_inc(vn_ready, 1)
            dve.wait_ge(vn_ready, 1)
            dve.wait_ge(vp_set, 1)
            values = VP[:, SP:SP + DK * SP].rearrange("b (k s) -> b k s", k=DK)[:, :, 1:SP]
            by_step = VN.rearrange(by_key).rearrange("b (k s) -> b k s", k=DK)
            dve.tensor_copy(values, by_step).then_inc(v_ready, 1)
            dve.wait_ge(v_ready, 1)
            dve.tensor_tensor(values[NB:2 * NB], by_step[NB:2 * NB], values[NB:2 * NB].bitcast(f32), ALU.subtract).then_inc(v_ready, 1)
            dve.wait_ge(early_in, 16 * 6)
            L.link(dve.tensor_copy(WPh[:], WP[:]))
            L.link(dve.tensor_scalar(WPm[:], WP[:], K[0:36, K_CV + 1:K_CV + 2], None, ALU.mult))
            dve.tensor_copy(BD[:], K[:, K_BD:K_BD + F + DK]).then_inc(bd_ready, 1)
            dve.scalar_tensor_tensor(W36[:], WPh[:].bitcast(f32), K[0:36, K_CV:K_CV + 1], WPm[:], ALU.mult, ALU.add).then_inc(w36_ready, 1)
            dve.wait_ge(exp_done, 1)
            L.link(dve.tensor_reduce(ksum[:], KS, AX.X, ALU.add))
            L.link(dve.reciprocal(krec[:], ksum[:]))
            dve.tensor_tensor(KS, KS, krec[:].unsqueeze(2).broadcast_to([128, G8, S]), ALU.mult).then_inc(k_ready, 1)
            def step(g, u):
                w = 1 - u

                def products(b):
                    n = g * GB + b
                    dve.wait_ge(conv_done, n + 1)
                    wait_from_one(dve, pl_ready, n - GB + 1)
                    for h, to in enumerate((P0[:, u, b], PF[:, b])):
                        ins = dve.scalar_tensor_tensor(to, psC[b % 2][h], 0.0,
                                                       QN[:, u, b:b + 1].broadcast_to([128, HV, SP]), ALU.max, ALU.mult)
                    ins.then_inc(p_ready, 1)
                if on(g, 0, NG):
                    dve.wait_ge(qn_ready, g + 1)
                    wait_from_one(dve, sum_done, g - 1)
                    products(0)
                    products(1)
                if on(g - 2, 0, NG):
                    dve.wait_ge(ht_done, g - 1)
                    wait_from_one(dve, h1_kept, g - 3)
                    dve.tensor_tensor(H1[:, u], psH, H[:, bass.ds((g - 2) * 2, 2)], ALU.add).then_inc(h1_ready, 1)
                    dve.wait_ge(h1_ready, g - 1)
                    for t in range(2):
                        L.made(dve.bn_stats(ST[:, u, t], H1[:, u, t]))
                    L.wait()
                    dve.memset(carrier[:], 0.0)
                    for t in range(2):
                        dve.bn_aggr(MV[:, u, t], ST[:, u, t]).then_inc(mv_ready, 1)
                if on(g, 0, NG):
                    products(2)
                    products(3)
                if on(g - 2, 0, NG):
                    dve.wait_ge(sd_ready, g - 1)
                    L.link(dve.reciprocal(SD[:, u, :, 1], SD[:, u, :, 0]))
                    if isinstance(g, int):
                        if g >= 4:
                            dve.wait_ge(xr_stored[u], 16 * ((g - 2) // 2))
                    else:
                        dve.wait_ge(xr_stored[u], freed[0])
                    wait_from_one(dve, xt_done, g - 3)
                    for t in range(2):
                        ins = dve.tensor_scalar(XR[:, u, t, 0:F], H1[:, u, t], MV[:, u, t, 0:1], SD[:, u, t, 1:2], ALU.subtract, ALU.mult)
                        if t == 0:
                            L.made(ins)
                    ins.then_inc(xn_ready, 1)
                if on(g - 3, 0, NG):
                    dve.wait_ge(gate_done, g - 2)
                    dve.tensor_copy(LG[:, bass.ds((g - 3) * 2, 2)], psG).then_inc(lg_ready, 1)
                if on(g + 1, 0, NG):
                    dve.wait_ge(lam_c_done, g + 2)
                    wait_from_one(dve, yc_done, g)
                    dve.tensor_tensor(LC[:, w], psL.unsqueeze(2).broadcast_to([128, GB, NH, DK]),
                                      K[:, K_MB:K_MB + NH].unsqueeze(1).unsqueeze(3).broadcast_to([128, GB, NH, DK]),
                                      ALU.mult).then_inc(lc_ready, 1)

            freed = [None]
            for g in range(-1, 4):
                step(g, g % 2)
                if g == 1:
                    dve.wait_ge(s_hi, 2)
                    dve.tensor_tensor(S1l[:], SR1[:], S1h[:].bitcast(f32), ALU.subtract).then_inc(s_lo, 1)
                    dve.tensor_tensor(S2[:, :, 1], SR2[:], S2[:, :, 0].bitcast(f32), ALU.subtract).then_inc(s_lo, 1)
            with dve.Fori(2, 7) as j:
                L.loop(2, j, 8)
                freed[0] = (j - 1) * 16
                step(j * 2, 0)
                step(j * 2 + 1, 1)
            L.end(5)
            for g in range(14, NG + 3):
                step(g, g % 2)

        @block.tensor
        def _(pe):
            pe.wait_ge(bnp_ready, 1)
            for c in range(2):
                ins = pe.matmul(psV[:, c], bnt[0:DK, 2 + c:3 + c].broadcast_to([DK, 2 * NB]), K[0:DK, K_ID:K_ID + DK], start=True, stop=True)
            ins.then_inc(bv_done, 1)
            pe.transpose(PS[6][0:2, 0:128], bnt[:, 0:2], ident).then_inc(bnt_done, 1)
            pe.wait_ge(vn_ready, 1)
            by_step = VN[0:NB].rearrange(by_key).rearrange("b (k s) -> b k s", k=DK)
            for k in range(DK):
                ins = pe.transpose(PS[2 + k // 8][0:S, NB * (k % 8):NB * (k % 8) + NB], by_step[:, k], K[0:NB, K_ID:K_ID + NB])
            ins.then_inc(vt_done, 1)
            pe.wait_ge(k_ready, 1)
            for q in range(G8):
                ins = pe.transpose(PS[q // 4][0:S, 128 * (q % 4):128 * (q % 4) + 128], KS[:, q], ident)
            ins.then_inc(kt_done, 1)
            pe.wait_ge(kvt_ready, 4)
            pe.wait_ge(w36_ready, 1)
            pe.wait_ge(bd_ready, 1)
            pe.wait_ge(early_in, 16 * 6)

            def step(g, u):
                w = 1 - u

                def conv(b):
                    n = g * GB + b
                    wait_from_one(pe, p_ready, n - 1)
                    for h in range(2):
                        ins = pe.matmul(psC[b % 2][h].rearrange("p v s -> p (v s)"), W36[:], IM[:, u, b * VB + 512 * h:b * VB + 512 * h + 512], start=True, stop=True)
                    ins.then_inc(conv_done, 1)

                def add_products(v):
                    window = slice(DK - 1 - v, DK - 1 - v + F)
                    if v < HV:
                        return pe.matmul(by_batch, K[:, K_BD:K_END][:, window], P0[:, w, :, v], start=False, stop=False)
                    pe.matmul(by_batch, BD[:, window], Ph[:, w, :, v - HV], start=False, stop=False)
                    return pe.matmul(by_batch, BD[:, window], Pl[:, w, :, v - HV], start=False, stop=(v == DK - 1))
                by_batch = psY.rearrange("p (b s) -> p b s", b=GB)
                if on(g, 0, NG):
                    if isinstance(g, int):
                        pe.wait_ge(im_in[u], 64 * (g // 2 + 1))
                    else:
                        pe.wait_ge(im_in[u], arrived[0])
                    conv(0)
                    conv(1)
                if on(g - 2, 0, NG):
                    pe.wait_ge(ot_ready, g - 1)
                    wait_from_one(pe, h1_ready, g - 2)
                    pe.wait_ge(lc_ready, min(g + 1, NG) if isinstance(g, int) else g + 1)
                    for t in range(2):
                        ins = pe.transpose(psH[:, t], OTs[:, u, 2 * t:2 * t + 2].rearrange("p b s -> p (b s)"), ident)
                    ins.then_inc(ht_done, 1)
                if on(g - 1, 0, NG):
                    pe.wait_ge(p_ready, g * GB)
                    for v in range(EARLY):
                        add_products(v)
                if on(g, 0, NG):
                    conv(2)
                    conv(3)
                if on(g - 3, 0, NG):
                    pe.wait_ge(xt_ready, 2 * (g - 2))
                    wait_from_one(pe, lg_ready, g - 3)
                    for t in range(2):
                        ins = pe.matmul(psG[:, t], XG[:, w, TOK * t:TOK * t + TOK], GW[:], start=True, stop=True)
                    ins.then_inc(gate_done, 1)
                if on(g + 1, 0, NG):
                    pe.wait_ge(kh_ready, g + 2)
                    if not isinstance(g, int) or g >= 2:
                        pe.wait_ge(h1_ready, g - 1)
                    for b in range(GB):
                        ins = pe.matmul(psL[:, b], KH[:, w, b].rearrange("p h k -> p (h k)"),
                                        VT[:, bass.ds((g + 1) * GB + b, 1)].rearrange("p b v -> p (b v)"), start=True, stop=True)
                    ins.then_inc(lam_c_done, 1)
                if on(g - 1, 0, NG):
                    for v in range(EARLY, HV):
                        add_products(v)
                    pe.wait_ge(pl_ready, g * GB)
                    for v in range(HV, DK):
                        ins = add_products(v)
                    ins.then_inc(sum_done, 1)
                if on(g - 2, 0, NG):
                    pe.wait_ge(xn_ready, g - 1)
                    wait_from_one(pe, lg_ready, g - 2)
                    for t in range(2):
                        ins = pe.transpose(psX[:, TOK * t:TOK * t + TOK], XR[:, u, t, 0:F], ident_t)
                    ins.then_inc(xt_done, 1)
                if on(g, 0, NG):
                    pe.wait_ge(lc_ready, g + 1)
                    pe.wait_ge(qn_ready, g + 1)
                    wait_from_one(pe, yc_ready, g)
                    for b in range(GB):
                        ins = pe.matmul(psY[:, SP * b:SP * b + SP], LC[:, u, b].rearrange("p h v -> p (h v)"), QN[:, u, b], start=(b == 0), stop=False)
                    ins.then_inc(yc_done, 1)
                if on(g - 1, 0, NG):
                    pe.wait_ge(yc_ready, g)
                    wait_from_one(pe, ot_ready, g - 1)
                    pe.matmul(psO, WO[:], YC[:, w], start=True, stop=True).then_inc(ot_done, 1)

            arrived = [None]
            for g in range(-1, 4):
                step(g, g % 2)
            with pe.Fori(2, 7) as j:
                arrived[0] = (j + 1) * 64
                step(j * 2, 0)
                step(j * 2 + 1, 1)
            for g in range(14, NG + 3):
                step(g, g % 2)


def ffn(nc, m):
    K, ident, ident_t, H, LG, X2h, X2l, PS = (m[n] for n in "K ident ident_t H LG X2h X2l PS".split())
    x_rows, routed, base, out_rows, w13, w2 = (m[n] for n in "x_rows routed base out_rows w13 w2".split())
    S1h, S1l, S2 = m["S1h"], m["S1l"], m["S2"]
    with ExitStack() as ctx:
        def sb(name, shape, dt=f32):
            return ctx.enter_context(nc.sbuf_tensor(name, shape, dt))

        def sem(name):
            return ctx.enter_context(nc.semaphore(name))

        CT = 2 * TOK
        NC = N // CT
        IC = I // 128
        of_slot, OF = sb("of_slot", [128, SLOTS]), sb("OF", [128, SLOTS], i32)
        W1h, W1l = (sb(n, [F, E, 2 * I], f32r) for n in ("W1h", "W1l"))
        W2 = sb("W2", [128, E, IC, 2, F], f32r)
        with ExitStack() as own:
            def sbo(name, shape, dt=f32):
                return own.enter_context(nc.sbuf_tensor(name, shape, dt))
            lmax, top = sbo("lmax", [TOK, NT]), sbo("top", [TOK, NT])
            OH, RK = sbo("OH", [TOK, E, NT]), sbo("RK", [TOK, E, NT])
            CNT, INCL, ones_s = sbo("CNT", [128, E, NT]), sbo("INCL", [128, E, NT]), sbo("ones_s", [128, E * NT])
            n_e, tiles_e, ends, starts, first = (sbo(n, [128, E]) for n in ("n_e", "tiles_e", "ends", "starts", "first"))
            n_i = sbo("n_int", [128, E], i32)
            posf, POS = sbo("posf", [TOK, NT]), sbo("POS", [TOK, NT], i32)
            WR1, WR2 = sbo("WR1", [F, 2 * I]), sbo("WR2", [128, IC, F])
            GF = sbo("GF", [128, 2, IC, CT])
            Gh, Gl = (sbo(n, [128, 2, IC, CT], f32r) for n in ("Gh", "Gl"))
            BS = sbo("BS", [TOK, 2, 2, F])
            RB = sbo("RB", [TOK, 3, 8, ROW])
            shared(nc, locals())
        XS = sb("XS", [128, 4, ROW])
        BG, TO = sb("BG", [128, 4, F]), sb("TO", [128, 4, 2], i32)
        Xh, Xl = (sb(n, [F, 2, 128], f32r) for n in ("Xh", "Xl"))
        SG, GX = sb("SG", [128, 2, I]), sb("GX", [128, 2, I])
        Gh, Gl = (sb(n, [128, 2, IC, 128], f32r) for n in ("GTh", "GTl"))
        OS = sb("OS", [128, 2, F])
        experts(nc, locals())


def shared(nc, m):
    K, ident, ident_t, H, LG, X2h, X2l, PS = (m[n] for n in "K ident ident_t H LG X2h X2l PS".split())
    x_rows, routed, base, w13, w2 = (m[n] for n in "x_rows routed base w13 w2".split())
    lmax, top, OH, RK, CNT, INCL, ones_s, n_e, n_i, tiles_e, ends, starts, first, posf, POS, of_slot, OF = (
        m[n] for n in "lmax top OH RK CNT INCL ones_s n_e n_i tiles_e ends starts first posf POS of_slot OF".split())
    S1h, S1l, S2, WR1, WR2, W1h, W1l, W2, GF, Gh, Gl, BS, RB = (
        m[n] for n in "S1h S1l S2 WR1 WR2 W1h W1l W2 GF Gh Gl BS RB".split())
    CT, NC, IC = m["CT"], m["NC"], m["IC"]
    with ExitStack() as ctx:
        def sem(name):
            return ctx.enter_context(nc.semaphore(name))

        w1_in, w2_in, w_hi, w1_split, w2_split = sem("w1_in"), sem("w2_in"), sem("we_hi"), sem("w1_split"), sem("w2_split")
        oh_ready, rank_done, pos_ready = sem("oh_ready"), sem("rank_done"), sem("pos_ready")
        rb_in, scattered = [sem(f"rb_in{n}") for n in range(4)], [sem(f"scattered{n}") for n in range(4)]
        g_done, gelu_ready, gh_ready, gl_ready = sem("g_done"), sem("gelu_ready"), sem("gh_ready"), sem("gl_ready")
        y_done, bs_ready, base_stored = sem("y_done"), sem("bs_ready"), [sem("base_stored0"), sem("base_stored1")]
        dve_link = sem("dve_link3")

        psG = [[PS[2 * u + h][:, 0:2 * CT].rearrange("p (i s) -> p i s", i=2) for h in range(2)] for u in range(2)]
        psY = [PS[4 + u][0:TOK, :].rearrange("p (t h f) -> p t h f", t=2, h=2) for u in range(2)]
        psR, psN = PS[6][0:TOK, 0:E * NT], PS[7][:, 0:E * NT]
        block = ctx.enter_context(nc.Block())

        @block.sync
        def _(sp):
            def weights(n, e):
                to, src, arrived = ((WR1, w13, w1_in), (WR2, w2, w2_in))[n]
                if n == 0:
                    sp.dma_start(to[:], src[:, bass.ds(e, 1)].rearrange("p e i -> p (e i)")).then_inc(arrived, 16)
                else:
                    sp.dma_start(to[:], src[:, bass.ds(e, 1)].rearrange("p e i f -> p (e i f)")).then_inc(arrived, 16)
            weights(0, 0)
            for q in range(3):
                sp.dma_start(RB[:, q], x_rows[8 * q * TOK:(8 * q + 8) * TOK, :].rearrange("(t p) c -> p t c", p=TOK)).then_inc(rb_in[q], 16)
                if q == 0:
                    weights(1, 0)

            def step(c, u):
                if u == 1 and on(c, 1, NC - 2):
                    e = c // 2 if isinstance(c, int) else expert[0]
                    sp.wait_ge(w1_split, e + 1)
                    weights(0, e + 1)
                if u == 0 and on(c, 2, NC):
                    e = c // 2 if isinstance(c, int) else expert[0]
                    sp.wait_ge(w2_split, e)
                    weights(1, e)
                if on(c - 2, 0, NC):
                    sp.wait_ge(bs_ready, c - 1)
                    sp.dma_start(base[bass.ds((c - 2) * CT, CT), :].rearrange("(t p) f -> p t f", p=TOK), BS[:, u]).then_inc(base_stored[u], 16)
            expert = [None]
            for c in range(0, 4):
                step(c, c % 2)
            with sp.Fori(2, 7) as j:
                expert[0] = j
                step(j * 2, 0)
                step(j * 2 + 1, 1)
            for c in range(NC - 2, NC + 2):
                step(c, c % 2)
            for u in range(2):
                sp.wait_ge(base_stored[u], 16 * NC // 2)

        @block.gpsimd
        def _(pool):
            pool.wait_ge(pos_ready, 1)
            for t in range(NT):
                q = t // 8
                if t % 8 == 0:
                    pool.wait_ge(rb_in[q], 16)
                pool.indirect_dma_start(routed, bass.IndirectOffsetOnAxis(POS[:, t:t + 1], 0), RB[:, q % 3, t % 8], None).then_inc(scattered[q], 16)
                if t == 15:
                    pool.wait_ge(scattered[0], 16 * 8)
                    pool.dma_start(RB[:, 0], x_rows[24 * TOK:32 * TOK, :].rearrange("(t p) c -> p t c", p=TOK)).then_inc(rb_in[3], 16)
            for n in range(4):
                pool.wait_ge(scattered[n], 16 * 8)

        @block.scalar
        def _(act):
            def step(c, u, e):
                wait_from_one(act, gl_ready, c - 1)
                wait_from_one(act, y_done, c - 1)
                for h in range(2):
                    act.wait_ge(g_done, 2 * c + h + 1)
                    act.activation(Gh[:, u, 2 * h:2 * h + 2], psG[u][h], ACT.Gelu).then_inc(gh_ready, 1)
                    act.activation(GF[:, u, 2 * h:2 * h + 2], psG[u][h], ACT.Gelu).then_inc(gelu_ready, 1)
                if u == 0:
                    act.wait_ge(w1_in, 16 * (e + 1))
                    act.activation(W1h[:, bass.ds(e, 1)].rearrange("p e i -> p (e i)"), WR1[:], ACT.Copy).then_inc(w_hi, 1)
                else:
                    act.wait_ge(w2_in, 16 * (e + 1))
                    act.activation(W2[:, bass.ds(e, 1), :, 0].rearrange("p e i f -> p (e i) f"), WR2[:], ACT.Copy).then_inc(w_hi, 1)
            for c in range(0, 4):
                step(c, c % 2, c // 2)
            with act.Fori(2, 8) as j:
                step(j * 2, 0, j)
                step(j * 2 + 1, 1, j)

        @block.vector
        def _(dve):
            L = Links(dve, dve_link)
            rev = K[0:TOK, K_REV:K_REV + E].unsqueeze(1).broadcast_to([TOK, NT, E])
            L.made(dve.memset(ones_s[:], 1.0))
            L.link(dve.tensor_reduce(lmax[:], LG[:], AX.X, ALU.max))
            L.link(dve.tensor_tensor(LG[:], LG[:], lmax[:].unsqueeze(2).broadcast_to([TOK, NT, E]), ALU.is_equal))
            L.link(dve.tensor_tensor(LG[:], LG[:], rev, ALU.mult))
            L.link(dve.tensor_reduce(top[:], LG[:], AX.X, ALU.max))
            dve.tensor_tensor(OH[:].rearrange("p e t -> p t e"), rev, top[:].unsqueeze(2).broadcast_to([TOK, NT, E]),
                              ALU.is_equal).then_inc(oh_ready, 1)
            dve.wait_ge(rank_done, 2)
            flat = "p e t -> p (e t)"
            L.link(dve.tensor_copy(CNT[:].rearrange(flat), psN))
            L.link(dve.tensor_tensor_scan(INCL[:].rearrange(flat), ones_s[:], CNT[:].rearrange(flat), 0.0, ALU.mult, ALU.add))
            L.link(dve.tensor_tensor(CNT[:], INCL[:], CNT[:], ALU.subtract))
            L.link(dve.tensor_tensor(n_e[:], INCL[:, :, NT - 1], CNT[:, :, 0], ALU.subtract))
            L.link(dve.tensor_scalar(n_i[:], n_e[:], 127.0, None, ALU.add))
            L.link(dve.tensor_scalar(n_i[:], n_i[:], 7, None, ALU.logical_shift_right))
            L.link(dve.tensor_copy(tiles_e[:], n_i[:]))
            L.link(dve.tensor_tensor_scan(ends[:], ones_s[:, 0:E], tiles_e[:], 0.0, ALU.mult, ALU.add))
            L.link(dve.tensor_tensor(starts[:], ends[:], tiles_e[:], ALU.subtract))
            L.link(dve.scalar_tensor_tensor(first[:], starts[:], 128.0, CNT[:, :, 0], ALU.mult, ALU.subtract))
            L.link(dve.tensor_tensor(RK[:].rearrange(flat), psR, CNT[0:TOK].rearrange(flat), ALU.add))
            L.link(dve.tensor_tensor(RK[:], RK[:], first[0:TOK].unsqueeze(2).broadcast_to([TOK, E, NT]), ALU.add))
            L.link(dve.tensor_tensor(RK[:], RK[:], OH[:], ALU.mult))
            L.link(dve.tensor_reduce(posf[:], RK[:].rearrange("p e t -> p t e"), AX.X, ALU.add))
            dve.tensor_copy(POS[:], posf[:]).then_inc(pos_ready, 1)
            L.link(dve.tensor_scalar(of_slot[:], K[:, K_IO:K_IO + SLOTS], starts[:, 1:2], None, ALU.is_ge))
            for e in range(2, E):
                L.link(dve.scalar_tensor_tensor(of_slot[:], K[:, K_IO:K_IO + SLOTS], starts[:, e:e + 1], of_slot[:], ALU.is_ge, ALU.add))
            L.link(dve.tensor_copy(OF[:], of_slot[:]))

            def step(c, u, e):
                w = 1 - u
                if on(c, 0, NC):
                    for h in range(2):
                        hs = slice(2 * h, 2 * h + 2)
                        dve.wait_ge(gelu_ready, 2 * c + h + 1)
                        if h == 0:
                            wait_from_one(dve, y_done, c - 1)
                        dve.wait_ge(gh_ready, 2 * c + h + 1)
                        ins = dve.tensor_tensor(Gl[:, u, hs], GF[:, u, hs], Gh[:, u, hs].bitcast(f32), ALU.subtract)
                    ins.then_inc(gl_ready, 1)
                    dve.wait_ge(w_hi, c + 1)
                    if u == 0:
                        dve.tensor_tensor(W1l[:, bass.ds(e, 1)].rearrange("p e i -> p (e i)"), WR1[:],
                                          W1h[:, bass.ds(e, 1)].rearrange("p e i -> p (e i)").bitcast(f32), ALU.subtract).then_inc(w1_split, 1)
                    else:
                        dve.tensor_tensor(W2[:, bass.ds(e, 1), :, 1].rearrange("p e i f -> p (e i) f"), WR2[:],
                                          W2[:, bass.ds(e, 1), :, 0].rearrange("p e i f -> p (e i) f").bitcast(f32), ALU.subtract).then_inc(w2_split, 1)
                if on(c - 1, 0, NC):
                    dve.wait_ge(y_done, c)
                    if isinstance(c, int):
                        if c >= 3:
                            dve.wait_ge(base_stored[w], 16 * ((c - 1) // 2))
                    else:
                        dve.wait_ge(base_stored[w], freed[0])
                    L.link(dve.tensor_tensor(BS[:, w], psY[w][:, :, 0], H[:, bass.ds((c - 1) * 2, 2)], ALU.add))
                    dve.tensor_tensor(BS[:, w], psY[w][:, :, 1], BS[:, w], ALU.add).then_inc(bs_ready, 1)
            freed = [None]
            for c in range(0, 4):
                step(c, c % 2, c // 2)
            with dve.Fori(2, 8) as j:
                L.loop(2, j, 2)
                freed[0] = (j - 1) * 16
                step(j * 2, 0, j)
                freed[0] = j * 16
                step(j * 2 + 1, 1, j)
            L.end(6)
            step(NC, 0, None)

        @block.tensor
        def _(pe):
            def step(c, u):
                w = 1 - u
                if on(c, 0, NC):
                    wait_from_one(pe, gelu_ready, 2 * (c - 1))
                    ts = bass.ds(c * CT, CT)
                    for i in range(IC):
                        for n, (a, x) in enumerate(((S1h, X2h), (S1l, X2h), (S1h, X2l))):
                            ins = pe.matmul(psG[u][i // 2][:, i % 2], a[:, 128 * i:128 * i + 128], x[:, ts], start=(n == 0), stop=(n == 2))
                        if i % 2:
                            ins.then_inc(g_done, 1)
                if on(c - 1, 0, NC):
                    pe.wait_ge(gl_ready, c)
                    wait_from_one(pe, bs_ready, c - 2)
                    for t in range(2):
                        for i in range(IC):
                            for n, a in enumerate((Gh, Gl)):
                                ins = pe.matmul(psY[w][:, t].rearrange("p h f -> p (h f)"), a[:, w, i, TOK * t:TOK * t + TOK],
                                                S2[:, i].rearrange("p h f -> p (h f)"), start=(i == 0 and n == 0), stop=(i == IC - 1 and n == 1))
                    ins.then_inc(y_done, 1)
            step(0, 0)
            pe.wait_ge(oh_ready, 1)
            flat = OH[:].rearrange("p e t -> p (e t)")
            pe.matmul(psR, K[0:TOK, K_LR:K_LR + TOK], flat, start=True, stop=True).then_inc(rank_done, 1)
            pe.matmul(psN, K[0:TOK, K_ONE:K_ONE + 128], flat, start=True, stop=True).then_inc(rank_done, 1)
            for c in range(1, 4):
                step(c, c % 2)
            with pe.Fori(2, 8) as j:
                step(j * 2, 0)
                step(j * 2 + 1, 1)
            step(NC, 0)


def experts(nc, m):
    K, ident, PS, OF = (m[n] for n in "K ident PS OF".split())
    routed, base, out_rows = m["routed"], m["base"], m["out_rows"]
    W1h, W1l, W2, XS, BG, TO, Xh, Xl, SG, GX, Gh, Gl, OS, IC = (
        m[n] for n in "W1h W1l W2 XS BG TO Xh Xl SG GX Gh Gl OS IC".split())
    with ExitStack() as ctx:
        def sem(name):
            return ctx.enter_context(nc.semaphore(name))

        xs_in, bg_in, stored = [sem(f"xs_in{n}") for n in range(4)], [sem(f"bg_in{n}") for n in range(4)], [sem("stored0"), sem("stored1")]
        bg_set, to_ready, dve_link, turn = sem("bg_set"), [sem("to_ready0"), sem("to_ready1")], sem("dve_link4"), sem("turn3")
        xt_done, xh_ready, xl_ready = sem("xt3_done"), sem("xh_ready"), sem("xl_ready")
        up_done, sg_ready, gx_ready, gt_done, gh_ready, gl_ready, y_done, os_ready = (
            sem(n) for n in ("up_done", "sg_ready", "gx_ready", "gt_done", "gth_ready", "gtl_ready", "y3_done", "os_ready"))
        psU = [[PS[2 * u + h][:, :] for h in range(2)] for u in range(2)]
        psX, psT = PS[4][:, 0:128], PS[5][:, :].rearrange("p (i s) -> p i s", i=IC)
        psY = [PS[6 + u][:, 0:2 * F] for u in range(2)]
        block = ctx.enter_context(nc.Block())

        LAST = SLOTS + 3

        def run(step, eng, links=None):
            for k in range(-2, 4):
                step(k, k % 4, None)
            with eng.Fori(1, 9) as j:
                if links is not None:
                    links.loop(1, j, 4)
                for n in range(4):
                    step(j * 4 + n, n, j)
            if links is not None:
                links.end(8)
            for k in range(36, LAST):
                step(k, k % 4, None)

        def wait_use(eng, sems, k, n, j, d):
            eng.wait_ge(sems[(n + d) % 4], 16 * ((k + d) // 4 + 1) if j is None else (j + (n + d) // 4) * 16 + 16)

        @block.sync
        def _(sp):
            def load(m, t):
                sp.dma_start(XS[:, t], routed[bass.ds(m * 128, 128), :]).then_inc(xs_in[t], 16)

            def step(k, n, j):
                if k is not None and on(k + 3, 0, SLOTS):
                    m = k + 3 if isinstance(k, int) else sp.snap(k + 3)
                    if not isinstance(k, int) or k > 0:
                        sp.wait_ge(xt_done, k)
                        sp.wait_ge(to_ready[1], k)
                    load(m, (n + 3) % 4)
            load(0, 0)
            run(step, sp)

        @block.gpsimd
        def _(pool):
            pool.memset(BG[:], 0.0).then_inc(bg_set, 1)
            pool.wait_ge(bg_set, 1)

            def step(k, n, j):
                t = (n + 2) % 4
                if on(k - 2, 0, SLOTS):
                    pool.wait_ge(os_ready, k - 1)
                    hold_waits(pool, turn)
                    pool.tensor_copy(TO[:, t, 0:1], TO[:, t, 1:2]).then_inc(to_ready[0], 1)
                    pool.wait_ge(to_ready[0], k - 1)
                if on(k + 2, 0, SLOTS):
                    wait_use(pool, xs_in, k, n, j, 2)
                    hold_waits(pool, turn)
                    pool.tensor_copy(TO[:, t, 1:2], XS[:, t, F:F + 1].bitcast(i32)).then_inc(to_ready[1], 1)
                if on(k - 2, 0, SLOTS):
                    hold_waits(pool, turn)
                    pool.indirect_dma_start(out_rows, bass.IndirectOffsetOnAxis(TO[:, t, 0:1], 0), OS[:, n % 2], None,
                                            bounds_check=N - 1, oob_is_err=False).then_inc(stored[n % 2], 16)
                if on(k + 2, 0, SLOTS):
                    pool.wait_ge(to_ready[1], k + 3)
                    hold_waits(pool, turn)
                    pool.indirect_dma_start(BG[:, t], None, base, bass.IndirectOffsetOnAxis(TO[:, t, 1:2], 0),
                                            bounds_check=N - 1, oob_is_err=False).then_inc(bg_in[t], 16)
            run(step, pool)
            pool.wait_ge(stored[0], 16 * ((SLOTS + 1) // 2))
            pool.wait_ge(stored[1], 16 * (SLOTS // 2))

        @block.scalar
        def _(act):
            def step(k, n, j):
                u, w = n % 2, 1 - n % 2
                if on(k + 1, 0, SLOTS):
                    act.wait_ge(xt_done, k + 2)
                    wait_from_one(act, up_done, 2 * k)
                    act.activation(Xh[:, w], psX, ACT.Copy).then_inc(xh_ready, 1)
                if on(k, 0, SLOTS):
                    act.wait_ge(up_done, 2 * k + 1)
                    wait_from_one(act, gx_ready, k - 1)
                    act.activation(SG[:, u], psU[u][0], ACT.Silu).then_inc(sg_ready, 1)
                if on(k - 1, 0, SLOTS):
                    act.wait_ge(gt_done, k)
                    wait_from_one(act, y_done, k - 2)
                    act.activation(Gh[:, w], psT, ACT.Copy).then_inc(gh_ready, 1)
            run(step, act)

        @block.vector
        def _(dve):
            L = Links(dve, dve_link)

            def step(k, n, j):
                u, w = n % 2, 1 - n % 2
                if on(k + 1, 0, SLOTS):
                    dve.wait_ge(xh_ready, k + 2)
                    dve.tensor_tensor(Xl[:, w], psX, Xh[:, w].bitcast(f32), ALU.subtract).then_inc(xl_ready, 1)
                if on(k, 0, SLOTS):
                    dve.wait_ge(up_done, 2 * k + 2)
                    dve.wait_ge(sg_ready, k + 1)
                    wait_from_one(dve, gt_done, k - 1)
                    dve.tensor_tensor(GX[:, u], psU[u][1], SG[:, u], ALU.mult).then_inc(gx_ready, 1)
                if on(k - 1, 0, SLOTS):
                    dve.wait_ge(gh_ready, k)
                    dve.tensor_tensor(Gl[:, w], psT, Gh[:, w].bitcast(f32), ALU.subtract).then_inc(gl_ready, 1)
                if on(k - 2, 0, SLOTS):
                    t = (n + 2) % 4
                    dve.wait_ge(y_done, k - 1)
                    if j is None:
                        dve.wait_ge(bg_in[t], 16 * ((k - 2) // 4 + 1))
                        if k - 4 >= 0:
                            dve.wait_ge(stored[u], 16 * ((k - 4) // 2 + 1))
                    else:
                        dve.wait_ge(bg_in[t], (j + (n - 2) // 4) * 16 + 16)
                        dve.wait_ge(stored[u], j * 32 + 16 * ((n - 4) // 2 + 1))
                    L.link(dve.tensor_tensor(OS[:, u], psY[u][:, 0:F], BG[:, t], ALU.add))
                    dve.tensor_tensor(OS[:, u], psY[u][:, F:2 * F], OS[:, u], ALU.add).then_inc(os_ready, 1)
            run(step, dve, L)

        @block.tensor
        def _(pe):
            def step(k, n, j):
                u, w = n % 2, 1 - n % 2
                if on(k + 1, 0, SLOTS):
                    wait_use(pe, xs_in, k, n, j, 1)
                    wait_from_one(pe, xl_ready, k + 1)
                    pe.transpose(psX, XS[:, (n + 1) % 4, 0:F], ident).then_inc(xt_done, 1)
                if on(k, 0, SLOTS):
                    e = pe.value_load(OF[0:1, bass.ds(k, 1)], min_val=0, max_val=E - 1)
                    pe.wait_ge(xl_ready, k + 1)
                    wait_from_one(pe, gx_ready, k - 1)
                    for h in range(2):
                        for p, (a, b) in enumerate(((Xh, W1h), (Xh, W1l), (Xl, W1h))):
                            ins = pe.matmul(psU[u][h], a[:, u], b[:, bass.ds(e, 1), I * h:I * h + I].rearrange("p e i -> p (e i)"), start=(p == 0), stop=(p == 2))
                        ins.then_inc(up_done, 1)
                if on(k - 1, 0, SLOTS):
                    pe.wait_ge(gx_ready, k)
                    wait_from_one(pe, gl_ready, k - 1)
                    for i in range(IC):
                        ins = pe.transpose(psT[:, i], GX[:, w, 128 * i:128 * i + 128], ident)
                    ins.then_inc(gt_done, 1)
                if on(k - 2, 0, SLOTS):
                    e = pe.value_load(OF[0:1, bass.ds(k - 2, 1)], min_val=0, max_val=E - 1)
                    pe.wait_ge(gl_ready, k - 1)
                    wait_from_one(pe, os_ready, k - 3)
                    for i in range(IC):
                        for p, a in enumerate((Gh, Gl)):
                            ins = pe.matmul(psY[u], a[:, u, i], W2[:, bass.ds(e, 1), i].rearrange("p e h f -> p (e h f)"),
                                            start=(i == 0 and p == 0), stop=(i == IC - 1 and p == 1))
                    ins.then_inc(y_done, 1)
            run(step, pe)


def lay_out(x, L0_tok_W, L0_tok_b, L0_attn_Wq, L0_attn_bq, L0_attn_Wk, L0_attn_bk, L0_attn_Wv, L0_attn_bv,
            L0_attn_gq, L0_attn_betaq, L0_attn_gv, L0_attn_betav, L0_attn_Wpos, L0_attn_Wout, L0_attn_bout,
            L0_ffn_gate_w, L0_ffn_w1, L0_ffn_w2, L0_ffn_w3, L0_ffn_sw1, L0_ffn_sw2):
    x = np.asarray(x)
    time = np.arange(S + 1, dtype=np.float32) / np.float32(S)
    path = np.empty((NB, S + 1, C), np.float32)
    path[:, :, 0] = time
    path[:, :, 1:] = x

    def tokens(a):
        return a.reshape(NT, TOK, C).transpose(1, 0, 2)
    W = np.asarray(L0_tok_W)
    o4 = C + C2 + C3
    wsig = np.zeros((128, NCH + 1, C, F), np.float32)
    wsig[:, :NCH] = W[:, o4:].reshape(F, NCH, 128, C).transpose(2, 1, 3, 0)
    wsig[0:C2, NCH] = W[:, C + C2:o4].reshape(F, C2, C).transpose(1, 2, 0)
    wsig[C2:C2 + C, NCH] = W[:, C:C + C2].reshape(F, C, C).transpose(1, 2, 0)
    wsig[C2 + C, NCH] = W[:, 0:C].T
    K = np.zeros((128, K_END), np.float32)
    K[:, K_ID:K_ID + 128] = np.eye(128)
    r, s = np.arange(TOK)[:, None], np.arange(TOK)[None, :]
    same = r // S == s // S
    K[0:TOK, K_LX:K_LX + TOK] = same & (r < s)
    K[0:TOK, K_LI:K_LI + TOK] = same & (r <= s)
    K[0:TOK, K_LR:K_LR + TOK] = r < s
    K[:, K_ONE:K_ONE + 128] = 1
    K[:, K_MB:K_MB + NH] = np.arange(128)[:, None] // DK == np.arange(NH)[None, :]
    K[:, K_REV:K_REV + E] = E - np.arange(E)
    K[:, K_IO:K_IO + SLOTS] = np.arange(SLOTS)
    K[0:18, K_CV], K[18:36, K_CV] = 1, -1
    K[18:36, K_CV + 1] = 1
    K[np.arange(128), K_BD + np.arange(128) // DK * DK + DK - 1] = 1

    def rows(a, n):
        return np.broadcast_to(np.asarray(a)[None, :], (n, len(a)))
    vecs = np.zeros((128, 7), np.float32)
    for c, a in enumerate((L0_attn_gq, L0_attn_betaq, L0_attn_bq, L0_attn_bout)):
        vecs[:, c] = np.asarray(a)
    for c, a in enumerate((L0_attn_gv, L0_attn_betav, L0_attn_bv)):
        vecs[0:DK, P_GV + c] = np.asarray(a)
    return dict(
        path_now=tokens(path[:, :-1]), path_next=tokens(path[:, 1:]),
        path_first=tokens(np.broadcast_to(path[:, 0:1], (NB, S, C))),
        wsig=wsig.reshape(128, NCH + 1, 2, 512), consts=K,
        token_ids=(np.arange(NT)[None, :] * TOK + np.arange(TOK)[:, None]).astype(np.int32), tok_b=rows(L0_tok_b, TOK),
        qkv_b=rows(np.concatenate([np.asarray(a) for a in (L0_attn_bq, L0_attn_bk, L0_attn_bv)]), TOK),
        vecs=vecs, wqkv=np.concatenate([np.asarray(a) for a in (L0_attn_Wq, L0_attn_Wk, L0_attn_Wv)], axis=1),
        wpos=np.broadcast_to(np.asarray(L0_attn_Wpos).reshape(DK, 9).T[None, :, None, :], (4, 9, NH, DK)).reshape(36, 128),
        wout=np.asarray(L0_attn_Wout), gate_w=np.asarray(L0_ffn_gate_w).T,
        sw1=np.asarray(L0_ffn_sw1).T, sw2=np.asarray(L0_ffn_sw2).T.reshape(4, 128, F).transpose(1, 0, 2),
        w13=np.concatenate([np.asarray(L0_ffn_w1), np.asarray(L0_ffn_w3)], axis=1).transpose(2, 0, 1),
        w2=np.asarray(L0_ffn_w2).transpose(0, 2, 1).reshape(E, 4, 128, F).transpose(2, 0, 1, 3),
    )


INPUTS = ("path_now", "path_next", "path_first", "wsig", "consts", "token_ids", "tok_b", "qkv_b", "vecs", "wqkv", "wpos",
          "wout", "gate_w", "sw1", "sw2", "w13", "w2")


def kernel(**inputs):
    import concourse.bacc as bacc
    from concourse.bass_utils import run_bass_kernel_spmd

    laid = lay_out(**inputs)
    nc = bacc.Bacc("TRN2", target_bir_lowering=False, num_devices=1)
    arrays, args = {}, []
    for name in INPUTS:
        a = np.ascontiguousarray(laid[name])
        arrays[f"in_{name}"] = a
        args.append(nc.dram_tensor(f"in_{name}", a.shape, mybir.dt.from_np(a.dtype), kind="ExternalInput").ap())
    args.append(nc.dram_tensor("out_h", (NB, S, F), f32, kind="ExternalOutput").ap())
    build(nc, *args)
    result = run_bass_kernel_spmd(nc, [arrays], core_ids=[0])
    return result.results[0]["out_h"]
```
